# Optimizing a Trainium2 kernel written in Bass

```python
import numpy as np
import jax
import jax.numpy as jnp

def _softmax(x, axis=-1):
    return jax.nn.softmax(x, axis=axis)

def _gelu(x):
    return jax.nn.gelu(x, approximate=True)

def _silu(x):
    return jax.nn.silu(x)

def _sigmoid(x):
    return jax.nn.sigmoid(x)

def _layernorm(x, axis=-1, eps=1e-05):
    m = jnp.mean(x, axis=axis, keepdims=True)
    v = jnp.var(x, axis=axis, keepdims=True)
    return (x - m) / jnp.sqrt(v + eps)

def _scatter_add(tgt, idx, src, axis=0):
    return tgt.at[idx].add(src)

def _segment_sum(src, seg, n):
    return jax.ops.segment_sum(src, seg, n)
kernel_name = 'mk_gps_d1_gnn_r8_d03654'

def setup_inputs(seed: int=0):
    np.random.seed(seed)
    _w = jnp.asarray

    def _rec_inputs():
        import jax
        import jax.numpy as jnp
        _gk = jax.random.key(seed)
        x = -0.0001126 + 1 * jax.random.normal(jax.random.fold_in(_gk, 1), (1250, 768), jnp.float32)
        src = jax.random.randint(jax.random.fold_in(_gk, 2), (20000,), 0, 1250, jnp.int32)
        dst = jax.random.randint(jax.random.fold_in(_gk, 3), (20000,), 0, 1250, jnp.int32)
        _o = jnp.argsort(dst, stable=True)
        src = src[_o]
        dst = dst[_o]
        return (x, src, dst)
    x, src, dst = _rec_inputs()

    def _L0_gnn_setup():
        import jax, jax.numpy as jnp
        import numpy as np
        N_NODES = 1250
        N_EDGES = 12500
        DIM = 768
        key = jax.random.key(seed)
        k1, k2, k3, k4 = jax.random.split(key, 4)
        x = jax.random.normal(k1, (N_NODES, DIM), dtype=jnp.float32)
        edge_index = jax.random.randint(k2, (2, N_EDGES), 0, N_NODES, dtype=jnp.int32)
        W = jax.random.normal(k3, (DIM, DIM), dtype=jnp.float32) / np.sqrt(DIM)
        b = jnp.zeros((DIM,), dtype=jnp.float32)
        return {'x': x, 'edge_index': edge_index, 'W': W, 'b': b}
    _L0_gnn_all = _L0_gnn_setup()
    _L0_gnn_in = {k: v for k, v in _L0_gnn_all.items() if k in ('W', 'b')}
    del _L0_gnn_all

    def _L0_mix_setup():
        import jax, jax.numpy as jnp
        import numpy as np
        NUM_HEADS = 12
        EPS = 0.0001

        def softmax_kernel(data, proj, is_query):
            d = data.shape[-1]
            data_normalizer = d ** (-0.25)
            ratio = proj.shape[0] ** (-0.5)
            data_dash = jnp.einsum('bhnd,md->bhnm', data_normalizer * data, proj)
            diag = jnp.sum(data * data, axis=-1, keepdims=True) * 0.5 * data_normalizer ** 2
            if is_query:
                m = jnp.max(data_dash, axis=-1, keepdims=True)
            else:
                m = jnp.max(data_dash, axis=(-3, -2, -1), keepdims=True)
            return ratio * (jnp.exp(data_dash - diag - m) + EPS)
        key = jax.random.key(seed)
        ks = jax.random.split(key, 5)
        B, N, C = (8, 512, 768)
        x = jax.random.normal(ks[0], (B, N, C), dtype=jnp.float32)
        w_qkv = jax.random.normal(ks[1], (3 * C, C), dtype=jnp.float32) * 0.02
        w_proj = jax.random.normal(ks[2], (C, C), dtype=jnp.float32) * 0.02
        b_proj = jnp.zeros((C,), dtype=jnp.float32)
        proj_mat = jax.random.normal(ks[3], (256, C // NUM_HEADS), dtype=jnp.float32)
        return {'x': x, 'w_qkv': w_qkv, 'w_proj': w_proj, 'b_proj': b_proj, 'proj_mat': proj_mat}
    _L0_mix_all = _L0_mix_setup()
    _L0_mix_in = {k: v for k, v in _L0_mix_all.items() if k in ('w_qkv', 'w_proj', 'b_proj', 'proj_mat')}
    del _L0_mix_all

    def _L0_ffn_setup():
        import jax, jax.numpy as jnp
        import numpy as np
        TOP_K = 2
        ROUTED_SCALE = 1.0

        def _swiglu_all(x, gw, uw, dw):
            g = jnp.einsum('th,eih->tei', x, gw)
            u = jnp.einsum('th,eih->tei', x, uw)
            h = jax.nn.silu(g) * u
            return jnp.einsum('tei,ehi->teh', h, dw)
        key = jax.random.key(seed)
        ks = jax.random.split(key, 8)
        B, S, H, I, E, NS = (2, 1024, 768, 384, 8, 2)
        w = lambda k, shape: jax.random.normal(k, shape, jnp.float32) * 0.02
        return {'hidden_states': jax.random.normal(ks[0], (B, S, H), jnp.float32), 'gate_w': w(ks[1], (E, H)), 'shared_gate': w(ks[2], (NS, I, H)), 'shared_up': w(ks[3], (NS, I, H)), 'shared_down': w(ks[4], (NS, H, I)), 'routed_gate': w(ks[5], (E, I, H)), 'routed_up': w(ks[6], (E, I, H)), 'routed_down': w(ks[7], (E, H, I))}
    _L0_ffn_all = _L0_ffn_setup()
    _L0_ffn_in = {k: v for k, v in _L0_ffn_all.items() if k in ('gate_w', 'shared_gate', 'shared_up', 'shared_down', 'routed_gate', 'routed_up', 'routed_down')}
    del _L0_ffn_all
    return {'x': x, 'src': src, 'dst': dst, 'L0_gnn_W': _L0_gnn_in['W'], 'L0_gnn_b': _L0_gnn_in['b'], 'L0_mix_w_qkv': _L0_mix_in['w_qkv'], 'L0_mix_w_proj': _L0_mix_in['w_proj'], 'L0_mix_b_proj': _L0_mix_in['b_proj'], 'L0_mix_proj_mat': _L0_mix_in['proj_mat'], 'L0_ffn_gate_w': _L0_ffn_in['gate_w'], 'L0_ffn_shared_gate': _L0_ffn_in['shared_gate'], 'L0_ffn_shared_up': _L0_ffn_in['shared_up'], 'L0_ffn_shared_down': _L0_ffn_in['shared_down'], 'L0_ffn_routed_gate': _L0_ffn_in['routed_gate'], 'L0_ffn_routed_up': _L0_ffn_in['routed_up'], 'L0_ffn_routed_down': _L0_ffn_in['routed_down']}

def reference(x, src, dst, L0_gnn_W, L0_gnn_b, L0_mix_w_qkv, L0_mix_w_proj, L0_mix_b_proj, L0_mix_proj_mat, L0_ffn_gate_w, L0_ffn_shared_gate, L0_ffn_shared_up, L0_ffn_shared_down, L0_ffn_routed_gate, L0_ffn_routed_up, L0_ffn_routed_down):
    import jax
    import jax.numpy as jnp

    def _L0_gnn_ref(x, edge_index, W, b):
        import jax, jax.numpy as jnp
        import numpy as np
        N_NODES = 1250
        N_EDGES = 12500
        DIM = 768
        n = x.shape[0]
        loop = jnp.arange(n, dtype=edge_index.dtype)
        src = jnp.concatenate([edge_index[0], loop])
        dst = jnp.concatenate([edge_index[1], loop])
        deg = jax.ops.segment_sum(jnp.ones_like(dst, dtype=x.dtype), dst, num_segments=n)
        deg_inv_sqrt = jnp.where(deg > 0, jax.lax.rsqrt(deg), 0.0)
        norm = deg_inv_sqrt[src] * deg_inv_sqrt[dst]
        h = x @ W
        msg = h[src] * norm[:, None]
        out = jax.ops.segment_sum(msg, dst, num_segments=n)
        return out + b

    def _L0_mix_ref(x, w_qkv, w_proj, b_proj, proj_mat):
        import jax, jax.numpy as jnp
        import numpy as np
        NUM_HEADS = 12
        EPS = 0.0001

        def softmax_kernel(data, proj, is_query):
            d = data.shape[-1]
            data_normalizer = d ** (-0.25)
            ratio = proj.shape[0] ** (-0.5)
            data_dash = jnp.einsum('bhnd,md->bhnm', data_normalizer * data, proj)
            diag = jnp.sum(data * data, axis=-1, keepdims=True) * 0.5 * data_normalizer ** 2
            if is_query:
                m = jnp.max(data_dash, axis=-1, keepdims=True)
            else:
                m = jnp.max(data_dash, axis=(-3, -2, -1), keepdims=True)
            return ratio * (jnp.exp(data_dash - diag - m) + EPS)
        B, N, C = x.shape
        H = NUM_HEADS
        d = C // H
        qkv = (x @ w_qkv.T).reshape(B, N, 3, H, d).transpose(2, 0, 3, 1, 4)
        q, k, v = (qkv[0], qkv[1], qkv[2])
        q_prime = softmax_kernel(q, proj_mat, is_query=True)
        k_prime = softmax_kernel(k, proj_mat, is_query=False)
        k_sum = jnp.sum(k_prime, axis=-2)
        d_inv = 1.0 / jnp.einsum('bhnm,bhm->bhn', q_prime, k_sum)
        context = jnp.einsum('bhnm,bhnd->bhmd', k_prime, v)
        out = jnp.einsum('bhnm,bhmd,bhn->bhnd', q_prime, context, d_inv)
        out = out.transpose(0, 2, 1, 3).reshape(B, N, C)
        return out @ w_proj.T + b_proj

    def _L0_ffn_ref(hidden_states, gate_w, shared_gate, shared_up, shared_down, routed_gate, routed_up, routed_down):
        import jax, jax.numpy as jnp
        import numpy as np
        TOP_K = 2
        ROUTED_SCALE = 1.0

        def _swiglu_all(x, gw, uw, dw):
            g = jnp.einsum('th,eih->tei', x, gw)
            u = jnp.einsum('th,eih->tei', x, uw)
            h = jax.nn.silu(g) * u
            return jnp.einsum('tei,ehi->teh', h, dw)
        B, S, H = hidden_states.shape
        T = B * S
        x = hidden_states.reshape(T, H)
        router_logits = x @ gate_w.T
        scores = jax.nn.softmax(router_logits, axis=-1)
        _, topk_idx = jax.lax.top_k(scores, TOP_K)
        topk_w = jnp.take_along_axis(scores, topk_idx, axis=-1)
        topk_w = topk_w / (topk_w.sum(axis=-1, keepdims=True) + 1e-08)
        topk_w = topk_w * ROUTED_SCALE
        E = gate_w.shape[0]
        combine = jnp.zeros((T, E), scores.dtype).at[jnp.arange(T)[:, None], topk_idx].add(topk_w)
        routed_all = _swiglu_all(x, routed_gate, routed_up, routed_down)
        routed_out = jnp.einsum('teh,te->th', routed_all, combine)
        NS = shared_gate.shape[0]
        shared_all = _swiglu_all(x, shared_gate, shared_up, shared_down)
        shared_out = shared_all.sum(axis=1) / NS
        out = (shared_out + routed_out).reshape(B, S, H)
        return out
    edge_index = jnp.stack([src, dst])
    xn = _layernorm(x, axis=-1)
    x = x + _L0_gnn_ref(xn, edge_index, L0_gnn_W, L0_gnn_b) + _L0_mix_ref(xn[None], L0_mix_w_qkv, L0_mix_w_proj, L0_mix_b_proj, L0_mix_proj_mat)[0]
    x = x + _L0_ffn_ref(_layernorm(x, axis=-1)[None], L0_ffn_gate_w, L0_ffn_shared_gate, L0_ffn_shared_up, L0_ffn_shared_down, L0_ffn_routed_gate, L0_ffn_routed_up, L0_ffn_routed_down)[0]
    return x

_drawn_inputs = setup_inputs


def setup_inputs(seed=0):
    import zlib

    import numpy as np

    out = dict(_drawn_inputs(seed))
    spreads = {'L0_gnn_b': (0.0, 0.1), 'L0_mix_b_proj': (0.0, 0.1)}
    factors = {'L0_mix_w_qkv': 5.653, 'L0_mix_w_proj': 6.402, 'L0_mix_proj_mat': 8.0}
    for name, (base, spread) in spreads.items():
        noise = np.random.default_rng([zlib.crc32(name.encode()), seed]).standard_normal(out[name].shape)
        drawn = base * np.exp(spread * noise) if base else spread * noise
        out[name] = jnp.asarray(drawn.astype(out[name].dtype))
    for name, factor in factors.items():
        out[name] = (out[name] * factor).astype(out[name].dtype)
    return out
```

```python
from contextlib import ExitStack

import concourse.bass as bass
from concourse import mybir

F32, F32R = mybir.dt.float32, mybir.dt.float32r
BF16, I32, I16, U32 = mybir.dt.bfloat16, mybir.dt.int32, mybir.dt.int16, mybir.dt.uint32
ALU = mybir.AluOpType
ACT = mybir.ActivationFunctionType
X = mybir.AxisListType.X

T, C = 1250, 768
P = 128
NT, TP = 10, 125
KB = C // P
HC = C // 2
CH = 418
CHUNKS = [(c, min(CH, T - c)) for c in range(0, T, CH)]
CHUNK_AT = [c for c, _ in CHUNKS]
LN_EPS = 1e-5

E_EDGES = 20000
EJ = E_EDGES // TP
NG = NT * len(CHUNKS)
EPAD = 512
NBATCH = (E_EDGES + NG * (EPAD - 1)) // EPAD
NBATCH += NBATCH % 2
ECOLS = NBATCH * EPAD // P
SCAT = 8

H, D, M = 12, 64, 256
HP = H // 2
DV = D + 2
NORM = float(D) ** -0.25
DIAG = 0.5 * float(D) ** -0.5
FEPS = 1e-4

NE, NS, I = 8, 2, 384
IB = I // P
TOPK = 2
UT = 256
NR = (T * TOPK + NE * (UT - 1)) // UT
SU = -(-T // UT)
NU = NR + NS * SU
UCOLS = NU * UT // P
RCOLS = NR * UT // P
TJ = NT * TOPK


def f32(ap):
    return ap.bitcast(F32)


class Chain:

    def __init__(self, sem):
        self.eng, self.sem, self.n = None, sem, 0

    def on(self, eng):
        self.eng = eng
        return self

    def __call__(self, ins):
        self.n += 1
        ins.then_inc(self.sem, 1)
        self.eng.wait_ge(self.sem, self.n)


def wait_alone(pool, sem, value, passed):
    pool.wait_ge(sem, value)
    pool.sem_inc(passed, 1)


def refine_rsqrt(dve, own, r, v, work):
    own(dve.tensor_tensor(work, r, r, ALU.mult))
    own(dve.tensor_tensor(work, work, v, ALU.mult))
    own(dve.tensor_scalar(work, work, -0.5, 1.5, ALU.mult, ALU.add))
    return dve.tensor_tensor(r, r, work, ALU.mult)


def three_products(pe, out, a_hi, a_lo, b_hi, b_lo, k, n):
    pe.matmul(out, a_hi, b_hi, start=(k == 0), stop=False)
    pe.matmul(out, a_hi, b_lo, start=False, stop=False)
    return pe.matmul(out, a_lo, b_hi, start=False, stop=(k == n - 1))


def program(nc, a, out):
    with ExitStack() as whole:
        sems = {}

        def sem(name):
            if name not in sems:
                sems[name] = whole.enter_context(nc.semaphore(name))
            return sems[name]

        def keep(name, shape, dtype, where=whole):
            return where.enter_context(nc.sbuf_tensor(name, shape, dtype))

        def dram(name, shape, dtype=F32):
            return nc.dram_tensor(name, shape, dtype, kind="Internal").ap()

        m = {
            "a": a, "out": out, "sem": sem, "keep": keep,
            "banks": [whole.enter_context(nc.psum_tensor(f"bank{i}", [P, 512], F32)) for i in range(8)],
            "ident": keep("ident", [P, P], F32),
            "before": keep("before", [P, P], F32),
            "ones": keep("ones", [P, P], F32),
            "batch_group": keep("batch_group", [1, NBATCH], I32),
            "passed": sem("passed"),
            "own": Chain(sem("dve_own")),
            "hv": dram("hv", [2, T, C]),
            "qk": dram("qk", [2, C, T]),
            "edges": dram("edges", [P * ECOLS, 2]),
            "xn2": dram("xn2", [T, C]),
            "slots": dram("slots", [P * RCOLS, 2]),
            "y": dram("y", [NU * UT, C]),
        }
        with ExitStack() as early:
            m["xn_hi"] = keep("xn_hi", [P, KB, T], F32R, early)
            m["xn_lo"] = keep("xn_lo", [P, KB, T], F32R, early)
            first_norm(nc, m)
            projections(nc, m)
        m["x1"] = keep("x1", [TP, NT, C], F32)
        graph(nc, m)
        m["slot_table"] = keep("slot_table", [P, UCOLS, 2], F32)
        m["slot_of"] = keep("slot_of", [TP, TJ], I32)
        m["unit_expert"] = keep("unit_expert", [1, NU], I32)
        with ExitStack() as mid:
            m["ctx_hi"] = keep("ctx_hi", [P, H, 2, DV], F32R, mid)
            m["ctx_lo"] = keep("ctx_lo", [P, H, 2, DV], F32R, mid)
            m["proj_hi"] = keep("proj_hi", [P, M], F32R, mid)
            m["proj_lo"] = keep("proj_lo", [P, M], F32R, mid)
            m["head_mask"] = keep("head_mask", [P, 2], F32, mid)
            keys(nc, m)
            m["att_hi"] = keep("att_hi", [P, HP, T], F32R, mid)
            m["att_lo"] = keep("att_lo", [P, HP, T], F32R, mid)
            queries(nc, m)
            mix_and_route(nc, m)
        experts(nc, m)
        combine(nc, m)


def first_norm(nc, m):
    a, sem, banks, ident = m["a"], m["sem"], m["banks"], m["ident"]
    with ExitStack() as ctx:
        x_in = m["keep"]("x_in", [TP, NT, C], F32, ctx)
        stats = m["keep"]("stats", [TP, NT, 2, 6], F32, ctx)
        mean_var = m["keep"]("mean_var", [TP, NT, 2], F32, ctx)
        spread = m["keep"]("spread", [TP, NT], F32, ctx)
        rstd = m["keep"]("rstd", [TP, NT], F32, ctx)
        work = m["keep"]("newton", [TP, NT], F32, ctx)
        zeros = m["keep"]("zeros", [P, RCOLS * 2], F32, ctx)
        filler = m["keep"]("filler", [P, ECOLS * 2], F32, ctx)
        x_loaded = [sem(f"x_loaded{i}") for i in range(NT // 2)]
        consts = sem("consts")
        var_ready, sd_ready, xn_ready = sem("var_ready"), sem("sd_ready"), sem("xn_ready")
        turned, hi_done, lo_done, filled = sem("turned"), sem("n1_hi"), sem("n1_lo"), sem("filled")
        NB = 4
        block = ctx.enter_context(nc.Block())

        @block.sync
        def _(sp):
            for i in range(0, NT, 2):
                sp.dma_start(x_in[:, i:i + 2, :], a["x"][i * TP:(i + 2) * TP, :].rearrange("(i p) c -> p i c", p=TP)
                             ).then_inc(x_loaded[i // 2], 16)
            sp.wait_ge(consts, 4)
            sp.dma_start(m["edges"].rearrange("(p c) k -> p (c k)", p=P), filler[:]).then_inc(filled, 16)
            sp.wait_ge(consts, 5)
            sp.dma_start(m["slots"].rearrange("(p c) k -> p (c k)", p=P),
                         zeros[:]).then_inc(filled, 16)
            sp.wait_ge(filled, 32)

        @block.gpsimd
        def _(pool):
            pool.memset(m["ones"][:], 1.0).then_inc(consts, 1)
            pool.wait_ge(consts, 1)
            pool.affine_select(out=ident[:], in_=m["ones"][:], compare_op=ALU.is_equal, fill=0.0, base=0,
                               pattern=[[-1, P]], channel_multiplier=1).then_inc(consts, 1)
            pool.affine_select(out=m["before"][:], in_=m["ones"][:], compare_op=ALU.is_gt, fill=0.0, base=0,
                               pattern=[[1, P]], channel_multiplier=-1).then_inc(consts, 1)
            pool.memset(filler[:], -1.0).then_inc(consts, 1)
            pool.memset(zeros[:], 0.0).then_inc(consts, 1)

        @block.vector
        def _(dve):
            own = m["own"].on(dve)
            for i in range(NT):
                dve.wait_ge(x_loaded[i // 2], 16)
                for h in range(2):
                    last = dve.bn_stats(stats[:, i, h, :], x_in[:, i, h * HC:(h + 1) * HC])
            own(last)
            for i in range(NT):
                last = dve.bn_aggr(mean_var[:, i, :], stats[:, i, :, :])
            own(last)
            dve.tensor_scalar(spread[:], mean_var[:, :, 1], LN_EPS, None, ALU.add).then_inc(var_ready, 1)
            dve.wait_ge(sd_ready, 1)
            own(dve.reciprocal(rstd[:], rstd[:]))
            own(refine_rsqrt(dve, own, rstd[:], spread[:], work[:]))

            def lows(n):
                dve.wait_ge(hi_done, n + 1)
                i, h = n // 2, n % 2
                at = (slice(None), slice(3 * h, 3 * h + 3), slice(i * TP, (i + 1) * TP))
                dve.tensor_tensor(m["xn_lo"][at], banks[n % NB][:, 0:3 * TP].rearrange("p (b t) -> p b t", b=3),
                                  f32(m["xn_hi"][at]), ALU.subtract).then_inc(lo_done, 1)

            for i in range(NT):
                dve.tensor_scalar(x_in[:, i, :], x_in[:, i, :], mean_var[:, i, 0:1], rstd[:, i:i + 1],
                                  ALU.subtract, ALU.mult).then_inc(xn_ready, 1)
                if i:
                    lows(2 * i - 2)
                    lows(2 * i - 1)
            lows(2 * NT - 2)
            lows(2 * NT - 1)

        @block.scalar
        def _(act):
            act.wait_ge(var_ready, 1)
            act.activation(rstd[:], spread[:], ACT.Sqrt).then_inc(sd_ready, 1)
            for n in range(2 * NT):
                i, h = n // 2, n % 2
                act.wait_ge(turned, n + 1)
                act.activation(m["xn_hi"][:, 3 * h:3 * h + 3, i * TP:(i + 1) * TP],
                               banks[n % NB][:, 0:3 * TP].rearrange("p (b t) -> p b t", b=3),
                               ACT.Copy).then_inc(hi_done, 1)

        @block.tensor
        def _(pe):
            pe.wait_ge(consts, 3)
            for n in range(2 * NT):
                i, h = n // 2, n % 2
                pe.wait_ge(xn_ready, i + 1)
                if n >= NB:
                    pe.wait_ge(lo_done, n - NB + 1)
                for b in range(3):
                    k = 3 * h + b
                    last = pe.transpose(banks[n % NB][:, b * TP:(b + 1) * TP],
                                        x_in[:, i, k * P:(k + 1) * P], ident[0:TP, 0:TP])
                last.then_inc(turned, 1)


def find_slots(dve, own, pe_ready, pe_done, s, group, groups, per, pad):
    shape = [TP, groups, per]
    own(dve.tensor_tensor(s["hot"], group.unsqueeze(1).broadcast_to(shape),
                          s["iota"].unsqueeze(2).broadcast_to(shape), ALU.is_equal))
    flat = "p g j -> p (g j)"
    own(dve.tensor_tensor_scan(s["rank"].rearrange(flat), s["keep_on"].rearrange(flat),
                               s["hot"].rearrange(flat), 0.0, ALU.mult, ALU.add))
    dve.tensor_copy(s["total"], s["rank"][:, :, per - 1]).then_inc(pe_ready, 1)
    dve.wait_ge(pe_done, 1)
    own(dve.tensor_scalar(s["count"], s["sums"][:, groups:2 * groups], float(pad - 1), None, ALU.add))
    own(dve.tensor_scalar(s["count"], s["count"], pad.bit_length() - 1, None, ALU.logical_shift_right))
    own(dve.tensor_copy(s["batches"], s["count"]))
    own(dve.tensor_tensor_scan(s["upto"], s["ones"], s["batches"], 0.0, ALU.mult, ALU.add))
    own(dve.tensor_tensor(s["base"], s["upto"], s["batches"], ALU.subtract))
    own(dve.tensor_scalar(s["base"], s["base"], float(pad), -1.0, ALU.mult, ALU.add))
    own(dve.tensor_tensor(s["base"], s["sums"][:, 0:groups], s["base"], ALU.add))
    own(dve.tensor_tensor(s["wide"], s["rank"], s["base"].unsqueeze(2).broadcast_to(shape), ALU.add))
    own(dve.tensor_tensor(s["wide"], s["wide"], s["hot"], ALU.mult))
    own(dve.tensor_reduce(s["slot"], s["wide"].rearrange("p g j -> p j g"), X, ALU.add))


def table_rows(dve, own, s, cols):
    own(dve.tensor_copy(s["slot_i"], s["slot"]))
    own(dve.tensor_scalar(s["part"], s["slot_i"], P - 1, None, ALU.bitwise_and))
    own(dve.tensor_scalar(s["col"], s["slot_i"], P.bit_length() - 1, None, ALU.logical_shift_right))
    return dve.scalar_tensor_tensor(s["row"], s["part"], float(cols), s["col"], ALU.mult, ALU.add)


def slot_buffers(m, ctx, name, groups, per, wide):
    k = m["keep"]
    s = {
        "iota": k(name + "_iota", [TP, groups], F32, ctx)[:],
        "hot": k(name + "_hot", [TP, groups, per], BF16, ctx)[:],
        "keep_on": k(name + "_keep_on", [TP, groups, per], BF16, ctx)[:],
        "rank": k(name + "_rank", [TP, groups, per], BF16, ctx)[:],
        "wide": wide,
        "ones": m["ones"][0:TP, 0:groups],
    }
    for n in ("total", "batches", "upto", "base"):
        s[n] = k(f"{name}_{n}", [TP, groups], F32, ctx)[:]
    s["count"] = k(name + "_count", [TP, groups], I32, ctx)[:]
    s["slot"] = k(name + "_slot", [TP, per], F32, ctx)[:]
    for n in ("slot_i", "part", "col", "row"):
        s[n] = k(f"{name}_{n}", [TP, per], I32, ctx)[:]
    return s


def projections(nc, m):
    a, sem, banks = m["a"], m["sem"], m["banks"]
    keep = m["keep"]
    NPIECE = 8
    NB = 6
    with ExitStack() as ctx:
        raw = [keep(f"raw{i}", [P, KB, HC], F32, ctx) for i in range(2)]
        w_hi = [keep(f"w_hi{i}", [P, KB, HC], F32R, ctx) for i in range(2)]
        w_lo = [keep(f"w_lo{i}", [P, KB, HC], F32R, ctx) for i in range(2)]
        stage = [keep(f"stage{i}", [P, NT * HC], F32, ctx) for i in range(2)]
        src_i = keep("src_i", [TP, EJ], I32, ctx)
        dst_i = keep("dst_i", [TP, EJ], I32, ctx)
        src_f = keep("src_f", [TP, EJ], F32, ctx)
        dst_f = keep("dst_f", [TP, EJ], F32, ctx)
        tile_f = keep("tile_f", [TP, EJ], F32, ctx)
        chunk_f = keep("chunk_f", [TP, EJ], F32, ctx)
        group = keep("group", [TP, EJ], F32, ctx)
        pair = keep("pair", [TP, EJ, 2], F32, ctx)
        wide = keep("wide", [TP, NG, EJ], F32, ctx)
        s = slot_buffers(m, ctx, "edge", NG, EJ, wide[:])
        s["sums"] = banks[7][0:TP, 0:2 * NG]
        batch_iota = keep("batch_iota", [1, NBATCH], F32, ctx)
        set_row = [keep(f"set_row{i}", [TP, SCAT], I32, ctx) for i in range(2)]
        set_pair = [keep(f"set_pair{i}", [TP, SCAT, 2], F32, ctx) for i in range(2)]

        w_loaded, stored = [sem("w_loaded0"), sem("w_loaded1")], [sem("stored0"), sem("stored1")]
        hi_ready, lo_ready = sem("w_hi"), sem("w_lo")
        product, evacuated = sem("product"), sem("evacuated")
        e_loaded, e_const = sem("e_loaded"), sem("e_const")
        totals_ready, sums_ready, rows_ready = sem("totals_ready"), sem("sums_ready"), sem("rows_ready")
        set_filled, scattered = sem("set_filled"), [sem("scattered0"), sem("scattered1")]

        def groups_upto(n):
            return NT * min(n, 4) + KB // 2 * len(CHUNKS) * max(n - 4, 0)

        def bank_of(n, j):
            return (n * NT + j) % NB if n < 4 else (4 * NT + n % 2 * 9 + j) % NB

        block = ctx.enter_context(nc.Block())

        @block.sync
        def _(sp):
            sp.dma_start(src_i[:], a["src"].rearrange("(p j) -> p j", p=TP)).then_inc(e_loaded, 16)
            sp.dma_start(dst_i[:], a["dst"].rearrange("(p j) -> p j", p=TP)).then_inc(e_loaded, 16)
            for n in range(NPIECE + 2):
                if n < NPIECE:
                    if n >= 2:
                        sp.wait_ge(lo_ready, n - 1)
                    sp.dma_start(raw[n % 2][:], a["w_pieces"][n].rearrange("p (k c) -> p k c", k=KB)
                                 ).then_inc(w_loaded[n % 2], 16)
                if n >= 2:
                    q = n - 2
                    sp.wait_ge(evacuated, NB + groups_upto(q + 1))
                    half = slice((q % 2) * HC, (q % 2 + 1) * HC)
                    if q < 4:
                        sp.dma_start(m["hv"][q // 2, :, half].rearrange("(i p) c -> p i c", p=TP),
                                     stage[q % 2][0:TP, :].rearrange("p (i c) -> p i c", i=NT)
                                     ).then_inc(stored[q % 2], 16)
                    else:
                        sp.dma_start(m["qk"][q // 2 - 2, half, :].rearrange("(b p) t -> p b t", p=P),
                                     stage[q % 2][:, 0:3 * T].rearrange("p (b t) -> p b t", b=3)
                                     ).then_inc(stored[q % 2], 16)
            for done in stored:
                sp.wait_ge(done, 8 * NPIECE)

        @block.tensor
        def _(pe):
            def piece(n, at, kind):
                pe.wait_ge(lo_ready, n + 1)
                if kind == "tokens":
                    for i in range(NT):
                        g = n * NT + i
                        pe.wait_ge(evacuated, g + 1)
                        bank = banks[bank_of(n, i)]
                        for k in range(KB):
                            last = three_products(
                                pe, bank[0:TP, 0:HC], m["xn_hi"][:, k, i * TP:(i + 1) * TP],
                                m["xn_lo"][:, k, i * TP:(i + 1) * TP], w_hi[at][:, k, :], w_lo[at][:, k, :], k, KB)
                        last.then_inc(product, 1)
                else:
                    for b in range(3):
                        for c, (c0, cn) in enumerate(CHUNKS):
                            j = 3 * b + c
                            pe.wait_ge(evacuated, n * 9 + 4 + j + 1)
                            bank = banks[bank_of(4 + at, j)]
                            for k in range(KB):
                                last = three_products(
                                    pe, bank[:, 0:cn], w_hi[at][:, k, b * P:(b + 1) * P],
                                    w_lo[at][:, k, b * P:(b + 1) * P], m["xn_hi"][:, k, c0:c0 + cn],
                                    m["xn_lo"][:, k, c0:c0 + cn], k, KB)
                            last.then_inc(product, 1)

            piece(0, 0, "tokens")
            piece(1, 1, "tokens")
            pe.wait_ge(totals_ready, 1)
            pe.matmul(s["sums"][:, 0:NG], m["before"][0:TP, 0:TP], s["total"], start=True, stop=True)
            pe.matmul(s["sums"][:, NG:2 * NG], m["ones"][0:TP, 0:TP], s["total"], start=True,
                      stop=True).then_inc(sums_ready, 1)
            piece(2, 0, "tokens")
            piece(3, 1, "tokens")
            with pe.Fori(4, 8, 2) as n:
                piece(n, 0, "features")
                piece(n + 1, 1, "features")

        @block.scalar
        def _(act):
            def high(n):
                act.wait_ge(w_loaded[n % 2], 16 * (n // 2 + 1))
                act.activation(w_hi[n % 2][:], raw[n % 2][:], ACT.Copy).then_inc(hi_ready, 1)

            act.sem_inc(evacuated, NB)
            high(0)
            high(1)
            g = 0
            for n in range(NPIECE):
                if n >= 2:
                    act.wait_ge(stored[n % 2], 16 * (n // 2))
                if n < 4:
                    for i in range(NT):
                        act.wait_ge(product, g + 1)
                        act.activation(stage[n % 2][0:TP, i * HC:(i + 1) * HC], banks[bank_of(n, i)][0:TP, 0:HC],
                                       ACT.Copy).then_inc(evacuated, 1)
                        g += 1
                else:
                    for j in range(9):
                        b, (c0, cn) = j // 3, CHUNKS[j % 3]
                        act.wait_ge(product, g + 1)
                        act.activation(stage[n % 2][:, b * T + c0:b * T + c0 + cn],
                                       banks[bank_of(n, j)][:, 0:cn], ACT.Copy).then_inc(evacuated, 1)
                        g += 1
                if n + 2 < NPIECE:
                    high(n + 2)

        @block.vector
        def _(dve):
            own = m["own"].on(dve)

            def low(n):
                dve.wait_ge(hi_ready, n + 1)
                dve.tensor_tensor(w_lo[n % 2][:], raw[n % 2][:], f32(w_hi[n % 2][:]),
                                  ALU.subtract).then_inc(lo_ready, 1)

            low(0)
            low(1)
            dve.wait_ge(e_loaded, 32)
            dve.tensor_copy(src_f[:], src_i[:])
            own(dve.tensor_copy(dst_f[:], dst_i[:]))
            own(dve.tensor_scalar(tile_f[:], src_f[:], float(TP), None, ALU.is_ge))
            own(dve.tensor_scalar(chunk_f[:], dst_f[:], float(CHUNK_AT[1]), None, ALU.is_ge))
            for i in range(2, NT):
                own(dve.scalar_tensor_tensor(tile_f[:], src_f[:], float(i * TP), tile_f[:], ALU.is_ge, ALU.add))
            own(dve.scalar_tensor_tensor(dst_f[:], chunk_f[:], -float(CHUNK_AT[1]), dst_f[:], ALU.mult, ALU.add))
            own(dve.tensor_scalar(group[:], dst_f[:], float(CHUNK_AT[2] - CHUNK_AT[1]), None, ALU.is_ge))
            own(dve.tensor_tensor(group[:], group[:], chunk_f[:], ALU.mult))
            own(dve.tensor_tensor(chunk_f[:], chunk_f[:], group[:], ALU.add))
            own(dve.scalar_tensor_tensor(pair[:, :, 1], group[:], -float(CHUNK_AT[2] - CHUNK_AT[1]), dst_f[:],
                                         ALU.mult, ALU.add))
            dve.scalar_tensor_tensor(pair[:, :, 0], tile_f[:], -float(TP), src_f[:], ALU.mult, ALU.add)
            own(dve.scalar_tensor_tensor(group[:], tile_f[:], float(len(CHUNKS)), chunk_f[:], ALU.mult, ALU.add))
            dve.wait_ge(e_const, 4)
            find_slots(dve, own, totals_ready, sums_ready, s, group[:], NG, EJ, EPAD)
            table_rows(dve, own, s, ECOLS).then_inc(rows_ready, 1)
            first = wide[0:1, 0:NG, 0:NBATCH]
            own(dve.tensor_tensor(first, batch_iota[:].unsqueeze(1).broadcast_to([1, NG, NBATCH]),
                                  s["upto"][0:1, :].unsqueeze(2).broadcast_to([1, NG, NBATCH]), ALU.is_ge))
            own(dve.tensor_reduce(batch_iota[:], first.rearrange("p g j -> p j g"), X, ALU.add))
            own(dve.tensor_scalar(m["batch_group"][:], batch_iota[:], float(NG - 1), None, ALU.min))
            for n in range(2, NPIECE):
                low(n)

        @block.gpsimd
        def _(pool):
            pool.iota(s["iota"], [[1, NG]], base=0, channel_multiplier=0,
                      allow_small_or_imprecise_dtypes=True).then_inc(e_const, 1)
            pool.iota(batch_iota[:], [[1, NBATCH]], base=0, channel_multiplier=0,
                      allow_small_or_imprecise_dtypes=True).then_inc(e_const, 1)
            pool.memset(s["keep_on"], 1.0).then_inc(e_const, 1)
            pool.wait_ge(e_const, 3)
            pool.memset(s["keep_on"][:, :, 0:1], 0.0).then_inc(e_const, 1)

            def send(n, at, turn):
                if turn is not None:
                    wait_alone(pool, scattered[at], 16 * SCAT * turn, m["passed"])
                pool.tensor_copy(set_row[at][:], s["row"][:, bass.ds(n * SCAT, SCAT)])
                pool.tensor_copy(set_pair[at][:], pair[:, bass.ds(n * SCAT, SCAT), :]).then_inc(set_filled, 1)
                wait_alone(pool, set_filled, n + 1, m["passed"])
                for u in range(SCAT):
                    pool.indirect_dma_start(m["edges"], bass.IndirectOffsetOnAxis(ap=set_row[at][:, u:u + 1], axis=0),
                                            set_pair[at][:, u, :], None).then_inc(scattered[at], 16)

            pool.wait_ge(rows_ready, 1)
            send(0, 0, None)
            send(1, 1, None)
            turns = EJ // SCAT // 2
            with pool.Fori(1, turns) as t:
                send(2 * t, 0, t)
                send(2 * t + 1, 1, t)
            pool.wait_ge(scattered[0], 16 * SCAT * turns)
            pool.wait_ge(scattered[1], 16 * SCAT * turns)


def graph(nc, m):
    a, sem, banks, keep, x1 = m["a"], m["sem"], m["banks"], m["keep"], m["x1"]
    AW = len(CHUNKS) * CH
    U = EPAD // P
    NHOT = 2 * U
    with ExitStack() as ctx:
        adj = keep("adj", [TP, NT * AW], F32, ctx)
        adj3 = adj[:].rearrange("p (a d) -> p a d", a=NT)
        table = keep("table", [P, ECOLS, 2], F32, ctx)
        iota = keep("iota", [P, CH], I16, ctx)
        hot_src = [keep(f"hot_src{i}", [P, TP], BF16, ctx) for i in range(NHOT)]
        hot_dst = [keep(f"hot_dst{i}", [P, CH], BF16, ctx) for i in range(NHOT)]
        h_in = [keep(f"h_in{i}", [TP, C], F32, ctx) for i in range(2)]
        h_hi = keep("h_hi", [TP, NT, C], F32R, ctx)
        h_lo = keep("h_lo", [TP, NT, C], F32R, ctx)
        a_hi = [keep(f"a_hi{i}", [TP, NT, TP], F32R, ctx) for i in range(2)]
        a_lo = [keep(f"a_lo{i}", [TP, NT, TP], F32R, ctx) for i in range(2)]
        bias = keep("bias", [TP, 2, C], F32, ctx)
        dis = keep("dis", [TP, NT], F32, ctx)
        dis_work = keep("dis_work", [TP, NT], F32, ctx)

        table_in, x_in, h_loaded = sem("table_in"), sem("g_x_in"), [sem("h_loaded0"), sem("h_loaded1")]
        consts, adj_zero, hot_ready, hot_used = sem("g_consts"), sem("adj_zero"), sem("hot_ready"), sem("hot_used")
        added = sem("added")
        degree_ready, sd_ready, dis_ready = sem("degree_ready"), sem("g_sd"), sem("dis_ready")
        h_hi_ready, h_lo_ready = sem("h_hi_ready"), sem("h_lo_ready")
        a_hi_ready, a_lo_ready, row_done, row_read = sem("a_hi"), sem("a_lo"), sem("row_done"), sem("row_read")
        bias_ready = sem("bias_ready")
        block = ctx.enter_context(nc.Block())

        @block.sync
        def _(sp):
            sp.dma_start(table[:].rearrange("p c k -> p (c k)"), m["edges"].rearrange("(p c) k -> p (c k)", p=P)
                         ).then_inc(table_in, 16)
            sp.dma_start(x1[:], a["x"].rearrange("(i p) c -> p i c", p=TP)).then_inc(x_in, 16)
            sp.dma_start(bias[:, 0, :], a["gnn_b"].partition_broadcast(TP)).then_inc(x_in, 16)
            sp.dma_start(bias[:, 1, :], a["b_proj"].partition_broadcast(TP)).then_inc(x_in, 16)
            for i in range(NT):
                if i >= 2:
                    sp.wait_ge(h_lo_ready, i - 1)
                sp.dma_start(h_in[i % 2][:], m["hv"][0, i * TP:(i + 1) * TP, :]).then_inc(h_loaded[i % 2], 16)

        @block.gpsimd
        def _(pool):
            pool.iota(iota[:], [[1, CH]], base=0, channel_multiplier=0,
                      allow_small_or_imprecise_dtypes=True).then_inc(consts, 1)
            pool.memset(adj[:], 0.0).then_inc(adj_zero, 1)
            pool.wait_ge(adj_zero, 1)
            pool.affine_select(out=adj3, in_=adj3, compare_op=ALU.not_equal, fill=1.0, base=0,
                               pattern=[[-TP, NT], [1, AW]], channel_multiplier=-1).then_inc(adj_zero, 1)
            pool.wait_ge(x_in, 48)
            pool.tensor_tensor(bias[:, 0, :], bias[:, 0, :], bias[:, 1, :], ALU.add).then_inc(bias_ready, 1)
            pool.wait_ge(bias_ready, 1)
            for i in range(NT):
                pool.tensor_tensor(x1[:, i, :], x1[:, i, :], bias[:, 0, :], ALU.add).then_inc(bias_ready, 1)

        @block.vector
        def _(dve):
            own = m["own"].on(dve)
            dve.sem_inc(added, 2)
            dve.wait_ge(table_in, 16)
            dve.wait_ge(consts, 1)
            dve.wait_ge(adj_zero, 2)
            with dve.Fori(0, NBATCH // 2) as step:
                n = 2 * step
                for v in range(2):
                    for u in range(U):
                        q = v * U + u
                        dve.wait_ge(hot_used, n * U + q + 1)
                        col = n * U + q
                        dve.tensor_scalar(hot_src[q][:], iota[:, 0:TP], table[:, bass.ds(col, 1), 0], None,
                                          ALU.is_equal)
                        dve.tensor_scalar(hot_dst[q][:], iota[:], table[:, bass.ds(col, 1), 1], None,
                                          ALU.is_equal).then_inc(hot_ready, 1)
                for v in range(2):
                    dve.wait_ge(hot_used, NHOT + (n + v + 1) * U)
                    dve.wait_ge(added, n + v + 2)
                    with dve.register(f"group{v}") as r:
                        dve.reg_load(r, m["batch_group"][0:1, bass.ds(n + v, 1)])
                        g = dve.snap(r, min_val=0, max_val=NG - 1)
                        at = adj[:, bass.ds(g * CH, CH)]
                        dve.tensor_tensor(at, at, banks[v][0:TP, 0:CH], ALU.add).then_inc(added, 1)
            dve.wait_ge(sd_ready, 1)
            own(dve.reciprocal(dis[:], dis[:]))
            refine_rsqrt(dve, own, dis[:], banks[6][0:TP, 0:NT], dis_work[:]).then_inc(dis_ready, 1)

            def a_low(i):
                dve.wait_ge(a_hi_ready, i + 1)
                dve.tensor_tensor(a_lo[i % 2][:], adj3[:, :, i * TP:(i + 1) * TP], f32(a_hi[i % 2][:]),
                                  ALU.subtract).then_inc(a_lo_ready, 1)

            dve.wait_ge(dis_ready, 1)
            for i in range(NT):
                dve.wait_ge(h_hi_ready, i + 1)
                dve.scalar_tensor_tensor(h_lo[:, i, :], h_in[i % 2][:], dis[:, i:i + 1], f32(h_hi[:, i, :]),
                                         ALU.mult, ALU.subtract).then_inc(h_lo_ready, 1)
                if i in (1, 3):
                    a_low(i // 2)
            for i in range(NT):
                for h in range(2):
                    n = 2 * i + h
                    dve.wait_ge(row_done, n + 1)
                    dve.wait_ge(bias_ready, i + 2)
                    at = x1[:, i, h * HC:(h + 1) * HC]
                    dve.scalar_tensor_tensor(at, banks[2 + n % 4][0:TP, 0:HC], dis[:, i:i + 1], at,
                                             ALU.mult, ALU.add).then_inc(row_read, 1)
                if i + 2 < NT:
                    a_low(i + 2)

        @block.scalar
        def _(act):
            def a_high(i):
                act.activation(a_hi[i % 2][:], adj3[:, :, i * TP:(i + 1) * TP], ACT.Copy).then_inc(a_hi_ready, 1)

            act.wait_ge(degree_ready, 1)
            act.activation(dis[:], banks[6][0:TP, 0:NT], ACT.Sqrt).then_inc(sd_ready, 1)
            a_high(0)
            a_high(1)
            act.wait_ge(dis_ready, 1)
            for i in range(NT):
                act.wait_ge(h_loaded[i % 2], 16 * (i // 2 + 1))
                act.activation(h_hi[:, i, :], h_in[i % 2][:], ACT.Copy,
                               scale=dis[:, i:i + 1]).then_inc(h_hi_ready, 1)
            for i in range(2, NT):
                act.wait_ge(row_read, 2 * (i - 1))
                a_high(i)

        @block.tensor
        def _(pe):
            pe.sem_inc(hot_used, NHOT)
            with pe.Fori(0, NBATCH // 2) as step:
                n = 2 * step
                for v in range(2):
                    pe.wait_ge(added, n + v + 1)
                    for u in range(U):
                        q = v * U + u
                        pe.wait_ge(hot_ready, n * U + q + 1)
                        last = pe.matmul(banks[v][0:TP, 0:CH], hot_src[q][:], hot_dst[q][:],
                                         start=(u == 0), stop=(u == U - 1))
                        last.then_inc(hot_used, 1)
            pe.wait_ge(added, NBATCH + 2)
            for i in range(NT):
                for s in range(NT):
                    last = pe.matmul(banks[6][0:TP, i:i + 1], adj3[:, s, i * TP:(i + 1) * TP],
                                     m["ones"][0:TP, 0:1], start=(s == 0), stop=(s == NT - 1))
            last.then_inc(degree_ready, 1)
            for i in range(NT):
                pe.wait_ge(a_lo_ready, i + 1)
                for h in range(2):
                    n = 2 * i + h
                    if n >= 4:
                        pe.wait_ge(row_read, n - 3)
                    for s in range(NT):
                        if i == 0 and h == 0:
                            pe.wait_ge(h_lo_ready, s + 1)
                        last = three_products(pe, banks[2 + n % 4][0:TP, 0:HC], a_hi[i % 2][:, s, :],
                                              a_lo[i % 2][:, s, :], h_hi[:, s, h * HC:(h + 1) * HC],
                                              h_lo[:, s, h * HC:(h + 1) * HC], s, NT)
                    last.then_inc(row_done, 1)


def keys(nc, m):
    a, sem, banks, keep = m["a"], m["sem"], m["banks"], m["keep"]
    GR = NT
    with ExitStack() as ctx:
        proj_in = keep("proj_in", [P, M], F32, ctx)
        k_in = keep("k_in", [P, T], F32, ctx)
        k_hi = keep("k_hi", [P, T], F32R, ctx)
        k_lo = keep("k_lo", [P, T], F32R, ctx)
        k_sq = keep("k_sq", [P, T], F32, ctx)
        v_in = [keep(f"v_in{i}", [TP, NT, 2, DV], F32, ctx) for i in range(2)]
        e_f = [keep(f"e_f{i}", [TP, 2, M], F32, ctx) for i in range(4)]
        e_hi = [keep(f"e_hi{i}", [TP, NT, 2, M], F32R, ctx) for i in range(2)]
        e_lo = [keep(f"e_lo{i}", [TP, NT, 2, M], F32R, ctx) for i in range(2)]
        neg_max = [keep(f"neg_max{i}", [TP, 2, NT], F32, ctx) for i in range(2)]
        shift = [keep(f"shift{i}", [TP, 2, NT], F32, ctx) for i in range(2)]
        weight = [keep(f"weight{i}", [TP, 2, NT], F32, ctx) for i in range(2)]
        top = [keep(f"top{i}", [P, 2], F32, ctx) for i in range(2)]
        head_top = [keep(f"head_top{i}", [P, 2], F32, ctx) for i in range(2)]
        neg_top = [keep(f"neg_top{i}", [P, 2], F32, ctx) for i in range(2)]
        tops = keep("tops", [P, H], F32, ctx)
        v_w = keep("v_w", [TP, NT, 2, DV], F32, ctx)
        v_hi = keep("v_hi", [TP, NT, 2, DV], F32R, ctx)
        v_lo = keep("v_lo", [TP, NT, 2, DV], F32R, ctx)
        sums = keep("sums", [P, H, 2, DV], F32, ctx)
        v_sum = keep("v_sum", [P, H, DV], F32, ctx)
        all_top = keep("all_top", [P, 1], F32, ctx)
        factor = keep("factor", [P, H], F32, ctx)

        p_loaded, k_loaded, v_loaded = sem("p_loaded"), sem("k_loaded"), [sem("v_loaded0"), sem("v_loaded1")]
        setup, p_scaled, p_hi_ready, p_ready = sem("k_setup"), sem("p_scaled"), sem("p_hi"), sem("p_ready")
        k_hi_r, k_lo_r, k_sq_r, diag_done = sem("k_hi"), sem("k_lo"), sem("k_sq"), sem("k_diag")
        product, maxed, exped = sem("k_product"), sem("k_maxed"), sem("k_exped")
        e_hi_r, e_lo_r, top_r, shifted = sem("e_hi"), sem("e_lo"), sem("k_top"), sem("k_shifted")
        all_red, neg_r, weight_r = sem("k_reduced"), sem("k_neg_top"), sem("k_weight")
        v_w_r, v_hi_r, v_lo_r = sem("v_weighed"), sem("v_hi"), sem("v_lo")
        summed, sums_read, fin = sem("k_summed"), sem("k_sums_read"), sem("k_final")
        fin_act = sem("k_final_act")
        block = ctx.enter_context(nc.Block())

        def pipeline(eng, front, back):
            front(0, 0)
            with eng.Fori(0, HP // 2 - 1) as turn:
                front(2 * turn + 1, 1)
                back(2 * turn, 0, turn)
                front(2 * turn + 2, 0)
                back(2 * turn + 1, 1, turn)
            front(HP - 1, 1)
            back(HP - 2, 0, HP // 2 - 1)
            back(HP - 1, 1, HP // 2 - 1)

        def group(v, g):
            return 2 * (g // 2), g % 2, (v * GR + g) % 4

        @block.sync
        def _(sp):
            for h in range(2):
                sp.dma_start(proj_in[h * D:(h + 1) * D, :], a["proj_t"]).then_inc(p_loaded, 16)
            sp.wait_ge(setup, 2)
            for hp in range(HP):
                if hp:
                    sp.wait_ge(k_lo_r, hp)
                    sp.wait_ge(k_sq_r, hp)
                sp.dma_start(k_in[:], m["qk"][1, hp * P:(hp + 1) * P, :]).then_inc(k_loaded, 16)
                if hp >= 2:
                    sp.wait_ge(summed, 2 + hp - 1)
                for j in range(2):
                    h = 2 * hp + j
                    sp.dma_start(v_in[hp % 2][:, :, j, 0:D],
                                 m["hv"][1, :, h * D:(h + 1) * D].rearrange("(i p) d -> p i d", p=TP)
                                 ).then_inc(v_loaded[hp % 2], 16)

        @block.gpsimd
        def _(pool):
            pool.memset(v_in[0][:], 1.0).then_inc(setup, 1)
            pool.memset(v_in[1][:], 1.0).then_inc(setup, 1)
            for t in top:
                pool.memset(t[:], -3e38).then_inc(setup, 1)
            pool.memset(m["head_mask"][:], 0.0).then_inc(setup, 1)
            pool.wait_ge(setup, 5)
            for j in range(2):
                pool.memset(m["head_mask"][j * D:(j + 1) * D, j:j + 1], DIAG).then_inc(setup, 1)
            pool.wait_ge(setup, 7)

            def front(hp, v):
                pool.wait_ge(k_loaded, 16 * (hp + 1))
                pool.wait_ge(diag_done, hp + 1)
                pool.tensor_tensor(k_sq[:], k_in[:], k_in[:], ALU.mult).then_inc(k_sq_r, 1)
                pool.wait_ge(summed, hp + 1)
                for g in range(GR):
                    i, j, r = group(v, g)
                    wait_alone(pool, exped, 4 + hp * GR + g + 1, m["passed"])
                    pool.tensor_copy(e_hi[v][:, i:i + 2, j, :], e_f[r][:]).then_inc(e_hi_r, 1)
                wait_alone(pool, top_r, hp + 1, m["passed"])
                pool.partition_all_reduce(head_top[v][:], top[v][:], P, bass.bass_isa.ReduceOp.max
                                          ).then_inc(all_red, 1)
                wait_alone(pool, all_red, hp + 1, m["passed"])
                pool.tensor_copy(tops[:, bass.ds(2 * hp, 2)], head_top[v][:])
                pool.tensor_scalar(neg_top[v][:], head_top[v][:], -1.0, None, ALU.mult).then_inc(neg_r, 1)

            def back(hp, v, turn):
                pool.wait_ge(weight_r, 2 * hp + 2)
                pool.wait_ge(v_loaded[v], 32 * (turn + 1))
                pool.wait_ge(v_lo_r, hp + 1)
                pool.tensor_tensor(v_w[:], v_in[v][:],
                                   weight[v][:].rearrange("p j i -> p i j").unsqueeze(3)
                                   .broadcast_to([TP, NT, 2, DV]), ALU.mult).then_inc(v_w_r, 1)

            pipeline(pool, front, back)

        @block.scalar
        def _(act):
            act.wait_ge(p_scaled, 1)
            act.activation(m["proj_hi"][:], proj_in[:], ACT.Copy).then_inc(p_hi_ready, 1)
            act.sem_inc(exped, 4)
            act.sem_inc(sums_read, 1)

            def front(hp, v):
                act.wait_ge(k_loaded, 16 * (hp + 1))
                act.activation(k_hi[:], k_in[:], ACT.Copy).then_inc(k_hi_r, 1)
                for g in range(GR):
                    i, j, r = group(v, g)
                    act.wait_ge(maxed, hp * GR + g + 1)
                    act.wait_ge(e_lo_r, hp * GR + g + 1)
                    for u in range(2):
                        last = act.activation(e_f[r][:, u, :], banks[r][0:TP, u * M:(u + 1) * M], ACT.Exp,
                                              bias=neg_max[v][:, j, i + u:i + u + 1])
                    last.then_inc(exped, 1)

            def back(hp, v, turn):
                act.wait_ge(neg_r, hp + 1)
                act.wait_ge(shifted, 2 + hp + 1)
                for j in range(2):
                    act.activation(weight[v][:, j, :], shift[v][:, j, :], ACT.Exp, scale=-1.0,
                                   bias=neg_top[v][0:TP, j:j + 1]).then_inc(weight_r, 1)
                act.wait_ge(v_w_r, hp + 1)
                act.wait_ge(summed, 2 + hp)
                act.activation(v_hi[:], v_w[:], ACT.Copy).then_inc(v_hi_r, 1)
                act.wait_ge(summed, 2 + hp + 1)
                act.activation(sums[:, bass.ds(2 * hp, 2), :, :].rearrange("p h b d -> p (h b d)"),
                               banks[7][:, 0:4 * DV], ACT.Copy)
                act.activation(v_sum[:, bass.ds(2 * hp, 2), :].rearrange("p h d -> p (h d)"),
                               banks[6][:, 0:2 * DV], ACT.Copy).then_inc(sums_read, 1)

            pipeline(act, front, back)
            act.wait_ge(fin, 1)
            act.activation(factor[:], tops[:], ACT.Exp, bias=all_top[:]).then_inc(fin_act, 1)
            act.wait_ge(fin, 4)
            act.activation(m["ctx_hi"][:], sums[:], ACT.Copy).then_inc(fin_act, 1)

        @block.vector
        def _(dve):
            dve.wait_ge(p_loaded, 32)
            dve.tensor_scalar(proj_in[:], proj_in[:], NORM, None, ALU.mult).then_inc(p_scaled, 1)
            dve.wait_ge(p_hi_ready, 1)
            dve.tensor_tensor(m["proj_lo"][:], proj_in[:], f32(m["proj_hi"][:]), ALU.subtract).then_inc(p_ready, 1)
            dve.sem_inc(e_lo_r, 4)
            dve.sem_inc(v_lo_r, 1)
            dve.sem_inc(shifted, 2)
            dve.wait_ge(setup, 7)

            def front(hp, v):
                dve.wait_ge(k_hi_r, hp + 1)
                dve.tensor_tensor(k_lo[:], k_in[:], f32(k_hi[:]), ALU.subtract).then_inc(k_lo_r, 1)
                for g in range(GR + 2):
                    if g < GR:
                        i, j, r = group(v, g)
                        dve.wait_ge(product, hp * GR + g + 1)
                        dve.tensor_reduce(neg_max[v][:, j, i:i + 2],
                                          banks[r][0:TP, :].rearrange("p (u f) -> p u f", u=2), X, ALU.max,
                                          negate=True).then_inc(maxed, 1)
                    if g >= 2:
                        i, j, r = group(v, g - 2)
                        dve.wait_ge(e_hi_r, hp * GR + g - 1)
                        dve.tensor_tensor(e_lo[v][:, i:i + 2, j, :], e_f[r][:], f32(e_hi[v][:, i:i + 2, j, :]),
                                          ALU.subtract).then_inc(e_lo_r, 1)
                dve.wait_ge(maxed, (hp + 1) * GR)
                dve.tensor_reduce(top[v][0:TP, :], neg_max[v][:], X, ALU.min, negate=True).then_inc(top_r, 1)
                dve.wait_ge(diag_done, hp + 2)
                dve.tensor_tensor(shift[v][:], neg_max[v][:],
                                  banks[4 + v][0:TP, 0:2 * NT].rearrange("p (i j) -> p j i", j=2),
                                  ALU.add).then_inc(shifted, 1)

            def back(hp, v, turn):
                dve.wait_ge(v_hi_r, hp + 1)
                dve.tensor_tensor(v_lo[:], v_w[:], f32(v_hi[:]), ALU.subtract).then_inc(v_lo_r, 1)

            pipeline(dve, front, back)
            dve.wait_ge(neg_r, HP)
            dve.tensor_reduce(all_top[:], tops[:], X, ALU.max, negate=True).then_inc(fin, 1)
            dve.wait_ge(fin_act, 1)
            dve.wait_ge(sums_read, HP + 1)
            both = sums[:].rearrange("p h b d -> p h (b d)")
            dve.tensor_tensor(both, both, factor[:].unsqueeze(2).broadcast_to([P, H, 2 * DV]),
                              ALU.mult).then_inc(fin, 1)
            dve.wait_ge(fin, 2)
            for b in range(2):
                dve.scalar_tensor_tensor(sums[:, :, b, :], v_sum[:], FEPS, sums[:, :, b, :],
                                         ALU.mult, ALU.add).then_inc(fin, 1)
            dve.wait_ge(fin_act, 2)
            dve.tensor_tensor(m["ctx_lo"][:], sums[:], f32(m["ctx_hi"][:]), ALU.subtract)

        @block.tensor
        def _(pe):
            pe.sem_inc(diag_done, 1)
            pe.sem_inc(summed, 2)
            pe.wait_ge(p_ready, 1)
            pe.wait_ge(setup, 7)

            def front(hp, v):
                pe.wait_ge(k_sq_r, hp + 1)
                pe.wait_ge(shifted, hp + 1)
                for i in range(NT):
                    last = pe.matmul(banks[4 + v][0:TP, 2 * i:2 * i + 2], k_sq[:, i * TP:(i + 1) * TP],
                                     m["head_mask"][:], start=True, stop=True)
                last.then_inc(diag_done, 1)
                pe.wait_ge(k_lo_r, hp + 1)
                for g in range(GR):
                    i, j, r = group(v, g)
                    pe.wait_ge(exped, hp * GR + g + 1)
                    features(pe, m, banks[r], k_hi, k_lo, i, j).then_inc(product, 1)

            def back(hp, v, turn):
                pe.wait_ge(sums_read, hp + 1)
                pe.wait_ge(v_loaded[v], 32 * (turn + 1))
                for i in range(NT):
                    pe.matmul(banks[6][:, 0:2 * DV], m["ones"][0:TP, :], v_in[v][:, i, :, :],
                              start=(i == 0), stop=(i == NT - 1))
                pe.wait_ge(v_lo_r, 1 + hp + 1)
                pe.wait_ge(e_lo_r, 4 + (hp + 1) * GR)
                for j in range(2):
                    for b in range(2):
                        for i in range(NT):
                            at = (slice(None), i, j, slice(b * P, (b + 1) * P))
                            last = three_products(pe, banks[7][:, (2 * j + b) * DV:(2 * j + b + 1) * DV],
                                                  e_hi[v][at], e_lo[v][at], v_hi[:, i, j, :], v_lo[:, i, j, :],
                                                  i, NT)
                last.then_inc(summed, 1)

            pipeline(pe, front, back)


def features(pe, m, bank, x_hi, x_lo, i, j):
    for u in range(2):
        rows, cols = slice(j * D, (j + 1) * D), slice((i + u) * TP, (i + u + 1) * TP)
        last = three_products(pe, bank[0:TP, u * M:(u + 1) * M], x_hi[rows, cols], x_lo[rows, cols],
                              m["proj_hi"][rows, :], m["proj_lo"][rows, :], 0, 1)
    return last


def queries(nc, m):
    sem, banks, keep = m["sem"], m["banks"], m["keep"]
    GR = NT
    STEP = 2 * GR
    T_LAG, O_LAG, A_LAG = 2, 4, 6
    with ExitStack() as ctx:
        q_in = [keep(f"q_in{i}", [P, T], F32, ctx) for i in range(2)]
        q_hi = [keep(f"q_hi{i}", [P, T], F32R, ctx) for i in range(2)]
        q_lo = [keep(f"q_lo{i}", [P, T], F32R, ctx) for i in range(2)]
        q_sq = [keep(f"q_sq{i}", [P, T], F32, ctx) for i in range(2)]
        diag = keep("diag", [TP, 2, NT, 2], F32, ctx)
        neg = keep("neg", [TP, 2, 2], F32, ctx)
        shift = keep("q_shift", [TP, 2, 2], F32, ctx)
        e_f = [keep(f"q_e{i}", [TP, 2, M], F32, ctx) for i in range(2)]
        f_hi = [keep(f"f_hi{i}", [P, 2, 2, TP], F32R, ctx) for i in range(2)]
        f_lo = [keep(f"f_lo{i}", [P, 2, 2, TP], F32R, ctx) for i in range(2)]
        inverse = keep("inverse", [TP, 2, 2], F32, ctx)
        o_f = [keep(f"o_f{i}", [TP, 2, P], F32, ctx) for i in range(2)]

        q_loaded = [sem("q_loaded0"), sem("q_loaded1")]
        q_hi_r, q_lo_r, q_sq_r = sem("q_hi"), sem("q_lo"), sem("q_sq")
        diag_done, diag_read, product = sem("q_diag"), sem("q_diag_read"), sem("q_product")
        maxed, shifted, exped, turned = sem("q_maxed"), sem("q_shifted"), sem("q_exped"), sem("q_turned")
        f_hi_r, f_lo_r, o_done, inverted, o_read = (sem("f_hi"), sem("f_lo"), sem("o_done"), sem("inverted"),
                                                    sem("o_read"))
        a_turned, a_hi_r, a_lo_r = sem("a_turned"), sem("att_hi_r"), sem("att_lo_r")
        block = ctx.enter_context(nc.Block())

        def group(s):
            return s // GR, 2 * (s % GR // 2), s % 2

        @block.sync
        def _(sp):
            for hp in range(HP):
                if hp >= 2:
                    sp.wait_ge(q_lo_r, hp - 1)
                    sp.wait_ge(q_sq_r, hp - 1)
                sp.dma_start(q_in[hp % 2][:], m["qk"][0, hp * P:(hp + 1) * P, :]).then_inc(q_loaded[hp % 2], 16)

        @block.gpsimd
        def _(pool):
            with pool.Fori(0, HP // 2) as step:
                hp = 2 * step
                for v in range(2):
                    pool.wait_ge(q_loaded[v], 16 * (step + 1))
                    pool.wait_ge(diag_done, hp + 2)
                    pool.tensor_tensor(q_sq[v][:], q_in[v][:], q_in[v][:], ALU.mult).then_inc(q_sq_r, 1)

        @block.scalar
        def _(act):
            act.sem_inc(exped, 4)
            with act.Fori(0, HP // 2) as step:
                hp = 2 * step
                first = hp * GR
                for v in range(2):
                    act.wait_ge(q_loaded[v], 16 * (step + 1))
                    act.activation(q_hi[v][:], q_in[v][:], ACT.Copy).then_inc(q_hi_r, 1)
                for s in range(STEP + A_LAG):
                    if s < STEP:
                        v, i, j = group(s)
                        act.wait_ge(shifted, first + s + 1)
                        act.wait_ge(turned, first + s + 1)
                        for u in range(2):
                            last = act.activation(e_f[s % 2][:, u, :], banks[s % 4][0:TP, u * M:(u + 1) * M],
                                                  ACT.Exp, bias=shift[:, s % 2, u:u + 1])
                        last.then_inc(exped, 1)
                    if T_LAG <= s < STEP + T_LAG:
                        t = s - T_LAG
                        act.wait_ge(turned, 2 + first + t + 1)
                        act.wait_ge(o_done, first + t + 1)
                        act.activation(f_hi[t % 2][:], banks[4 + t % 2][:, 0:4 * TP].rearrange(
                            "p (u b t) -> p u b t", u=2, b=2), ACT.Copy, bias=FEPS).then_inc(f_hi_r, 1)
                    if s >= A_LAG and s % 2:
                        t = (s - A_LAG) // 2
                        v, i, _ = group(2 * t)
                        act.wait_ge(a_turned, 2 + step * GR + t + 1)
                        act.activation(m["att_hi"][:, bass.ds(hp + v, 1), i * TP:(i + 2) * TP],
                                       banks[7][:, 0:2 * TP].unsqueeze(1), ACT.Copy).then_inc(a_hi_r, 1)

        @block.vector
        def _(dve):
            dve.sem_inc(diag_read, 1)
            dve.sem_inc(f_lo_r, 2)
            dve.sem_inc(o_read, 1)
            dve.sem_inc(a_lo_r, 1)
            with dve.Fori(0, HP // 2) as step:
                hp = 2 * step
                first = hp * GR
                for v in range(2):
                    dve.wait_ge(q_hi_r, hp + v + 1)
                    dve.tensor_tensor(q_lo[v][:], q_in[v][:], f32(q_hi[v][:]), ALU.subtract).then_inc(q_lo_r, 1)
                dve.wait_ge(diag_done, 2 + hp + 2)
                dve.tensor_copy(diag[:].rearrange("p v i j -> p (v i j)"), banks[7][0:TP, 0:4 * NT]
                                ).then_inc(diag_read, 1)
                dve.wait_ge(diag_read, step + 2)
                for s in range(STEP + A_LAG):
                    if s < STEP:
                        v, i, j = group(s)
                        dve.wait_ge(product, first + s + 1)
                        dve.tensor_reduce(neg[:, s % 2, :], banks[s % 4][0:TP, :].rearrange(
                            "p (u f) -> p u f", u=2), X, ALU.max, negate=True).then_inc(maxed, 1)
                        dve.wait_ge(maxed, first + s + 1)
                        dve.wait_ge(exped, 2 + first + s + 1)
                        dve.tensor_tensor(shift[:, s % 2, :], neg[:, s % 2, :], diag[:, v, i:i + 2, j],
                                          ALU.subtract).then_inc(shifted, 1)
                    if T_LAG <= s < STEP + T_LAG:
                        t = s - T_LAG
                        dve.wait_ge(f_hi_r, first + t + 1)
                        dve.scalar_tensor_tensor(
                            f_lo[t % 2][:].rearrange("p u b t -> p (u b t)"), banks[4 + t % 2][:, 0:4 * TP], FEPS,
                            f32(f_hi[t % 2][:].rearrange("p u b t -> p (u b t)")), ALU.add,
                            ALU.subtract).then_inc(f_lo_r, 1)
                    if O_LAG <= s < STEP + O_LAG:
                        t = s - O_LAG
                        v, i, j = group(t)
                        o = banks[6][0:TP, 0:2 * DV].rearrange("p (u d) -> p u d", u=2)
                        dve.wait_ge(o_done, 2 + first + t + 1)
                        dve.reciprocal(inverse[:, t % 2, :].unsqueeze(2), o[:, :, D:D + 1]).then_inc(inverted, 1)
                        dve.wait_ge(inverted, first + t + 1)
                        dve.wait_ge(a_turned, step * GR + t // 2 + 1)
                        dve.tensor_tensor(o_f[t // 2 % 2][:, :, j * D:(j + 1) * D], o[:, :, 0:D],
                                          inverse[:, t % 2, :].unsqueeze(2).broadcast_to([TP, 2, D]),
                                          ALU.mult).then_inc(o_read, 1)
                    if s >= A_LAG and s % 2:
                        t = (s - A_LAG) // 2
                        v, i, _ = group(2 * t)
                        at = (slice(None), bass.ds(hp + v, 1), slice(i * TP, (i + 2) * TP))
                        dve.wait_ge(a_hi_r, step * GR + t + 1)
                        dve.tensor_tensor(m["att_lo"][at], banks[7][:, 0:2 * TP].unsqueeze(1),
                                          f32(m["att_hi"][at]), ALU.subtract).then_inc(a_lo_r, 1)

        @block.tensor
        def _(pe):
            pe.sem_inc(diag_done, 2)
            pe.sem_inc(turned, 2)
            pe.sem_inc(o_done, 2)
            pe.sem_inc(a_turned, 2)
            with pe.Fori(0, HP // 2) as step:
                hp = 2 * step
                first = hp * GR
                pe.wait_ge(a_lo_r, step * GR + 1)
                for v in range(2):
                    pe.wait_ge(q_sq_r, hp + v + 1)
                    for i in range(NT):
                        c = 2 * (v * NT + i)
                        last = pe.matmul(banks[7][0:TP, c:c + 2], q_sq[v][:, i * TP:(i + 1) * TP],
                                         m["head_mask"][:], start=True, stop=True)
                    last.then_inc(diag_done, 1)
                for s in range(STEP + A_LAG):
                    if s < STEP:
                        v, i, j = group(s)
                        pe.wait_ge(q_lo_r, hp + v + 1)
                        pe.wait_ge(exped, first + s + 1)
                        features(pe, m, banks[s % 4], q_hi[v], q_lo[v], i, j).then_inc(product, 1)
                    if T_LAG <= s < STEP + T_LAG:
                        t = s - T_LAG
                        pe.wait_ge(exped, 4 + first + t + 1)
                        pe.wait_ge(f_lo_r, first + t + 1)
                        for u in range(2):
                            for b in range(2):
                                c = (2 * u + b) * TP
                                last = pe.transpose(banks[4 + t % 2][:, c:c + TP],
                                                    e_f[t % 2][:, u, b * P:(b + 1) * P], m["ident"][0:TP, 0:TP])
                        last.then_inc(turned, 1)
                    if O_LAG <= s < STEP + O_LAG:
                        t = s - O_LAG
                        v, i, j = group(t)
                        pe.wait_ge(f_lo_r, 2 + first + t + 1)
                        pe.wait_ge(o_read, first + t + 1)
                        head = bass.ds(2 * hp + 2 * v + j, 1)
                        for u in range(2):
                            for b in range(2):
                                last = three_products(
                                    pe, banks[6][0:TP, u * DV:(u + 1) * DV], f_hi[t % 2][:, u, b, :],
                                    f_lo[t % 2][:, u, b, :], m["ctx_hi"][:, head, b, :],
                                    m["ctx_lo"][:, head, b, :], b, 2)
                        last.then_inc(o_done, 1)
                    if s >= A_LAG and s % 2:
                        t = (s - A_LAG) // 2
                        pe.wait_ge(o_read, 1 + first + 2 * t + 2)
                        pe.wait_ge(a_lo_r, step * GR + t + 1)
                        for u in range(2):
                            last = pe.transpose(banks[7][:, u * TP:(u + 1) * TP], o_f[t % 2][:, u, :],
                                                m["ident"][0:TP, 0:TP])
                        last.then_inc(a_turned, 1)


def mix_and_route(nc, m):
    a, sem, banks, keep, x1 = m["a"], m["sem"], m["banks"], m["keep"], m["x1"]
    with ExitStack() as ctx:
        raw = [keep(f"mix_raw{i}", [P, KB, HC], F32, ctx) for i in range(1)] * 2
        w_hi = [keep(f"mix_hi{i}", [P, KB, HC], F32R, ctx) for i in range(2)]
        w_lo = [keep(f"mix_lo{i}", [P, KB, HC], F32R, ctx) for i in range(2)]
        stats = keep("stats2", [TP, NT, 2, 6], F32, ctx)
        mean_var = keep("mean_var2", [TP, NT, 2], F32, ctx)
        spread = keep("spread2", [TP, NT], F32, ctx)
        rstd = keep("rstd2", [TP, NT], F32, ctx)
        xn = [keep(f"xn{i}", [TP, C], F32, ctx) for i in range(2)]
        xn_t = [keep(f"xn_t{i}", [P, KB, TP], F32, ctx) for i in range(2)]
        gate = keep("gate", [P, KB, NE], F32, ctx)
        logits = keep("logits", [TP, NT, NE], F32, ctx)
        best = keep("best", [TP, NT], F32, ctx)
        total = keep("total", [TP, NT], F32, ctx)
        order = keep("order", [TP, NT, 8], F32, ctx)
        which = keep("which", [TP, NT, 8], U32, ctx)
        expert = keep("expert", [TP, NT, TOPK], F32, ctx)
        token_i = keep("token_i", [TP, NT, TOPK], I32, ctx)
        pair = keep("moe_pair", [TP, TJ, 2], F32, ctx)
        wide = keep("moe_wide", [TP, NE, TJ], F32, ctx)
        s = slot_buffers(m, ctx, "moe", NE, TJ, wide[:])
        s["sums"] = banks[7][0:TP, 0:2 * NE]
        unit_iota = keep("unit_iota", [1, NR], F32, ctx)
        unit_hot = keep("unit_hot", [1, NE, NR], F32, ctx)

        w_loaded, hi_r, lo_r, product = sem("m_w_loaded"), sem("m_w_hi"), sem("m_w_lo"), sem("m_product")
        added, var_r, sd_r = sem("m_added"), sem("m_var"), sem("m_sd")
        gate_loaded, xn_stored = sem("gate_loaded"), [sem("xn2_stored0"), sem("xn2_stored1")]
        xn_r, xt_done, xt_r, l_done = sem("xn2_ready"), sem("xt_done"), sem("xt_ready"), sem("logits_done")
        e_ready, e_done, consts = sem("m_exp_ready"), sem("m_exp_done"), sem("m_consts")
        totals_r, sums_r, rows_r, sent = sem("m_totals"), sem("m_sums"), sem("m_rows"), sem("m_sent")
        block = ctx.enter_context(nc.Block())

        @block.sync
        def _(sp):
            sp.dma_start(gate[:], a["gate_t"].rearrange("(k p) e -> p k e", p=P)).then_inc(gate_loaded, 16)
            for n in range(2):
                if n:
                    sp.wait_ge(lo_r, 1)
                sp.dma_start(raw[n][:], a["w_pieces"][8 + n].rearrange("p (k c) -> p k c", k=KB)
                             ).then_inc(w_loaded, 16)
            for i in range(NT):
                sp.wait_ge(xn_r, i + 1)
                sp.dma_start(m["xn2"][i * TP:(i + 1) * TP, :], xn[i % 2][:]).then_inc(xn_stored[i % 2], 16)
            for done in xn_stored:
                sp.wait_ge(done, 8 * NT)

        @block.tensor
        def _(pe):
            for h in range(2):
                pe.wait_ge(lo_r, h + 1)
                for i in range(NT):
                    n = h * NT + i
                    if n >= 4:
                        pe.wait_ge(added, n - 3)
                    for k in range(HP):
                        last = three_products(
                            pe, banks[n % 4][0:TP, 0:HC], m["att_hi"][:, k, i * TP:(i + 1) * TP],
                            m["att_lo"][:, k, i * TP:(i + 1) * TP], w_hi[h][:, k, :], w_lo[h][:, k, :], k, HP)
                    last.then_inc(product, 1)
            pe.wait_ge(added, 2 * NT)
            pe.wait_ge(gate_loaded, 16)
            for i in range(NT + 1):
                if i < NT:
                    pe.wait_ge(xn_r, i + 1)
                    if i >= 2:
                        pe.wait_ge(xt_r, i - 1)
                    for k in range(KB):
                        bank = banks[2 * (i % 2) + k // 3]
                        last = pe.transpose(bank[:, k % 3 * TP:(k % 3 + 1) * TP], xn[i % 2][:, k * P:(k + 1) * P],
                                            m["ident"][0:TP, 0:TP])
                    last.then_inc(xt_done, 1)
                if i:
                    pe.wait_ge(xt_r, i)
                    for k in range(KB):
                        last = pe.matmul(banks[6][0:TP, (i - 1) * NE:i * NE], xn_t[(i - 1) % 2][:, k, :],
                                         gate[:, k, :], start=(k == 0), stop=(k == KB - 1))
                    last.then_inc(l_done, 1)
            pe.wait_ge(totals_r, 1)
            pe.matmul(s["sums"][:, 0:NE], m["before"][0:TP, 0:TP], s["total"], start=True, stop=True)
            pe.matmul(s["sums"][:, NE:2 * NE], m["ones"][0:TP, 0:TP], s["total"], start=True,
                      stop=True).then_inc(sums_r, 1)

        @block.scalar
        def _(act):
            for n in range(2):
                act.wait_ge(w_loaded, 16 * (n + 1))
                act.activation(w_hi[n][:], raw[n][:], ACT.Copy).then_inc(hi_r, 1)
            act.wait_ge(var_r, 1)
            act.activation(rstd[:], spread[:], ACT.Sqrt).then_inc(sd_r, 1)
            for i in range(NT):
                act.wait_ge(xt_done, i + 1)
                if i >= 2:
                    act.wait_ge(l_done, i - 1)
                for h in range(2):
                    last = act.activation(xn_t[i % 2][:, 3 * h:3 * h + 3, :], banks[2 * (i % 2) + h][:, 0:3 * TP]
                                          .rearrange("p (b t) -> p b t", b=3), ACT.Copy)
                last.then_inc(xt_r, 1)
            act.wait_ge(e_ready, 1)
            act.activation(logits[:], logits[:], ACT.Exp).then_inc(e_done, 1)

        @block.vector
        def _(dve):
            own = m["own"].on(dve)
            for n in range(2):
                dve.wait_ge(hi_r, n + 1)
                dve.tensor_tensor(w_lo[n][:], raw[n][:], f32(w_hi[n][:]), ALU.subtract).then_inc(lo_r, 1)
            for h in range(2):
                for i in range(NT):
                    dve.wait_ge(product, h * NT + i + 1)
                    at = x1[:, i, h * HC:(h + 1) * HC]
                    dve.tensor_tensor(at, at, banks[(h * NT + i) % 4][0:TP, 0:HC], ALU.add).then_inc(added, 1)
            dve.wait_ge(added, 2 * NT)
            for i in range(NT):
                for h in range(2):
                    last = dve.bn_stats(stats[:, i, h, :], x1[:, i, h * HC:(h + 1) * HC])
            own(last)
            for i in range(NT):
                last = dve.bn_aggr(mean_var[:, i, :], stats[:, i, :, :])
            own(last)
            dve.tensor_scalar(spread[:], mean_var[:, :, 1], LN_EPS, None, ALU.add).then_inc(var_r, 1)
            dve.wait_ge(sd_r, 1)
            own(dve.reciprocal(rstd[:], rstd[:]))
            own(refine_rsqrt(dve, own, rstd[:], spread[:], best[:]))
            for i in range(NT):
                if i >= 2:
                    dve.wait_ge(xn_stored[i % 2], 16 * (i // 2))
                    dve.wait_ge(xt_done, i - 1)
                dve.tensor_scalar(xn[i % 2][:], x1[:, i, :], mean_var[:, i, 0:1], rstd[:, i:i + 1],
                                  ALU.subtract, ALU.mult).then_inc(xn_r, 1)
            dve.wait_ge(l_done, NT)
            own(dve.tensor_copy(logits[:].rearrange("p i e -> p (i e)"), banks[6][0:TP, 0:NT * NE]))
            own(dve.tensor_reduce(best[:], logits[:], X, ALU.max))
            own(dve.tensor_tensor(logits[:], logits[:], best[:].unsqueeze(2).broadcast_to([TP, NT, NE]),
                                  ALU.subtract))
            dve.sem_inc(e_ready, 1)
            dve.wait_ge(e_done, 1)
            own(dve.tensor_reduce(total[:], logits[:], X, ALU.add))
            own(dve.reciprocal(total[:], total[:]))
            own(dve.tensor_tensor(logits[:], logits[:], total[:].unsqueeze(2).broadcast_to([TP, NT, NE]),
                                  ALU.mult))
            for i in range(NT):
                last = dve.max(order[:, i, :], logits[:, i, :])
            own(last)
            for i in range(NT):
                last = dve.max_index(which[:, i, :], order[:, i, :], logits[:, i, :])
            own(last)
            own(dve.tensor_copy(expert[:], which[:, :, 0:TOPK]))
            own(dve.tensor_tensor(total[:], order[:, :, 0], order[:, :, 1], ALU.add))
            own(dve.tensor_scalar(total[:], total[:], 1e-8, None, ALU.add))
            own(dve.reciprocal(total[:], total[:]))
            dve.wait_ge(consts, 5)
            own(dve.tensor_tensor(pair[:, :, 1].rearrange("p (i k) -> p i k", k=TOPK), order[:, :, 0:TOPK],
                                  total[:].unsqueeze(2).broadcast_to([TP, NT, TOPK]), ALU.mult))
            find_slots(dve, own, totals_r, sums_r, s, expert[:].rearrange("p i k -> p (i k)"), NE, TJ, UT)
            own(table_rows(dve, own, s, RCOLS))
            own(dve.tensor_copy(m["slot_of"][:], s["slot_i"]))
            dve.sem_inc(rows_r, 1)
            own(dve.tensor_tensor(unit_hot[:], unit_iota[:].unsqueeze(1).broadcast_to([1, NE, NR]),
                                  s["upto"][0:1, :].unsqueeze(2).broadcast_to([1, NE, NR]), ALU.is_ge))
            own(dve.tensor_reduce(unit_iota[:], unit_hot[:].rearrange("p g j -> p j g"), X, ALU.add))
            own(dve.tensor_scalar(m["unit_expert"][:, 0:NR], unit_iota[:], float(NE - 1), None, ALU.min))

        @block.gpsimd
        def _(pool):
            pool.iota(s["iota"], [[1, NE]], base=0, channel_multiplier=0,
                      allow_small_or_imprecise_dtypes=True).then_inc(consts, 1)
            pool.iota(unit_iota[:], [[1, NR]], base=0, channel_multiplier=0,
                      allow_small_or_imprecise_dtypes=True).then_inc(consts, 1)
            pool.memset(s["keep_on"], 1.0).then_inc(consts, 1)
            pool.wait_ge(consts, 3)
            pool.memset(s["keep_on"][:, :, 0:1], 0.0).then_inc(consts, 1)
            pool.iota(pair[:, :, 0].bitcast(I32).rearrange("p (i k) -> p i k", k=TOPK), [[TP, NT], [0, TOPK]],
                      base=0, channel_multiplier=1).then_inc(consts, 1)
            for e in range(NS):
                at = m["slot_table"][:, RCOLS + e * SU * UT // P:RCOLS + (e + 1) * SU * UT // P, :]
                pool.iota(at[:, :, 0].bitcast(I32), [[P, SU * UT // P]], base=0,
                          channel_multiplier=1).then_inc(consts, 1)
                pool.memset(at[:, :, 1], 1.0 / NS).then_inc(consts, 1)
                pool.memset(m["unit_expert"][:, NR + e * SU:NR + (e + 1) * SU], NE + e).then_inc(consts, 1)
            pool.wait_ge(consts, 5 + 3 * NS)
            shared = m["slot_table"][:, RCOLS:UCOLS, 0].bitcast(I32)
            pool.tensor_scalar(shared, shared, float(T - 1), None, ALU.min).then_inc(consts, 1)
            pool.wait_ge(rows_r, 1)
            for u in range(TJ):
                pool.indirect_dma_start(m["slots"], bass.IndirectOffsetOnAxis(ap=s["row"][:, u:u + 1], axis=0),
                                        pair[:, u, :], None).then_inc(sent, 16)
            pool.wait_ge(sent, 16 * TJ)


def experts(nc, m):
    a, sem, banks, keep = m["a"], m["sem"], m["banks"], m["keep"]
    UB = UT // P
    with ExitStack() as ctx:
        raw = {w: keep(f"raw_{w}", [P, KB * HC], F32, ctx) for w in "gud"}
        w_hi = {w: keep(f"hi_{w}", [P, KB * HC], F32R, ctx) for w in "gud"}
        w_lo = {w: keep(f"lo_{w}", [P, KB * HC], F32R, ctx) for w in "gud"}
        x_in = keep("unit_x", [P, UB, C], F32, ctx)
        x_hi = keep("unit_hi", [P, KB, UT], F32R, ctx)
        x_lo = keep("unit_lo", [P, KB, UT], F32R, ctx)
        act_f = keep("act_f", [P, IB, UT], F32, ctx)
        h_f = keep("h_f", [P, IB, UT], F32, ctx)
        h_hi = keep("unit_h_hi", [P, IB, UT], F32R, ctx)
        h_lo = keep("unit_h_lo", [P, IB, UT], F32R, ctx)
        y_f = [keep(f"y_f{i}", [P, C], F32, ctx) for i in range(UB)]
        tokens = keep("tokens", [P, UB], I32, ctx)
        loaded = {w: sem(f"u_loaded_{w}") for w in "gud"}
        hi_r = {w: sem(f"u_hi_{w}") for w in "gud"}
        lo_r = {w: sem(f"u_lo_{w}") for w in "gud"}
        table_in, picked, gathered = sem("u_table"), sem("u_picked"), sem("u_gathered")
        x_turned, x_hi_r, x_lo_r = sem("u_turned"), sem("u_x_hi"), sem("u_x_lo")
        g_done, u_done, silu_r, h_r, h_hi_r, h_lo_r = (sem("u_gate"), sem("u_up"), sem("u_silu"), sem("u_h"),
                                                       sem("u_h_hi"), sem("u_h_lo"))
        d_done, y_r, y_stored, y_free = sem("u_down"), sem("u_y"), sem("u_y_stored"), sem("u_y_free")
        ND = 2 * UB
        G, U, TB, DB = banks[0:2], banks[2:4], banks[4:6], banks[6:8]
        block = ctx.enter_context(nc.Block())

        @block.sync
        def _(sp):
            for w in "gud":
                sp.sem_inc(lo_r[w], 1)
            which = ctx.enter_context(sp.register("expert"))

            def load(n, ws):
                sp.reg_load(which, m["unit_expert"][0:1, bass.ds(n, 1)])
                e = sp.snap(which, min_val=0, max_val=NE + NS - 1)
                for w in ws:
                    sp.wait_ge(lo_r[w], n + 1)
                    sp.dma_start(raw[w][:], a["experts"]["gud".index(w), bass.ds(e, 1), :, :].rearrange(
                        "a p c -> (a p) c")).then_inc(loaded[w], 16)

            load(0, "gu")
            with sp.Fori(0, NU - 1) as n:
                load(n + 1, "gu")
                load(n, "d")
            load(NU - 1, "d")

        @block.gpsimd
        def _(pool):
            pool.dma_start(m["slot_table"][:, 0:RCOLS, :].rearrange("p c k -> p (c k)"),
                           m["slots"].rearrange("(p c) k -> p (c k)", p=P)).then_inc(table_in, 16)
            pool.sem_inc(y_free, 1)
            pool.wait_ge(table_in, 16)

            def gather(n, first=False):
                if not first:
                    wait_alone(pool, x_turned, IB * n, m["passed"])
                pool.tensor_copy(tokens[:], m["slot_table"][:, bass.ds(n * UB, UB), 0].bitcast(I32)
                                 ).then_inc(picked, 1)
                wait_alone(pool, picked, n + 1, m["passed"])
                for u in range(UB):
                    pool.indirect_dma_start(x_in[:, u, :], None, m["xn2"],
                                            bass.IndirectOffsetOnAxis(ap=tokens[:, u:u + 1], axis=0)
                                            ).then_inc(gathered, 16)

            def low_down(n):
                pool.wait_ge(hi_r["d"], n + 1)
                pool.tensor_tensor(w_lo["d"][:], raw["d"][:], f32(w_hi["d"][:]), ALU.subtract
                                   ).then_inc(lo_r["d"], 1)

            def allow(n):
                pool.wait_ge(y_stored, 16 * UB * n)
                pool.sem_inc(y_free, 1)

            def store(n):
                for u in range(UB):
                    pool.wait_ge(y_r, 2 + ND * n + 2 * u + 2)
                    pool.dma_start(m["y"][bass.ds(n * UT + u * P, P), :], y_f[u][:]).then_inc(y_stored, 16)

            gather(0, first=True)
            gather(1)
            low_down(0)
            gather(2)
            low_down(1)
            store(0)
            with pool.Fori(2, NU - 1) as n:
                gather(n + 1)
                allow(n - 1)
                low_down(n)
                store(n - 1)
            allow(NU - 2)
            low_down(NU - 1)
            store(NU - 2)
            allow(NU - 1)
            store(NU - 1)
            pool.wait_ge(y_stored, 16 * UB * NU)

        @block.tensor
        def _(pe):
            pe.sem_inc(d_done, 1)

            def turn(n):
                pe.wait_ge(gathered, 16 * UB * (n + 1))
                for q in range(IB):
                    pe.wait_ge(x_lo_r, IB * n + (2 if q == 2 else 1))
                    for b in range(2):
                        for u in range(UB):
                            c = b * UT + u * P
                            last = pe.transpose(TB[q % 2][:, c:c + P],
                                                x_in[:, u, (2 * q + b) * P:(2 * q + b + 1) * P], m["ident"][:])
                    last.then_inc(x_turned, 1)

            def into(n, w, bank, done, read):
                pe.wait_ge(lo_r[w], 1 + n + 1)
                pe.wait_ge(read, 2 * n + 1)
                for i in range(IB):
                    for k in range(KB):
                        c = k * HC + i * P
                        last = three_products(pe, bank[i // 2][:, i % 2 * UT:(i % 2 + 1) * UT],
                                              w_hi[w][:, c:c + P], w_lo[w][:, c:c + P],
                                              x_hi[:, k, :], x_lo[:, k, :], k, KB)
                    if i:
                        last.then_inc(done, 1)

            def down(n):
                pe.wait_ge(lo_r["d"], 1 + n + 1)
                pe.wait_ge(h_lo_r, n + 1)
                for q in range(ND):
                    u, h = q // 2, q % 2
                    pe.wait_ge(y_r, ND * n + q + 1)
                    for i in range(IB):
                        c = i * C + h * HC
                        last = three_products(pe, DB[q % 2][:, 0:HC], h_hi[:, i, u * P:(u + 1) * P],
                                              h_lo[:, i, u * P:(u + 1) * P], w_hi["d"][:, c:c + HC],
                                              w_lo["d"][:, c:c + HC], i, IB)
                    last.then_inc(d_done, 1)

            def gate_up(n):
                pe.wait_ge(x_lo_r, 1 + IB * (n + 1))
                into(n, "g", G, g_done, silu_r)
                into(n, "u", U, u_done, h_r)

            turn(0)
            gate_up(0)
            turn(1)
            with pe.Fori(1, NU - 1) as n:
                gate_up(n)
                turn(n + 1)
                down(n - 1)
            gate_up(NU - 1)
            down(NU - 2)
            down(NU - 1)

        @block.scalar
        def _(act):
            act.sem_inc(silu_r, 1)

            def high(w, n, used=None):
                act.wait_ge(loaded[w], 16 * (n + 1))
                if used is not None:
                    act.wait_ge(*used)
                act.activation(w_hi[w][:], raw[w][:], ACT.Copy).then_inc(hi_r[w], 1)

            def x_high(n):
                for q in range(IB):
                    act.wait_ge(x_turned, IB * n + q + 1)
                    act.activation(x_hi[:, 2 * q:2 * q + 2, :], TB[q % 2][:].rearrange("p (b t) -> p b t", b=2),
                                   ACT.Copy).then_inc(x_hi_r, 1)

            def silu(n):
                act.wait_ge(h_r, 2 * n + 1)
                act.wait_ge(g_done, 2 * n + 1)
                act.activation(act_f[:, 0:2, :].rearrange("p i t -> p (i t)"), G[0][:], ACT.Silu
                               ).then_inc(silu_r, 1)
                act.wait_ge(g_done, 2 * n + 2)
                act.activation(act_f[:, 2, :], G[1][:, 0:UT], ACT.Silu).then_inc(silu_r, 1)

            def h_high(n):
                act.wait_ge(d_done, ND * n + 1)
                act.wait_ge(h_r, 1 + 2 * n + 2)
                act.activation(h_hi[:], h_f[:], ACT.Copy).then_inc(h_hi_r, 1)
                high("d", n)

            high("g", 0)
            high("u", 0)
            x_high(0)
            with act.Fori(0, NU - 1) as n:
                silu(n)
                high("g", n + 1, (g_done, 2 * n + 2))
                act.wait_ge(u_done, 2 * n + 2)
                x_high(n + 1)
                high("u", n + 1)
                h_high(n)
            silu(NU - 1)
            h_high(NU - 1)

        @block.vector
        def _(dve):
            dve.sem_inc(x_lo_r, 1)
            dve.sem_inc(h_r, 1)
            dve.sem_inc(y_r, 2)

            def low(w, n):
                dve.wait_ge(hi_r[w], n + 1)
                dve.tensor_tensor(w_lo[w][:], raw[w][:], f32(w_hi[w][:]), ALU.subtract).then_inc(lo_r[w], 1)

            def x_low(n):
                for q in range(IB):
                    dve.wait_ge(x_hi_r, IB * n + q + 1)
                    dve.tensor_tensor(x_lo[:, 2 * q:2 * q + 2, :], TB[q % 2][:].rearrange(
                        "p (b t) -> p b t", b=2), f32(x_hi[:, 2 * q:2 * q + 2, :]), ALU.subtract
                        ).then_inc(x_lo_r, 1)

            def hidden(n):
                dve.wait_ge(silu_r, 1 + 2 * n + 2)
                dve.wait_ge(u_done, 2 * n + 1)
                if not isinstance(n, int) or n:
                    dve.wait_ge(h_lo_r, n)
                dve.tensor_tensor(h_f[:, 0:2, :].rearrange("p i t -> p (i t)"), act_f[:, 0:2, :].rearrange(
                    "p i t -> p (i t)"), U[0][:], ALU.mult).then_inc(h_r, 1)
                dve.wait_ge(u_done, 2 * n + 2)
                dve.tensor_tensor(h_f[:, 2, :], act_f[:, 2, :], U[1][:, 0:UT], ALU.mult).then_inc(h_r, 1)

            def h_low(n):
                dve.wait_ge(h_hi_r, n + 1)
                dve.tensor_tensor(h_lo[:], h_f[:], f32(h_hi[:]), ALU.subtract).then_inc(h_lo_r, 1)

            def y_rows(n, qs):
                for q in qs:
                    u, h = q // 2, q % 2
                    if q == 0:
                        dve.wait_ge(y_free, n + 1)
                    dve.wait_ge(d_done, 1 + ND * n + q + 1)
                    dve.tensor_scalar(y_f[u][:, h * HC:(h + 1) * HC], DB[q % 2][:, 0:HC],
                                      m["slot_table"][:, bass.ds(n * UB + u, 1), 1], None, ALU.mult
                                      ).then_inc(y_r, 1)

            def body(n, behind):
                low("g", n + 1)
                hidden(n)
                x_low(n + 1)
                if behind:
                    y_rows(n - 1, [0])
                low("u", n + 1)
                if behind:
                    y_rows(n - 1, range(1, ND))
                h_low(n)

            low("g", 0)
            low("u", 0)
            x_low(0)
            dve.wait_ge(table_in, 16)
            body(0, False)
            with dve.Fori(1, NU - 1) as n:
                body(n, True)
            hidden(NU - 1)
            y_rows(NU - 2, range(ND))
            h_low(NU - 1)
            y_rows(NU - 1, range(ND))


def combine(nc, m):
    sem, keep, x1, out = m["sem"], m["keep"], m["x1"], m["out"]
    NBUF = 3
    with ExitStack() as ctx:
        rows = [keep(f"rows{i}", [TP, TOPK + NS, C], F32, ctx) for i in range(NBUF)]
        loaded, gathered = [sem(f"c_loaded{i}") for i in range(NBUF)], [sem(f"c_gathered{i}") for i in range(NBUF)]
        shared_r, chosen_r, done, stored = sem("c_shared"), sem("c_chosen"), sem("c_done"), sem("c_stored")
        block = ctx.enter_context(nc.Block())

        @block.sync
        def _(sp):
            for i in range(NT):
                if i >= NBUF:
                    sp.wait_ge(shared_r, 1 + i - NBUF)
                    sp.wait_ge(done, 1 + i - NBUF)
                for e in range(NS):
                    first = (NR + e * SU) * UT + i * TP
                    sp.dma_start(rows[i % NBUF][:, TOPK + e, :], m["y"][first:first + TP, :]
                                 ).then_inc(loaded[i % NBUF], 16)

        @block.scalar
        def _(act):
            for i in range(NT):
                act.wait_ge(done, i + 1)
                act.dma_start(out[i * TP:(i + 1) * TP, :], x1[:, i, :]).then_inc(stored, 16)
            act.wait_ge(stored, 16 * NT)

        @block.gpsimd
        def _(pool):
            def shared(i):
                r = rows[i % NBUF]
                pool.wait_ge(loaded[i % NBUF], 16 * NS * (i // NBUF + 1))
                pool.tensor_tensor(r[:, TOPK, :], r[:, TOPK, :], r[:, TOPK + 1, :], ALU.add).then_inc(shared_r, 1)

            for i in range(NT):
                if i >= NBUF:
                    pool.wait_ge(done, 1 + i - NBUF)
                for k in range(TOPK):
                    pool.indirect_dma_start(rows[i % NBUF][:, k, :], None, m["y"], bass.IndirectOffsetOnAxis(
                        ap=m["slot_of"][:, TOPK * i + k:TOPK * i + k + 1], axis=0)).then_inc(gathered[i % NBUF], 16)
                if i:
                    shared(i - 1)
            shared(NT - 1)

        @block.vector
        def _(dve):
            for i in range(NT):
                r = rows[i % NBUF]
                dve.wait_ge(gathered[i % NBUF], 16 * TOPK * (i // NBUF + 1))
                for k in range(TOPK):
                    dve.tensor_tensor(r[:, 0, :], r[:, 0, :], r[:, 1, :] if k else x1[:, i, :],
                                      ALU.add).then_inc(chosen_r, 1)
                    dve.wait_ge(chosen_r, TOPK * i + k + 1)
                dve.wait_ge(shared_r, i + 1)
                dve.tensor_tensor(x1[:, i, :], r[:, 0, :], r[:, TOPK, :], ALU.add).then_inc(done, 1)


def kernel(x, src, dst, L0_gnn_W, L0_gnn_b, L0_mix_w_qkv, L0_mix_w_proj, L0_mix_b_proj, L0_mix_proj_mat,
           L0_ffn_gate_w, L0_ffn_shared_gate, L0_ffn_shared_up, L0_ffn_shared_down, L0_ffn_routed_gate,
           L0_ffn_routed_up, L0_ffn_routed_down):
    import numpy as np
    import concourse.bacc as bacc
    from concourse.bass_utils import run_bass_kernel_spmd

    def flat(w):
        n, c = w.shape[-2] // P, w.shape[-1]
        w = w.reshape(*w.shape[:-2], n, P, c)
        return np.swapaxes(w, -3, -2).reshape(*w.shape[:-3], P, n * c)

    def halves(w):
        return [flat(w[:, :HC]), flat(w[:, HC:])]

    arr = np.asarray
    qkv_t = arr(L0_mix_w_qkv).T
    pieces = []
    for w in (arr(L0_gnn_W), qkv_t[:, 2 * C:], qkv_t[:, :C], qkv_t[:, C:2 * C], arr(L0_mix_w_proj).T):
        pieces += halves(w)
    into = [np.concatenate([arr(r), arr(s)]).transpose(0, 2, 1)
            for r, s in ((L0_ffn_routed_gate, L0_ffn_shared_gate), (L0_ffn_routed_up, L0_ffn_shared_up))]
    down = np.concatenate([arr(L0_ffn_routed_down), arr(L0_ffn_shared_down)]).transpose(0, 2, 1)
    arrays = {
        "x": arr(x), "src": arr(src), "dst": arr(dst), "w_pieces": np.stack(pieces),
        "gnn_b": arr(L0_gnn_b), "b_proj": arr(L0_mix_b_proj), "proj_t": arr(L0_mix_proj_mat).T,
        "gate_t": arr(L0_ffn_gate_w).T, "experts": np.stack([flat(into[0]), flat(into[1]), flat(down)]),
    }
    arrays = {"in_" + k: np.ascontiguousarray(v) for k, v in arrays.items()}
    nc = bacc.Bacc("TRN2", target_bir_lowering=False, num_devices=1)
    a = {k[3:]: nc.dram_tensor(k, v.shape, mybir.dt.from_np(v.dtype), kind="ExternalInput").ap()
         for k, v in arrays.items()}
    out = nc.dram_tensor("out", (T, C), F32, kind="ExternalOutput").ap()
    program(nc, a, out)
    return run_bass_kernel_spmd(nc, [arrays], core_ids=[0]).results[0]["out"]
```

```python
from contextlib import ExitStack

import concourse.bass as bass
from concourse import mybir

F32, F32R = mybir.dt.float32, mybir.dt.float32r
BF16, I32, I16, U32 = mybir.dt.bfloat16, mybir.dt.int32, mybir.dt.int16, mybir.dt.uint32
ALU = mybir.AluOpType
ACT = mybir.ActivationFunctionType
X = mybir.AxisListType.X

T, C = 1250, 768
P = 128
NT, TP = 10, 125
KB = C // P
HC = C // 2
CH = 418
CHUNKS = [(c, min(CH, T - c)) for c in range(0, T, CH)]
CHUNK_AT = [c for c, _ in CHUNKS]
LN_EPS = 1e-5

E_EDGES = 20000
EJ = E_EDGES // TP
NG = NT * len(CHUNKS)
EPAD = 512
NBATCH = (E_EDGES + NG * (EPAD - 1)) // EPAD
NBATCH += NBATCH % 2
ECOLS = NBATCH * EPAD // P
SCAT = 8

H, D, M = 12, 64, 256
HP = H // 2
DV = D + 2
NORM = float(D) ** -0.25
DIAG = 0.5 * float(D) ** -0.5
FEPS = 1e-4

NE, NS, I = 8, 2, 384
IB = I // P
TOPK = 2
UT = 256
NR = (T * TOPK + NE * (UT - 1)) // UT
SU = -(-T // UT)
NU = NR + NS * SU
UCOLS = NU * UT // P
RCOLS = NR * UT // P
TJ = NT * TOPK


def f32(ap):
    return ap.bitcast(F32)


class Chain:

    def __init__(self, sem):
        self.eng, self.sem, self.n = None, sem, 0

    def on(self, eng):
        self.eng = eng
        return self

    def __call__(self, ins):
        self.n += 1
        ins.then_inc(self.sem, 1)
        self.eng.wait_ge(self.sem, self.n)


def wait_alone(eng, sem, value, passed):
    eng.wait_ge(sem, value)
    eng.sem_inc(passed, 1)


def refine_rsqrt(dve, own, r, v, work):
    own(dve.tensor_tensor(work, r, r, ALU.mult))
    own(dve.tensor_tensor(work, work, v, ALU.mult))
    own(dve.tensor_scalar(work, work, -0.5, 1.5, ALU.mult, ALU.add))
    return dve.tensor_tensor(r, r, work, ALU.mult)


def three_products(pe, out, a_hi, a_lo, b_hi, b_lo, k, n):
    pe.matmul(out, a_hi, b_hi, start=(k == 0), stop=False)
    pe.matmul(out, a_hi, b_lo, start=False, stop=False)
    return pe.matmul(out, a_lo, b_hi, start=False, stop=(k == n - 1))


def program(nc, a, out):
    with ExitStack() as whole:
        live, done = [], []

        def sem(name):
            live.append(nc.alloc_semaphore(name))
            return live[-1]

        def next_phase():
            done.extend(live)
            live.clear()

        def recycle():
            nc.clear_and_free_semaphores(done)
            done.clear()

        def keep(name, shape, dtype, where=whole):
            return where.enter_context(nc.sbuf_tensor(name, shape, dtype))

        def dram(name, shape, dtype=F32):
            return nc.dram_tensor(name, shape, dtype, kind="Internal").ap()

        m = {
            "a": a, "out": out, "sem": sem, "keep": keep,
            "banks": [whole.enter_context(nc.psum_tensor(f"bank{i}", [P, 512], F32)) for i in range(8)],
            "ident": keep("ident", [P, P], F32),
            "before": keep("before", [P, P], F32),
            "ones": keep("ones", [P, P], F32),
            "batch_group": keep("batch_group", [1, NBATCH], I32),
            "passed": nc.alloc_semaphore("passed"),
            "own": Chain(nc.alloc_semaphore("dve_own")),
            "recycle": recycle,
            "hv": dram("hv", [2, T, C]),
            "qk": dram("qk", [2, C, T]),
            "edges": dram("edges", [P * ECOLS, 2]),
            "xn2": dram("xn2", [T, C]),
            "slots": dram("slots", [P * RCOLS, 2]),
            "att_raw": dram("att_raw", [H, DV, T]),
            "inverse": dram("inverse", [H, T]),
            "y": dram("y", [NU * UT, C]),
        }
        with ExitStack() as early:
            m["xn_hi"] = keep("xn_hi", [P, KB, T], F32R, early)
            m["xn_lo"] = keep("xn_lo", [P, KB, T], F32R, early)
            for name, dtype in (("raw", F32), ("w_hi", F32R), ("w_lo", F32R)):
                m[name] = [keep(f"{name}{i}", [P, KB, HC], dtype, early) for i in range(2)]
            first_norm(nc, m)
            next_phase()
            projections(nc, m)
            next_phase()
        m["x1"] = keep("x1", [TP, NT, C], F32)
        graph(nc, m)
        next_phase()
        m["slot_table"] = keep("slot_table", [P, UCOLS, 2], F32)
        m["slot_of"] = keep("slot_of", [TP, TJ], I32)
        m["unit_expert"] = keep("unit_expert", [1, NU], I32)
        with ExitStack() as mid:
            m["ctx"] = keep("ctx", [P, H, 2, DV], F32, mid)
            m["proj_hi"] = keep("proj_hi", [P, 2, M], F32R, mid)
            m["proj_lo"] = keep("proj_lo", [P, 2, M], F32R, mid)
            m["head_mask"] = keep("head_mask", [P, 2], F32, mid)
            keys(nc, m)
            next_phase()
            m["att_hi"] = keep("att_hi", [P, HP, T], F32R, mid)
            m["att_lo"] = keep("att_lo", [P, HP, T], F32R, mid)
            queries(nc, m)
            next_phase()
            mix_and_route(nc, m)
            next_phase()
        experts(nc, m)
        next_phase()
        combine(nc, m)


def first_norm(nc, m):
    a, sem, banks, ident = m["a"], m["sem"], m["banks"], m["ident"]
    with ExitStack() as ctx:
        x_in = m["keep"]("x_in", [TP, NT, C], F32, ctx)
        stats = m["keep"]("stats", [TP, NT, 2, 6], F32, ctx)
        mean_var = m["keep"]("mean_var", [TP, NT, 2], F32, ctx)
        spread = m["keep"]("spread", [TP, NT], F32, ctx)
        rstd = m["keep"]("rstd", [TP, NT], F32, ctx)
        work = m["keep"]("newton", [TP, NT], F32, ctx)
        zeros = m["keep"]("zeros", [P, RCOLS * 2], F32, ctx)
        filler = m["keep"]("filler", [P, ECOLS * 2], F32, ctx)
        x_loaded = [sem(f"x_loaded{i}") for i in range(NT // 2)]
        consts = sem("consts")
        var_ready, sd_ready, xn_ready = sem("var_ready"), sem("sd_ready"), sem("xn_ready")
        turned, hi_done, lo_done, filled = sem("turned"), sem("n1_hi"), sem("n1_lo"), sem("filled")
        w_loaded, w_high = [sem("n1_w_loaded0"), sem("n1_w_loaded1")], sem("n1_w_hi")
        NB = 4
        block = ctx.enter_context(nc.Block())

        @block.sync
        def _(sp):
            for i in range(0, NT, 2):
                sp.dma_start(x_in[:, i:i + 2, :], a["x"][i * TP:(i + 2) * TP, :].rearrange("(i p) c -> p i c", p=TP)
                             ).then_inc(x_loaded[i // 2], 16)
            for n in range(2):
                sp.dma_start(m["raw"][n][:], a["w_pieces"][n].rearrange("p (k c) -> p k c", k=KB)
                             ).then_inc(w_loaded[n], 16)
            sp.wait_ge(consts, 4)
            sp.dma_start(m["edges"].rearrange("(p c) k -> p (c k)", p=P), filler[:]).then_inc(filled, 16)
            sp.wait_ge(consts, 5)
            sp.dma_start(m["slots"].rearrange("(p c) k -> p (c k)", p=P),
                         zeros[:]).then_inc(filled, 16)
            sp.wait_ge(filled, 32)

        @block.gpsimd
        def _(pool):
            pool.memset(m["ones"][:], 1.0).then_inc(consts, 1)
            pool.wait_ge(consts, 1)
            pool.affine_select(out=ident[:], in_=m["ones"][:], compare_op=ALU.is_equal, fill=0.0, base=0,
                               pattern=[[-1, P]], channel_multiplier=1).then_inc(consts, 1)
            pool.affine_select(out=m["before"][:], in_=m["ones"][:], compare_op=ALU.is_gt, fill=0.0, base=0,
                               pattern=[[1, P]], channel_multiplier=-1).then_inc(consts, 1)
            pool.memset(filler[:], -1.0).then_inc(consts, 1)
            pool.memset(zeros[:], 0.0).then_inc(consts, 1)
            for n in range(2):
                pool.wait_ge(w_high, n + 1)
                pool.tensor_tensor(m["w_lo"][n][:], m["raw"][n][:], f32(m["w_hi"][n][:]), ALU.subtract)

        @block.vector
        def _(dve):
            own = m["own"].on(dve)
            for i in range(NT):
                dve.wait_ge(x_loaded[i // 2], 16)
                for h in range(2):
                    last = dve.bn_stats(stats[:, i, h, :], x_in[:, i, h * HC:(h + 1) * HC])
            own(last)
            for i in range(NT):
                last = dve.bn_aggr(mean_var[:, i, :], stats[:, i, :, :])
            own(last)
            dve.tensor_scalar(spread[:], mean_var[:, :, 1], LN_EPS, None, ALU.add).then_inc(var_ready, 1)
            dve.wait_ge(sd_ready, 1)
            own(dve.reciprocal(rstd[:], rstd[:]))
            own(refine_rsqrt(dve, own, rstd[:], spread[:], work[:]))

            def lows(n):
                dve.wait_ge(hi_done, n + 1)
                i, h = n // 2, n % 2
                at = (slice(None), slice(3 * h, 3 * h + 3), slice(i * TP, (i + 1) * TP))
                dve.tensor_tensor(m["xn_lo"][at], banks[n % NB][:, 0:3 * TP].rearrange("p (b t) -> p b t", b=3),
                                  f32(m["xn_hi"][at]), ALU.subtract).then_inc(lo_done, 1)

            for i in range(NT):
                dve.tensor_scalar(x_in[:, i, :], x_in[:, i, :], mean_var[:, i, 0:1], rstd[:, i:i + 1],
                                  ALU.subtract, ALU.mult).then_inc(xn_ready, 1)
                if i:
                    lows(2 * i - 2)
                    lows(2 * i - 1)
            lows(2 * NT - 2)
            lows(2 * NT - 1)

        @block.scalar
        def _(act):
            act.wait_ge(var_ready, 1)
            act.activation(rstd[:], spread[:], ACT.Sqrt).then_inc(sd_ready, 1)
            for n in range(2 * NT):
                i, h = n // 2, n % 2
                act.wait_ge(turned, n + 1)
                act.activation(m["xn_hi"][:, 3 * h:3 * h + 3, i * TP:(i + 1) * TP],
                               banks[n % NB][:, 0:3 * TP].rearrange("p (b t) -> p b t", b=3),
                               ACT.Copy).then_inc(hi_done, 1)
                if n in (3, 7):
                    act.wait_ge(w_loaded[n // 4], 16)
                    act.activation(m["w_hi"][n // 4][:], m["raw"][n // 4][:], ACT.Copy).then_inc(w_high, 1)

        @block.tensor
        def _(pe):
            pe.wait_ge(consts, 3)
            for n in range(2 * NT):
                i, h = n // 2, n % 2
                pe.wait_ge(xn_ready, i + 1)
                if n >= NB:
                    pe.wait_ge(lo_done, n - NB + 1)
                for b in range(3):
                    k = 3 * h + b
                    last = pe.transpose(banks[n % NB][:, b * TP:(b + 1) * TP],
                                        x_in[:, i, k * P:(k + 1) * P], ident[0:TP, 0:TP])
                last.then_inc(turned, 1)


def find_slots(dve, own, pe_ready, pe_done, s, group, groups, per, pad):
    shape = [TP, groups, per]
    own(dve.tensor_tensor(s["hot"], group.unsqueeze(1).broadcast_to(shape),
                          s["iota"].unsqueeze(2).broadcast_to(shape), ALU.is_equal))
    flat = "p g j -> p (g j)"
    own(dve.tensor_tensor_scan(s["rank"].rearrange(flat), s["keep_on"].rearrange(flat),
                               s["hot"].rearrange(flat), 0.0, ALU.mult, ALU.add))
    dve.tensor_copy(s["total"], s["rank"][:, :, per - 1]).then_inc(pe_ready, 1)
    dve.wait_ge(pe_done, 1)
    own(dve.tensor_scalar(s["count"], s["sums"][:, groups:2 * groups], float(pad - 1), None, ALU.add))
    own(dve.tensor_scalar(s["count"], s["count"], pad.bit_length() - 1, None, ALU.logical_shift_right))
    own(dve.tensor_copy(s["batches"], s["count"]))
    own(dve.tensor_tensor_scan(s["upto"], s["ones"], s["batches"], 0.0, ALU.mult, ALU.add))
    own(dve.tensor_tensor(s["base"], s["upto"], s["batches"], ALU.subtract))
    own(dve.tensor_scalar(s["base"], s["base"], float(pad), -1.0, ALU.mult, ALU.add))
    own(dve.tensor_tensor(s["base"], s["sums"][:, 0:groups], s["base"], ALU.add))
    own(dve.tensor_tensor(s["wide"], s["rank"], s["base"].unsqueeze(2).broadcast_to(shape), ALU.add))
    own(dve.tensor_tensor(s["wide"], s["wide"], s["hot"], ALU.mult))
    own(dve.tensor_reduce(s["slot"], s["wide"].rearrange("p g j -> p j g"), X, ALU.add))


def table_rows(dve, own, s, cols):
    own(dve.tensor_copy(s["slot_i"], s["slot"]))
    own(dve.tensor_scalar(s["part"], s["slot_i"], P - 1, None, ALU.bitwise_and))
    own(dve.tensor_scalar(s["col"], s["slot_i"], P.bit_length() - 1, None, ALU.logical_shift_right))
    return dve.scalar_tensor_tensor(s["row"], s["part"], float(cols), s["col"], ALU.mult, ALU.add)


def slot_buffers(m, ctx, name, groups, per, wide):
    k = m["keep"]
    s = {
        "iota": k(name + "_iota", [TP, groups], F32, ctx)[:],
        "hot": k(name + "_hot", [TP, groups, per], BF16, ctx)[:],
        "keep_on": k(name + "_keep_on", [TP, groups, per], BF16, ctx)[:],
        "rank": k(name + "_rank", [TP, groups, per], BF16, ctx)[:],
        "wide": wide,
        "ones": m["ones"][0:TP, 0:groups],
    }
    for n in ("total", "batches", "upto", "base"):
        s[n] = k(f"{name}_{n}", [TP, groups], F32, ctx)[:]
    s["count"] = k(name + "_count", [TP, groups], I32, ctx)[:]
    s["slot"] = k(name + "_slot", [TP, per], F32, ctx)[:]
    for n in ("slot_i", "part", "col", "row"):
        s[n] = k(f"{name}_{n}", [TP, per], I32, ctx)[:]
    return s


def projections(nc, m):
    a, sem, banks = m["a"], m["sem"], m["banks"]
    keep = m["keep"]
    NPIECE = 8
    NB = 6
    with ExitStack() as ctx:
        raw, w_hi, w_lo = m["raw"], m["w_hi"], m["w_lo"]
        stage = [keep(f"stage{i}", [P, NT * HC], F32, ctx) for i in range(2)]
        src_i = keep("src_i", [TP, EJ], I32, ctx)
        dst_i = keep("dst_i", [TP, EJ], I32, ctx)
        src_f = keep("src_f", [TP, EJ], F32, ctx)
        dst_f = keep("dst_f", [TP, EJ], F32, ctx)
        tile_f = keep("tile_f", [TP, EJ], F32, ctx)
        chunk_f = keep("chunk_f", [TP, EJ], F32, ctx)
        group = keep("group", [TP, EJ], F32, ctx)
        pair = keep("pair", [TP, EJ, 2], F32, ctx)
        wide = keep("wide", [TP, NG, EJ], F32, ctx)
        s = slot_buffers(m, ctx, "edge", NG, EJ, wide[:])
        s["sums"] = banks[7][0:TP, 0:2 * NG]
        batch_iota = keep("batch_iota", [1, NBATCH], F32, ctx)
        set_row = [keep(f"set_row{i}", [TP, SCAT], I32, ctx) for i in range(2)]
        set_pair = [keep(f"set_pair{i}", [TP, SCAT, 2], F32, ctx) for i in range(2)]

        w_loaded, stored = [sem("w_loaded0"), sem("w_loaded1")], [sem("stored0"), sem("stored1")]
        hi_ready, lo_ready = sem("w_hi"), sem("w_lo")
        product, evacuated = sem("product"), sem("evacuated")
        e_loaded, e_const = sem("e_loaded"), sem("e_const")
        totals_ready, sums_ready, rows_ready = sem("totals_ready"), sem("sums_ready"), sem("rows_ready")
        set_filled, scattered = sem("set_filled"), [sem("scattered0"), sem("scattered1")]

        def groups_upto(n):
            return NT * min(n, 4) + KB // 2 * len(CHUNKS) * max(n - 4, 0)

        def bank_of(n, j):
            return (n * NT + j) % NB if n < 4 else (4 * NT + n % 2 * 9 + j) % NB

        block = ctx.enter_context(nc.Block())

        @block.sync
        def _(sp):
            sp.dma_start(src_i[:], a["src"].rearrange("(p j) -> p j", p=TP)).then_inc(e_loaded, 16)
            sp.dma_start(dst_i[:], a["dst"].rearrange("(p j) -> p j", p=TP)).then_inc(e_loaded, 16)
            for n in range(2, NPIECE + 2):
                if n < NPIECE:
                    if n >= 4:
                        sp.wait_ge(lo_ready, n - 3)
                    sp.dma_start(raw[n % 2][:], a["w_pieces"][n].rearrange("p (k c) -> p k c", k=KB)
                                 ).then_inc(w_loaded[n % 2], 16)
                if True:
                    q = n - 2
                    sp.wait_ge(evacuated, NB + groups_upto(q + 1))
                    half = slice((q % 2) * HC, (q % 2 + 1) * HC)
                    if q < 4:
                        sp.dma_start(m["hv"][q // 2, :, half].rearrange("(i p) c -> p i c", p=TP),
                                     stage[q % 2][0:TP, :].rearrange("p (i c) -> p i c", i=NT)
                                     ).then_inc(stored[q % 2], 16)
                    else:
                        sp.dma_start(m["qk"][q // 2 - 2, half, :].rearrange("(b p) t -> p b t", p=P),
                                     stage[q % 2][:, 0:3 * T].rearrange("p (b t) -> p b t", b=3)
                                     ).then_inc(stored[q % 2], 16)
            for done in stored:
                sp.wait_ge(done, 8 * NPIECE)

        @block.tensor
        def _(pe):
            def piece(n, at, kind):
                if not isinstance(n, int) or n >= 2:
                    pe.wait_ge(lo_ready, n - 1)
                if kind == "tokens":
                    for i in range(NT):
                        g = n * NT + i
                        pe.wait_ge(evacuated, g + 1)
                        bank = banks[bank_of(n, i)]
                        for k in range(KB):
                            last = three_products(
                                pe, bank[0:TP, 0:HC], m["xn_hi"][:, k, i * TP:(i + 1) * TP],
                                m["xn_lo"][:, k, i * TP:(i + 1) * TP], w_hi[at][:, k, :], w_lo[at][:, k, :], k, KB)
                        last.then_inc(product, 1)
                        if isinstance(n, int) and n * NT + i == 7:
                            group_sums()
                else:
                    for b in range(3):
                        for c, (c0, cn) in enumerate(CHUNKS):
                            j = 3 * b + c
                            pe.wait_ge(evacuated, n * 9 + 4 + j + 1)
                            bank = banks[bank_of(4 + at, j)]
                            for k in range(KB):
                                last = three_products(
                                    pe, bank[:, 0:cn], w_hi[at][:, k, b * P:(b + 1) * P],
                                    w_lo[at][:, k, b * P:(b + 1) * P], m["xn_hi"][:, k, c0:c0 + cn],
                                    m["xn_lo"][:, k, c0:c0 + cn], k, KB)
                            last.then_inc(product, 1)

            def group_sums():
                pe.wait_ge(totals_ready, 1)
                pe.matmul(s["sums"][:, 0:NG], m["before"][0:TP, 0:TP], s["total"], start=True, stop=True)
                pe.matmul(s["sums"][:, NG:2 * NG], m["ones"][0:TP, 0:TP], s["total"], start=True,
                          stop=True).then_inc(sums_ready, 1)

            piece(0, 0, "tokens")
            piece(1, 1, "tokens")
            piece(2, 0, "tokens")
            piece(3, 1, "tokens")
            with pe.Fori(4, 8, 2) as n:
                piece(n, 0, "features")
                piece(n + 1, 1, "features")

        @block.scalar
        def _(act):
            def high(n):
                act.wait_ge(w_loaded[n % 2], 16 * (n // 2))
                act.activation(w_hi[n % 2][:], raw[n % 2][:], ACT.Copy).then_inc(hi_ready, 1)

            act.sem_inc(evacuated, NB)
            g = 0
            for n in range(NPIECE):
                if n >= 2:
                    act.wait_ge(stored[n % 2], 16 * (n // 2))
                if n < 4:
                    for i in range(NT):
                        act.wait_ge(product, g + 1)
                        act.activation(stage[n % 2][0:TP, i * HC:(i + 1) * HC], banks[bank_of(n, i)][0:TP, 0:HC],
                                       ACT.Copy).then_inc(evacuated, 1)
                        g += 1
                else:
                    for j in range(9):
                        b, (c0, cn) = j // 3, CHUNKS[j % 3]
                        act.wait_ge(product, g + 1)
                        act.activation(stage[n % 2][:, b * T + c0:b * T + c0 + cn],
                                       banks[bank_of(n, j)][:, 0:cn], ACT.Copy).then_inc(evacuated, 1)
                        g += 1
                if n + 2 < NPIECE:
                    high(n + 2)

        @block.vector
        def _(dve):
            own = m["own"].on(dve)

            def low(n):
                dve.wait_ge(hi_ready, n - 1)
                dve.tensor_tensor(w_lo[n % 2][:], raw[n % 2][:], f32(w_hi[n % 2][:]),
                                  ALU.subtract).then_inc(lo_ready, 1)

            dve.wait_ge(e_loaded, 32)
            dve.tensor_copy(src_f[:], src_i[:])
            own(dve.tensor_copy(dst_f[:], dst_i[:]))
            own(dve.tensor_scalar(tile_f[:], src_f[:], float(TP), None, ALU.is_ge))
            own(dve.tensor_scalar(chunk_f[:], dst_f[:], float(CHUNK_AT[1]), None, ALU.is_ge))
            for i in range(2, NT):
                own(dve.scalar_tensor_tensor(tile_f[:], src_f[:], float(i * TP), tile_f[:], ALU.is_ge, ALU.add))
            own(dve.scalar_tensor_tensor(dst_f[:], chunk_f[:], -float(CHUNK_AT[1]), dst_f[:], ALU.mult, ALU.add))
            own(dve.tensor_scalar(group[:], dst_f[:], float(CHUNK_AT[2] - CHUNK_AT[1]), None, ALU.is_ge))
            own(dve.tensor_tensor(group[:], group[:], chunk_f[:], ALU.mult))
            own(dve.tensor_tensor(chunk_f[:], chunk_f[:], group[:], ALU.add))
            own(dve.scalar_tensor_tensor(pair[:, :, 1], group[:], -float(CHUNK_AT[2] - CHUNK_AT[1]), dst_f[:],
                                         ALU.mult, ALU.add))
            dve.scalar_tensor_tensor(pair[:, :, 0], tile_f[:], -float(TP), src_f[:], ALU.mult, ALU.add)
            own(dve.scalar_tensor_tensor(group[:], tile_f[:], float(len(CHUNKS)), chunk_f[:], ALU.mult, ALU.add))
            dve.wait_ge(e_const, 4)
            find_slots(dve, own, totals_ready, sums_ready, s, group[:], NG, EJ, EPAD)
            table_rows(dve, own, s, ECOLS).then_inc(rows_ready, 1)
            first = wide[0:1, 0:NG, 0:NBATCH]
            own(dve.tensor_tensor(first, batch_iota[:].unsqueeze(1).broadcast_to([1, NG, NBATCH]),
                                  s["upto"][0:1, :].unsqueeze(2).broadcast_to([1, NG, NBATCH]), ALU.is_ge))
            own(dve.tensor_reduce(batch_iota[:], first.rearrange("p g j -> p j g"), X, ALU.add))
            own(dve.tensor_scalar(m["batch_group"][:], batch_iota[:], float(NG - 1), None, ALU.min))
            for n in range(2, NPIECE):
                low(n)

        @block.gpsimd
        def _(pool):
            pool.iota(s["iota"], [[1, NG]], base=0, channel_multiplier=0,
                      allow_small_or_imprecise_dtypes=True).then_inc(e_const, 1)
            pool.iota(batch_iota[:], [[1, NBATCH]], base=0, channel_multiplier=0,
                      allow_small_or_imprecise_dtypes=True).then_inc(e_const, 1)
            pool.memset(s["keep_on"], 1.0).then_inc(e_const, 1)
            pool.wait_ge(e_const, 3)
            pool.memset(s["keep_on"][:, :, 0:1], 0.0).then_inc(e_const, 1)

            def send(n, at, turn):
                if turn is not None:
                    wait_alone(pool, scattered[at], 16 * SCAT * turn, m["passed"])
                pool.tensor_copy(set_row[at][:], s["row"][:, bass.ds(n * SCAT, SCAT)])
                pool.tensor_copy(set_pair[at][:], pair[:, bass.ds(n * SCAT, SCAT), :]).then_inc(set_filled, 1)
                wait_alone(pool, set_filled, n + 1, m["passed"])
                for u in range(SCAT):
                    pool.indirect_dma_start(m["edges"], bass.IndirectOffsetOnAxis(ap=set_row[at][:, u:u + 1], axis=0),
                                            set_pair[at][:, u, :], None).then_inc(scattered[at], 16)

            pool.wait_ge(rows_ready, 1)
            send(0, 0, None)
            send(1, 1, None)
            turns = EJ // SCAT // 2
            with pool.Fori(1, turns) as t:
                send(2 * t, 0, t)
                send(2 * t + 1, 1, t)
            pool.wait_ge(scattered[0], 16 * SCAT * turns)
            pool.wait_ge(scattered[1], 16 * SCAT * turns)


def graph(nc, m):
    a, sem, banks, keep, x1 = m["a"], m["sem"], m["banks"], m["keep"], m["x1"]
    AW = len(CHUNKS) * CH
    U = EPAD // P
    NHOT = 2 * U
    HALF = NT * AW // 2
    with ExitStack() as ctx:
        adj = keep("adj", [TP, NT * AW], F32, ctx)
        adj3 = adj[:].rearrange("p (a d) -> p a d", a=NT)
        table = keep("table", [P, ECOLS, 2], F32, ctx)
        iota = keep("iota", [P, CH], I16, ctx)
        hot_src = [keep(f"hot_src{i}", [P, TP], BF16, ctx) for i in range(NHOT)]
        column = keep("column", [TP, AW], F32, ctx)
        hot_dst = [keep(f"hot_dst{i}", [P, CH], BF16, ctx) for i in range(NHOT)]
        h_hi = keep("h_hi", [TP, NT, C], F32R, ctx)
        h_lo = keep("h_lo", [TP, NT, C], F32R, ctx)
        a_hi = [keep(f"a_hi{i}", [TP, NT, TP], F32R, ctx) for i in range(2)]
        a_lo = [keep(f"a_lo{i}", [TP, NT, TP], F32R, ctx) for i in range(2)]
        bias = keep("bias", [TP, 2, C], F32, ctx)
        dis = keep("dis", [TP, NT], F32, ctx)
        dis_work = keep("dis_work", [TP, NT], F32, ctx)

        table_in, x_in, h_loaded = sem("table_in"), sem("g_x_in"), sem("h_loaded")
        consts, adj_zero, hot_ready, hot_used = sem("g_consts"), sem("adj_zero"), sem("hot_ready"), sem("hot_used")
        added, column_ready = sem("added"), sem("column_ready")
        degree_ready, sd_ready, dis_ready = sem("degree_ready"), sem("g_sd"), sem("dis_ready")
        h_hi_ready, h_lo_ready = sem("h_hi_ready"), sem("h_lo_ready")
        a_hi_ready, a_lo_ready, row_done, row_read = sem("a_hi"), sem("a_lo"), sem("row_done"), sem("row_read")
        bias_ready = sem("bias_ready")
        block = ctx.enter_context(nc.Block())

        @block.sync
        def _(sp):
            sp.dma_start(table[:].rearrange("p c k -> p (c k)"), m["edges"].rearrange("(p c) k -> p (c k)", p=P)
                         ).then_inc(table_in, 16)
            sp.dma_start(x1[:], a["x"].rearrange("(i p) c -> p i c", p=TP)).then_inc(x_in, 16)
            sp.dma_start(bias[:, 0, :], a["gnn_b"].partition_broadcast(TP)).then_inc(x_in, 16)
            sp.dma_start(bias[:, 1, :], a["b_proj"].partition_broadcast(TP)).then_inc(x_in, 16)
            sp.dma_start(f32(h_lo[:]), m["hv"][0].rearrange("(i p) c -> p i c", p=TP)).then_inc(h_loaded, 16)

        @block.gpsimd
        def _(pool):
            pool.iota(iota[:], [[1, CH]], base=0, channel_multiplier=0,
                      allow_small_or_imprecise_dtypes=True).then_inc(consts, 1)
            pool.memset(adj[:, HALF:], 0.0).then_inc(adj_zero, 1)
            pool.wait_ge(adj_zero, 2)
            for i in range(NT):
                pool.tensor_copy(adj3[:, i, i * TP:(i + 1) * TP], m["ident"][0:TP, 0:TP]).then_inc(adj_zero, 1)
            pool.wait_ge(x_in, 48)
            pool.tensor_tensor(bias[:, 0, :], bias[:, 0, :], bias[:, 1, :], ALU.add).then_inc(bias_ready, 1)
            pool.wait_ge(bias_ready, 1)
            for i in range(NT):
                pool.tensor_tensor(x1[:, i, :], x1[:, i, :], bias[:, 0, :], ALU.add).then_inc(bias_ready, 1)

        @block.vector
        def _(dve):
            own = m["own"].on(dve)
            dve.sem_inc(added, 2)
            dve.memset(adj[:, 0:HALF], 0.0).then_inc(adj_zero, 1)
            dve.wait_ge(table_in, 16)
            dve.wait_ge(consts, 1)
            dve.wait_ge(adj_zero, 2 + NT)
            def hots(n, v):
                for u in range(U):
                    q = v * U + u
                    col = n * U + q
                    dve.wait_ge(hot_used, n * U + q + 1)
                    dve.tensor_scalar(hot_src[q][:], iota[:, 0:TP], table[:, bass.ds(col, 1), 0], None,
                                      ALU.is_equal)
                    dve.tensor_scalar(hot_dst[q][:], iota[:], table[:, bass.ds(col, 1), 1], None,
                                      ALU.is_equal).then_inc(hot_ready, 1)

            groups = [ctx.enter_context(dve.register(f"group{v}")) for v in range(2)]

            def group_of(b, v):
                dve.reg_load(groups[v], m["batch_group"][0:1, bass.ds(b, 1)])
                return dve.snap(groups[v], min_val=0, max_val=NG - 1) * CH

            def add(b, v, at):
                dve.wait_ge(hot_used, NHOT + (b + 1) * U)
                dve.wait_ge(added, b + 2)
                at = adj[:, bass.ds(at, CH)]
                dve.tensor_tensor(at, at, banks[v][0:TP, 0:CH], ALU.add).then_inc(added, 1)

            hots(0, 0)
            with dve.Fori(0, NBATCH // 2 - 1) as step:
                n = 2 * step
                at = group_of(n, 0)
                hots(n, 1)
                add(n, 0, at)
                at = group_of(n + 1, 1)
                hots(n + 2, 0)
                add(n + 1, 1, at)
            hots(NBATCH - 2, 1)
            add(NBATCH - 2, 0, group_of(NBATCH - 2, 0))
            add(NBATCH - 1, 1, group_of(NBATCH - 1, 1))
            dve.wait_ge(added, NBATCH + 2)
            dve.tensor_reduce(column[:], adj[:].rearrange("p (a d) -> p d a", a=NT), X, ALU.add
                              ).then_inc(column_ready, 1)
            dve.wait_ge(sd_ready, 1)
            own(dve.reciprocal(dis[:], dis[:]))
            refine_rsqrt(dve, own, dis[:], banks[6][0:TP, 0:NT], dis_work[:]).then_inc(dis_ready, 1)

            def a_low(i):
                dve.wait_ge(a_hi_ready, i + 1)
                dve.tensor_tensor(a_lo[i % 2][:], adj3[:, :, i * TP:(i + 1) * TP], f32(a_hi[i % 2][:]),
                                  ALU.subtract).then_inc(a_lo_ready, 1)

            dve.wait_ge(dis_ready, 1)
            for i in range(NT):
                dve.wait_ge(h_hi_ready, i + 1)
                dve.scalar_tensor_tensor(h_lo[:, i, :], f32(h_lo[:, i, :]), dis[:, i:i + 1], f32(h_hi[:, i, :]),
                                         ALU.mult, ALU.subtract).then_inc(h_lo_ready, 1)
                if i in (1, 3):
                    a_low(i // 2)
            for i in range(NT):
                for h in range(2):
                    n = 2 * i + h
                    dve.wait_ge(row_done, n + 1)
                    dve.wait_ge(bias_ready, i + 2)
                    at = x1[:, i, h * HC:(h + 1) * HC]
                    dve.scalar_tensor_tensor(at, banks[2 + n % 4][0:TP, 0:HC], dis[:, i:i + 1], at,
                                             ALU.mult, ALU.add).then_inc(row_read, 1)
                if i + 2 < NT:
                    a_low(i + 2)

        @block.scalar
        def _(act):
            def a_high(i):
                act.activation(a_hi[i % 2][:], adj3[:, :, i * TP:(i + 1) * TP], ACT.Copy).then_inc(a_hi_ready, 1)

            act.wait_ge(added, NBATCH + 2)
            a_high(0)
            a_high(1)
            act.wait_ge(degree_ready, 1)
            act.activation(dis[:], banks[6][0:TP, 0:NT], ACT.Sqrt).then_inc(sd_ready, 1)
            act.wait_ge(dis_ready, 1)
            act.wait_ge(h_loaded, 16)
            for i in range(NT):
                act.activation(h_hi[:, i, :], f32(h_lo[:, i, :]), ACT.Copy,
                               scale=dis[:, i:i + 1]).then_inc(h_hi_ready, 1)
            for i in range(2, NT):
                act.wait_ge(row_read, 2 * (i - 1))
                a_high(i)

        @block.tensor
        def _(pe):
            pe.sem_inc(hot_used, NHOT)
            with pe.Fori(0, NBATCH // 2) as step:
                n = 2 * step
                for v in range(2):
                    pe.wait_ge(added, n + v + 1)
                    for u in range(U):
                        q = v * U + u
                        pe.wait_ge(hot_ready, n * U + q + 1)
                        last = pe.matmul(banks[v][0:TP, 0:CH], hot_src[q][:], hot_dst[q][:],
                                         start=(u == 0), stop=(u == U - 1))
                        last.then_inc(hot_used, 1)
            pe.wait_ge(column_ready, 1)
            for i in range(NT):
                last = pe.matmul(banks[6][0:TP, i:i + 1], column[:, i * TP:(i + 1) * TP], m["ones"][0:TP, 0:1],
                                 start=True, stop=True)
            last.then_inc(degree_ready, 1)
            for i in range(NT):
                pe.wait_ge(a_lo_ready, i + 1)
                for h in range(2):
                    n = 2 * i + h
                    if n >= 4:
                        pe.wait_ge(row_read, n - 3)
                    for s in range(NT):
                        if i == 0 and h == 0:
                            pe.wait_ge(h_lo_ready, s + 1)
                        last = three_products(pe, banks[2 + n % 4][0:TP, 0:HC], a_hi[i % 2][:, s, :],
                                              a_lo[i % 2][:, s, :], h_hi[:, s, h * HC:(h + 1) * HC],
                                              h_lo[:, s, h * HC:(h + 1) * HC], s, NT)
                    last.then_inc(row_done, 1)


def keys(nc, m):
    a, sem, banks, keep = m["a"], m["sem"], m["banks"], m["keep"]
    with ExitStack() as ctx:
        proj_in = keep("proj_in", [P, 2, M], F32, ctx)
        k_in = keep("k_in", [P, T], F32, ctx)
        k_hi = keep("k_hi", [P, T], F32R, ctx)
        k_lo = keep("k_lo", [P, T], F32R, ctx)
        k_sq = keep("k_sq", [P, T], F32, ctx)
        v_in = [keep(f"v_in{i}", [TP, NT, 2, DV], F32, ctx) for i in range(2)]
        e_f = [keep(f"e_f{i}", [TP, 2, M], F32, ctx) for i in range(4)]
        e_hi = [keep(f"e_hi{i}", [TP, NT, 2, M], F32R, ctx) for i in range(2)]
        e_lo = [keep(f"e_lo{i}", [TP, NT, 2, M], F32R, ctx) for i in range(2)]
        neg_max = [keep(f"neg_max{i}", [TP, NT, 2], F32, ctx) for i in range(2)]
        shift = [keep(f"shift{i}", [TP, NT, 2], F32, ctx) for i in range(2)]
        weight = [keep(f"weight{i}", [TP, NT, 2], F32, ctx) for i in range(2)]
        top = [keep(f"top{i}", [P, 2], F32, ctx) for i in range(2)]
        head_top = [keep(f"head_top{i}", [P, 2], F32, ctx) for i in range(2)]
        neg_top = [keep(f"neg_top{i}", [P, 2], F32, ctx) for i in range(2)]
        tops = keep("tops", [P, H], F32, ctx)
        v_w = keep("v_w", [TP, NT, 2, DV], F32, ctx)
        v_hi = keep("v_hi", [TP, NT, 2, DV], F32R, ctx)
        v_lo = keep("v_lo", [TP, NT, 2, DV], F32R, ctx)
        sums = keep("sums", [DV, H, M], F32, ctx)
        v_sum = keep("v_sum", [DV, H], F32, ctx)
        all_top = keep("all_top", [P, 1], F32, ctx)
        factor = keep("factor", [P, H], F32, ctx)

        p_loaded, k_loaded, v_loaded = sem("p_loaded"), sem("k_loaded"), [sem("v_loaded0"), sem("v_loaded1")]
        setup, p_scaled, p_hi_ready, p_ready = sem("k_setup"), sem("p_scaled"), sem("p_hi"), sem("p_ready")
        k_hi_r, k_lo_r, k_sq_r, diag_done = sem("k_hi"), sem("k_lo"), sem("k_sq"), sem("k_diag")
        product, maxed, exped = sem("k_product"), sem("k_maxed"), sem("k_exped")
        e_hi_r, e_lo_r, top_r, shifted = sem("e_hi"), sem("e_lo"), sem("k_top"), sem("k_shifted")
        all_red, neg_r, weight_r = sem("k_reduced"), sem("k_neg_top"), sem("k_weight")
        v_w_r, v_hi_r, v_lo_r = sem("v_weighed"), sem("v_hi"), sem("v_lo")
        summed, sums_read, fin = sem("k_summed"), sem("k_sums_read"), sem("k_final")
        fin_act, fin_turned = sem("k_final_act"), sem("k_final_turned")
        m["recycle"]()
        block = ctx.enter_context(nc.Block())

        def drive(eng, step):
            step(0, 0, True, False)
            with eng.Fori(0, HP // 2 - 1) as turn:
                step(2 * turn + 1, 1, False, False)
                step(2 * turn + 2, 0, False, False)
            step(HP - 1, 1, False, True)

        def ring(v, i):
            return (v * NT + i) % 4

        @block.sync
        def _(sp):
            sp.wait_ge(setup, 3)
            for h in range(2):
                sp.dma_start(proj_in[h * D:(h + 1) * D, h, :], a["proj_t"]).then_inc(p_loaded, 16)
            for hp in range(HP):
                if hp:
                    sp.wait_ge(k_lo_r, hp)
                    sp.wait_ge(k_sq_r, hp)
                sp.dma_start(k_in[:], m["qk"][1, hp * P:(hp + 1) * P, :]).then_inc(k_loaded, 16)
                if hp >= 2:
                    sp.wait_ge(summed, 2 + hp - 1)
                for j in range(2):
                    h = 2 * hp + j
                    sp.dma_start(v_in[hp % 2][:, :, j, 0:D],
                                 m["hv"][1, :, h * D:(h + 1) * D].rearrange("(i p) d -> p i d", p=TP)
                                 ).then_inc(v_loaded[hp % 2], 16)

        @block.gpsimd
        def _(pool):
            pool.memset(proj_in[:], 0.0).then_inc(setup, 1)
            pool.memset(v_in[0][:], 1.0).then_inc(setup, 1)
            pool.memset(v_in[1][:], 1.0).then_inc(setup, 1)
            for t in top:
                pool.memset(t[:], -3e38).then_inc(setup, 1)
            pool.memset(m["head_mask"][:], 0.0).then_inc(setup, 1)
            pool.wait_ge(setup, 6)
            for j in range(2):
                pool.memset(m["head_mask"][j * D:(j + 1) * D, j:j + 1], DIAG).then_inc(setup, 1)
            pool.wait_ge(setup, 8)

            def square(hp):
                pool.wait_ge(k_loaded, 16 * (hp + 1))
                pool.wait_ge(diag_done, hp + 1)
                pool.tensor_tensor(k_sq[:], k_in[:], k_in[:], ALU.mult).then_inc(k_sq_r, 1)

            def weigh(hp, v):
                pool.wait_ge(weight_r, 2 * hp + 2)
                if isinstance(hp, int):
                    pool.wait_ge(v_loaded[v], 32 * (hp // 2 + 1))
                else:
                    pool.wait_ge(v_loaded[v], 16 * (hp + 2 - v))
                pool.wait_ge(v_lo_r, hp + 1)
                pool.tensor_tensor(v_w[:], v_in[v][:], weight[v][:].unsqueeze(3)
                                   .broadcast_to([TP, NT, 2, DV]), ALU.mult).then_inc(v_w_r, 1)

            def step(hp, v, first, last):
                if not first:
                    weigh(hp - 1, 1 - v)
                if not last:
                    square(hp + 1)
                wait_alone(pool, top_r, hp + 1, m["passed"])
                pool.partition_all_reduce(head_top[v][:], top[v][:], P, bass.bass_isa.ReduceOp.max
                                          ).then_inc(all_red, 1)
                wait_alone(pool, all_red, hp + 1, m["passed"])
                pool.tensor_copy(tops[:, bass.ds(2 * hp, 2)], head_top[v][:])
                pool.tensor_scalar(neg_top[v][:], head_top[v][:], -1.0, None, ALU.mult).then_inc(neg_r, 1)

            square(0)
            drive(pool, step)
            weigh(HP - 1, 1)

        @block.scalar
        def _(act):
            act.wait_ge(p_scaled, 1)
            act.activation(m["proj_hi"][:], proj_in[:], ACT.Copy).then_inc(p_hi_ready, 1)
            act.sem_inc(exped, 4)
            act.sem_inc(sums_read, 1)

            def high(hp):
                act.wait_ge(k_loaded, 16 * (hp + 1))
                act.activation(k_hi[:], k_in[:], ACT.Copy).then_inc(k_hi_r, 1)

            def weights(hp, v):
                act.wait_ge(neg_r, hp + 1)
                act.wait_ge(shifted, 2 + hp + 1)
                for j in range(2):
                    act.activation(weight[v][:, :, j], shift[v][:, :, j], ACT.Exp, scale=-1.0,
                                   bias=neg_top[v][0:TP, j:j + 1]).then_inc(weight_r, 1)

            def values(hp):
                act.wait_ge(v_w_r, hp + 1)
                act.wait_ge(summed, 2 + hp)
                act.activation(v_hi[:], v_w[:], ACT.Copy).then_inc(v_hi_r, 1)

            def read_sums(hp):
                act.wait_ge(summed, 2 + hp + 1)
                act.activation(sums[:, bass.ds(2 * hp, 2), :].rearrange("p h f -> p (h f)"), banks[7][0:DV, :],
                               ACT.Copy)
                act.activation(v_sum[:, bass.ds(2 * hp, 2)], banks[6][0:DV, 0:2], ACT.Copy
                               ).then_inc(sums_read, 1)

            def step(hp, v, first, last):
                for i in range(NT + 1):
                    if i < NT:
                        r = ring(v, i)
                        act.wait_ge(maxed, hp * NT + i + 1)
                        act.wait_ge(e_lo_r, hp * NT + i + 1)
                        for j in range(2):
                            done = act.activation(e_f[r][:, j, :], banks[r][0:TP, j * M:(j + 1) * M], ACT.Exp,
                                                  bias=neg_max[v][:, i, j:j + 1])
                        done.then_inc(exped, 1)
                    if i == 1:
                        act.wait_ge(summed, hp + 1)
                    if i:
                        act.wait_ge(exped, 4 + hp * NT + i)
                        act.activation(e_hi[v][:, i - 1, :, :], e_f[ring(v, i - 1)][:], ACT.Copy
                                       ).then_inc(e_hi_r, 1)
                    if not first and i == 0:
                        weights(hp - 1, 1 - v)
                    if not first and i == 3:
                        values(hp - 1)
                if not last:
                    act.wait_ge(product, (hp + 1) * NT)
                    high(hp + 1)
                if not first:
                    read_sums(hp - 1)

            high(0)
            drive(act, step)
            weights(HP - 1, 1)
            values(HP - 1)
            read_sums(HP - 1)
            act.wait_ge(fin, 1)
            act.activation(factor[:], tops[:], ACT.Exp, bias=all_top[:]).then_inc(fin_act, 1)

        @block.vector
        def _(dve):
            dve.wait_ge(p_loaded, 32)
            dve.tensor_scalar(proj_in[:], proj_in[:], NORM, None, ALU.mult).then_inc(p_scaled, 1)
            dve.wait_ge(p_hi_ready, 1)
            dve.tensor_tensor(m["proj_lo"][:], proj_in[:], f32(m["proj_hi"][:]), ALU.subtract).then_inc(p_ready, 1)
            dve.sem_inc(e_lo_r, 4)
            dve.sem_inc(v_lo_r, 1)
            dve.sem_inc(shifted, 2)
            dve.wait_ge(setup, 8)

            def low(hp):
                dve.wait_ge(k_hi_r, hp + 1)
                dve.tensor_tensor(k_lo[:], k_in[:], f32(k_hi[:]), ALU.subtract).then_inc(k_lo_r, 1)

            def value_lows(hp):
                dve.wait_ge(v_hi_r, hp + 1)
                dve.tensor_tensor(v_lo[:], v_w[:], f32(v_hi[:]), ALU.subtract).then_inc(v_lo_r, 1)

            def step(hp, v, first, last):
                for i in range(NT + 2):
                    if i < NT:
                        dve.wait_ge(product, hp * NT + i + 1)
                        dve.tensor_reduce(neg_max[v][:, i, :],
                                          banks[ring(v, i)][0:TP, :].rearrange("p (j f) -> p j f", j=2), X,
                                          ALU.max, negate=True).then_inc(maxed, 1)
                    if i >= 2:
                        dve.wait_ge(e_hi_r, hp * NT + i - 1)
                        dve.tensor_tensor(e_lo[v][:, i - 2, :, :], e_f[ring(v, i - 2)][:],
                                          f32(e_hi[v][:, i - 2, :, :]), ALU.subtract).then_inc(e_lo_r, 1)
                    if not first and i == 4:
                        value_lows(hp - 1)
                    if i == NT:
                        dve.wait_ge(maxed, (hp + 1) * NT)
                        dve.tensor_reduce(top[v][0:TP, :], neg_max[v][:].rearrange("p i j -> p j i"), X, ALU.min,
                                          negate=True).then_inc(top_r, 1)
                dve.wait_ge(diag_done, hp + 2)
                dve.tensor_tensor(shift[v][:], neg_max[v][:],
                                  banks[4 + v][0:TP, 0:2 * NT].rearrange("p (i j) -> p i j", j=2),
                                  ALU.add).then_inc(shifted, 1)
                if not last:
                    low(hp + 1)

            low(0)
            drive(dve, step)
            value_lows(HP - 1)
            dve.wait_ge(neg_r, HP)
            dve.tensor_reduce(all_top[:], tops[:], X, ALU.max, negate=True).then_inc(fin, 1)
            dve.wait_ge(fin_act, 1)
            dve.wait_ge(sums_read, HP + 1)
            dve.tensor_scalar(v_sum[:], v_sum[:], FEPS, None, ALU.mult).then_inc(fin, 1)
            dve.wait_ge(fin, 2)
            for h in range(H):
                last = dve.tensor_scalar(sums[:, h, :], sums[:, h, :], factor[0:DV, h:h + 1], v_sum[:, h:h + 1],
                                         ALU.mult, ALU.add)
            last.then_inc(fin, 1)
            for q in range(4):
                dve.wait_ge(fin_turned, q + 1)
                dve.tensor_copy(m["ctx"][:, 3 * q:3 * q + 3, :, :].rearrange("p h b d -> p (h b d)"),
                                banks[q][:, 0:6 * DV])

        @block.tensor
        def _(pe):
            pe.sem_inc(diag_done, 1)
            pe.sem_inc(summed, 2)
            pe.wait_ge(p_ready, 1)
            pe.wait_ge(setup, 8)

            def diagonal(hp, v):
                pe.wait_ge(k_sq_r, hp + 1)
                pe.wait_ge(shifted, hp + 1)
                for i in range(NT):
                    last = pe.matmul(banks[4 + v][0:TP, 2 * i:2 * i + 2], k_sq[:, i * TP:(i + 1) * TP],
                                     m["head_mask"][:], start=True, stop=True)
                last.then_inc(diag_done, 1)

            def plain_sums(hp, v):
                pe.wait_ge(sums_read, hp + 1)
                pe.wait_ge(v_w_r, hp + 1)
                for j in range(2):
                    for i in range(NT):
                        pe.matmul(banks[6][0:DV, j:j + 1], v_in[v][:, i, j, :], m["ones"][0:TP, 0:1],
                                  start=(i == 0), stop=(i == NT - 1))

            def sum_head(hp, v, j):
                if j == 0:
                    pe.wait_ge(v_lo_r, 1 + hp + 1)
                    pe.wait_ge(e_lo_r, 4 + (hp + 1) * NT)
                for i in range(NT):
                    done = three_products(pe, banks[7][0:DV, j * M:(j + 1) * M], v_hi[:, i, j, :],
                                          v_lo[:, i, j, :], e_hi[v][:, i, j, :], e_lo[v][:, i, j, :], i, NT)
                if j == 1:
                    done.then_inc(summed, 1)

            def step(hp, v, first, last):
                pe.wait_ge(k_lo_r, hp + 1)
                for i in range(NT):
                    pe.wait_ge(exped, hp * NT + i + 1)
                    features(pe, m, banks[ring(v, i)], k_hi, k_lo, i).then_inc(product, 1)
                    if not first and i == 6:
                        plain_sums(hp - 1, 1 - v)
                    if not first and i == 8:
                        sum_head(hp - 1, 1 - v, 0)
                if not last:
                    diagonal(hp + 1, 1 - v)
                if not first:
                    sum_head(hp - 1, 1 - v, 1)

            diagonal(0, 0)
            drive(pe, step)
            plain_sums(HP - 1, 1)
            sum_head(HP - 1, 1, 0)
            sum_head(HP - 1, 1, 1)
            pe.wait_ge(fin, 3)
            for q in range(4):
                for n in range(6):
                    h, b = 3 * q + n // 2, n % 2
                    last = pe.transpose(banks[q][:, n * DV:(n + 1) * DV], sums[:, h, b * P:(b + 1) * P],
                                        m["ident"][0:DV, 0:DV])
                last.then_inc(fin_turned, 1)


def features(pe, m, bank, x_hi, x_lo, i):
    at = (slice(None), slice(i * TP, (i + 1) * TP))
    return three_products(pe, bank[0:TP, :], x_hi[at], x_lo[at], m["proj_hi"][:].rearrange("p j f -> p (j f)"),
                          m["proj_lo"][:].rearrange("p j f -> p (j f)"), 0, 1)


def queries(nc, m):
    sem, banks, keep = m["sem"], m["banks"], m["keep"]
    STEP = 2 * NT
    SLOTS = HP * NT
    LEAD = 10
    E_LAG, T_LAG, HI_LAG, LO_LAG, O_LAG, D_LAG, N_LAG = 1, 2, 3, 4, 5, 15, 19
    CT = 2
    with ExitStack() as ctx:
        q_in = [keep(f"q_in{i}", [P, T], F32, ctx) for i in range(2)]
        q_hi = [keep(f"q_hi{i}", [P, T], F32R, ctx) for i in range(2)]
        q_lo = [keep(f"q_lo{i}", [P, T], F32R, ctx) for i in range(2)]
        q_sq = keep("q_sq", [P, T], F32, ctx)
        diag = [keep(f"diag{i}", [TP, NT, 2], F32, ctx) for i in range(2)]
        neg = keep("neg", [TP, 4, 2], F32, ctx)
        shift = keep("q_shift", [TP, 4, 2], F32, ctx)
        e_f = [keep(f"q_e{i}", [TP, 2, M], F32, ctx) for i in range(4)]
        f_hi = [keep(f"f_hi{i}", [P, 2, 2, CT * TP], F32R, ctx) for i in range(2)]
        f_lo = [keep(f"f_lo{i}", [P, 2, 2, CT * TP], F32R, ctx) for i in range(2)]
        c_hi = [keep(f"c_hi{i}", [P, 2, 2, DV], F32R, ctx) for i in range(2)]
        c_lo = [keep(f"c_lo{i}", [P, 2, 2, DV], F32R, ctx) for i in range(2)]
        o_f = [keep(f"o_f{i}", [DV, 2, CT * TP], F32, ctx) for i in range(2)]
        upper = [keep(f"upper{i}", [P, T], F32, ctx) for i in range(2)]
        lower = [keep(f"lower{i}", [P, T], F32, ctx) for i in range(2)]

        divisors = keep("divisors", [TP, 2, NT], F32, ctx)
        F_BANKS, T_BANKS = banks[0:2], banks[2:6]

        q_loaded = [sem("q_loaded0"), sem("q_loaded1")]
        q_hi_r, q_lo_r, q_sq_r = sem("q_hi"), sem("q_lo"), sem("q_sq")
        diag_done, diag_read, product = sem("q_diag"), sem("q_diag_read"), sem("q_product")
        maxed, shifted, exped, turned = sem("q_maxed"), sem("q_shifted"), sem("q_exped"), sem("q_turned")
        c_hi_r, c_lo_r = sem("c_hi"), sem("c_lo")
        f_hi_r, f_lo_r, o_done, o_copied = sem("f_hi"), sem("f_lo"), sem("o_done"), sem("o_copied")
        o_stored, parts_in = [sem("o_stored0"), sem("o_stored1")], [sem("parts_in0"), sem("parts_in1")]
        inverted, divided, a_hi_r, a_lo_r = sem("inverted"), sem("divided"), sem("att_hi_r"), sem("att_lo_r")
        d_in, d_out = sem("divisors_in"), sem("divisors_out")
        block = ctx.enter_context(nc.Block())

        def drive(eng, slot):
            for s in range(LEAD):
                slot(s, None)
            with eng.Fori(0, 2) as t:
                for s in range(LEAD, LEAD + STEP):
                    slot(s, t)
            for s in range(LEAD + 2 * STEP, SLOTS + N_LAG + 3):
                slot(s, None)

        def live(s, t, lag=0):
            return t is not None or 0 <= s - lag < SLOTS

        def nth(n, t, step):
            return n if t is None else n + step * t

        @block.sync
        def _(sp):
            def load(hp, at):
                sp.dma_start(q_in[at][:], m["qk"][0, bass.ds(hp * P, P), :]).then_inc(q_loaded[at], 16)

            load(0, 0)
            load(1, 1)

            def slot(s, t):
                if s % NT == 0 and s and (t is not None or s // NT + 1 < HP):
                    hp, at = nth(s // NT + 1, t, 2), (s // NT + 1) % 2
                    sp.wait_ge(q_lo_r, hp - 1)
                    wait_alone(sp, q_sq_r, hp - 1, m["passed"])
                    load(hp, at)
                if live(s, t, O_LAG + 1) and (s - O_LAG - 1) % CT == 1:
                    n = (s - O_LAG - 1) // CT
                    c = n % (NT // CT)
                    hp = nth(n // (NT // CT), t, 2)
                    wait_alone(sp, o_copied, nth(n, t, NT) + 3, m["passed"])
                    sp.dma_start(m["att_raw"][bass.ds(hp * 2, 2), :, c * CT * TP:(c + 1) * CT * TP]
                                 .rearrange("j d t -> d j t"), o_f[n % 2][:]).then_inc(o_stored[n % 2], 16)
                if live(s, t, D_LAG) and (s - D_LAG) % NT == 0:
                    n = (s - D_LAG) // NT
                    hp = nth(n, t, 2)
                    chunks = NT // CT * (n + 1)
                    sp.wait_ge(o_stored[0], 16 * nth((chunks + 1) // 2, t, NT // CT))
                    wait_alone(sp, o_stored[1], 16 * nth(chunks // 2, t, NT // CT), m["passed"])
                    for j in range(2):
                        sp.dma_start(divisors[:, j, :], m["att_raw"][bass.ds(hp * 2 + j, 1), D, :].rearrange(
                            "j (p c) -> (j p) c", p=TP)).then_inc(d_in, 16)
                if live(s, t, D_LAG + 1) and (s - D_LAG - 1) % NT == 0:
                    n = (s - D_LAG - 1) // NT
                    hp, at = nth(n, t, 2), n % 2
                    wait_alone(sp, inverted, hp + 1, m["passed"])
                    for j in range(2):
                        sp.dma_start(m["inverse"][bass.ds(hp * 2 + j, 1), :].rearrange("j (p c) -> (j p) c", p=TP),
                                     divisors[:, j, :]).then_inc(d_out, 16)
                    sp.wait_ge(d_out, 32 * (hp + 1))
                    sp.wait_ge(divided, hp + 1)
                    wait_alone(sp, a_lo_r, hp + 1, m["passed"])
                    for j in range(2):
                        rows, h = slice(j * D, (j + 1) * D), bass.ds(hp * 2 + j, 1)
                        sp.dma_start(upper[at][rows, :], m["att_raw"][h, 0:D, :].rearrange("j d t -> (j d) t")
                                     ).then_inc(parts_in[at], 16)
                        sp.dma_start(lower[at][rows, :], m["inverse"][h, :].broadcast_to([D, T])
                                     ).then_inc(parts_in[at], 16)

            drive(sp, slot)

        @block.gpsimd
        def _(pool):
            def slot(s, t):
                if s % NT == 5 and (t is not None or s // NT + 1 < HP):
                    square(s // NT + 1, t)
                if live(s, t, D_LAG + 2) and (s - D_LAG - 2) % NT == 0:
                    n = (s - D_LAG - 2) // NT
                    pool.wait_ge(parts_in[n % 2], 64 * (nth(n // 2, t, 1) + 1))
                    pool.tensor_tensor(upper[n % 2][:], upper[n % 2][:], lower[n % 2][:], ALU.mult
                                       ).then_inc(divided, 1)

            def square(n, t):
                pool.wait_ge(q_loaded[n % 2], 16 * (nth(n // 2, t, 1) + 1))
                pool.wait_ge(diag_done, nth(n, t, 2) + 1)
                pool.tensor_tensor(q_sq[:], q_in[n % 2][:], q_in[n % 2][:], ALU.mult).then_inc(q_sq_r, 1)

            pool.sem_inc(divided, 2)
            square(0, None)
            drive(pool, slot)

        @block.scalar
        def _(act):
            act.sem_inc(exped, 4)
            act.sem_inc(o_copied, 2)

            def high(n, t):
                act.wait_ge(q_loaded[n % 2], 16 * (nth(n // 2, t, 1) + 1))
                act.activation(q_hi[n % 2][:], q_in[n % 2][:], ACT.Copy).then_inc(q_hi_r, 1)

            def slot(s, t):
                if live(s, t) and s % NT == 0:
                    n = s // NT
                    act.activation(c_hi[n % 2][:], m["ctx"][:, bass.ds(nth(2 * n, t, 4), 2), :, :],
                                   ACT.Copy).then_inc(c_hi_r, 1)
                if live(s, t) and s % NT == 5 and (t is not None or s // NT + 1 < HP):
                    high(s // NT + 1, t)
                if live(s, t, E_LAG):
                    g = s - E_LAG
                    act.wait_ge(shifted, nth(g, t, STEP) + 1)
                    act.wait_ge(turned, nth(g, t, STEP) + 1)
                    for j in range(2):
                        last = act.activation(e_f[g % 4][:, j, :], F_BANKS[g % 2][0:TP, j * M:(j + 1) * M],
                                              ACT.Exp, bias=shift[:, g % 4, j:j + 1])
                    last.then_inc(exped, 1)
                if live(s, t, HI_LAG):
                    g = s - HI_LAG
                    c, u = g // CT, g % CT
                    act.wait_ge(turned, nth(g, t, STEP) + 5)
                    act.wait_ge(o_done, nth(c, t, NT) + 1)
                    act.activation(f_hi[c % 2][:, :, :, u * TP:(u + 1) * TP], T_BANKS[g % 4][:, 0:4 * TP]
                                   .rearrange("p (j b t) -> p j b t", j=2, b=2), ACT.Copy, bias=FEPS
                                   ).then_inc(f_hi_r, 1)
                if live(s, t, O_LAG + 1) and (s - O_LAG - 1) % CT == 1:
                    n = (s - O_LAG - 1) // CT
                    act.wait_ge(o_done, nth(n, t, NT) + 3)
                    if t is not None or n >= 2:
                        act.wait_ge(o_stored[n % 2], 16 * nth(n // 2, t, NT // CT))
                    act.activation(o_f[n % 2][:], banks[6][0:DV, 0:2 * CT * TP].rearrange(
                        "p (j t) -> p j t", j=2), ACT.Copy).then_inc(o_copied, 1)
                if live(s, t, N_LAG) and (s - N_LAG) % NT == 0:
                    n = (s - N_LAG) // NT
                    act.wait_ge(divided, nth(n, t, 2) + 3)
                    act.activation(m["att_hi"][:, bass.ds(nth(n, t, 2), 1), :], upper[n % 2][:].unsqueeze(1),
                                   ACT.Copy).then_inc(a_hi_r, 1)

            high(0, None)
            drive(act, slot)

        @block.vector
        def _(dve):
            dve.sem_inc(diag_read, 1)
            dve.sem_inc(f_lo_r, 4)
            dve.sem_inc(a_lo_r, 2)

            def low(n, t):
                dve.wait_ge(q_hi_r, nth(n, t, 2) + 1)
                dve.tensor_tensor(q_lo[n % 2][:], q_in[n % 2][:], f32(q_hi[n % 2][:]), ALU.subtract
                                  ).then_inc(q_lo_r, 1)

            def read_diag(n, t):
                dve.wait_ge(diag_done, nth(n, t, 2) + 2)
                dve.tensor_copy(diag[n % 2][:].rearrange("p i j -> p (i j)"), banks[7][0:TP, 0:2 * NT]
                                ).then_inc(diag_read, 1)

            def slot(s, t):
                if live(s, t) and s % NT == 1:
                    n = s // NT
                    dve.wait_ge(c_hi_r, nth(n, t, 2) + 1)
                    dve.tensor_tensor(c_lo[n % 2][:], m["ctx"][:, bass.ds(nth(2 * n, t, 4), 2), :, :],
                                      f32(c_hi[n % 2][:]), ALU.subtract).then_inc(c_lo_r, 1)
                if live(s, t) and (t is not None or s // NT + 1 < HP):
                    if s % NT == 5:
                        low(s // NT + 1, t)
                    if s % NT == 9:
                        read_diag(s // NT + 1, t)
                if live(s, t):
                    dve.wait_ge(product, nth(s, t, STEP) + 1)
                    dve.tensor_reduce(neg[:, s % 4, :], F_BANKS[s % 2][0:TP, :].rearrange(
                        "p (j f) -> p j f", j=2), X, ALU.max, negate=True).then_inc(maxed, 1)
                if live(s, t, LO_LAG):
                    g = s - LO_LAG
                    c, u = g // CT, g % CT
                    dve.wait_ge(f_hi_r, nth(g, t, STEP) + 1)
                    at = (slice(None), slice(None), slice(None), slice(u * TP, (u + 1) * TP))
                    dve.scalar_tensor_tensor(
                        f_lo[c % 2][at], T_BANKS[g % 4][:, 0:4 * TP].rearrange(
                            "p (j b t) -> p j b t", j=2, b=2), FEPS, f32(f_hi[c % 2][at]), ALU.add,
                        ALU.subtract).then_inc(f_lo_r, 1)
                if live(s, t):
                    n = s // NT
                    dve.wait_ge(maxed, nth(s, t, STEP) + 1)
                    if s % NT == 0:
                        dve.wait_ge(diag_read, nth(n, t, 2) + 2)
                    dve.wait_ge(exped, nth(s, t, STEP) + 1)
                    dve.tensor_tensor(shift[:, s % 4, :], neg[:, s % 4, :], diag[n % 2][:, s % NT, :],
                                      ALU.subtract).then_inc(shifted, 1)
                if live(s, t, D_LAG + 1) and (s - D_LAG - 1) % NT == 0:
                    n = (s - D_LAG - 1) // NT
                    dve.wait_ge(d_in, 32 * (nth(n, t, 2) + 1))
                    dve.reciprocal(divisors[:], divisors[:]).then_inc(inverted, 1)
                if live(s, t, N_LAG) and (s - N_LAG) % NT == 0:
                    n = (s - N_LAG) // NT
                    dve.wait_ge(a_hi_r, nth(n, t, 2) + 1)
                    at = bass.ds(nth(n, t, 2), 1)
                    dve.tensor_tensor(m["att_lo"][:, at, :], upper[n % 2][:].unsqueeze(1),
                                      f32(m["att_hi"][:, at, :]), ALU.subtract).then_inc(a_lo_r, 1)

            low(0, None)
            read_diag(0, None)
            drive(dve, slot)

        @block.tensor
        def _(pe):
            pe.sem_inc(diag_done, 1)
            pe.sem_inc(turned, 4)
            pe.sem_inc(o_done, 2)

            def diagonal(n, t):
                pe.wait_ge(q_sq_r, nth(n, t, 2) + 1)
                pe.wait_ge(diag_read, nth(n, t, 2) + 1)
                for i in range(NT):
                    last = pe.matmul(banks[7][0:TP, 2 * i:2 * i + 2], q_sq[:, i * TP:(i + 1) * TP],
                                     m["head_mask"][:], start=True, stop=True)
                last.then_inc(diag_done, 1)

            def slot(s, t):
                if live(s, t):
                    n, i = s // NT, s % NT
                    if i == 0:
                        pe.wait_ge(q_lo_r, nth(n, t, 2) + 1)
                    pe.wait_ge(exped, nth(s, t, STEP) + 3)
                    features(pe, m, F_BANKS[s % 2], q_hi[n % 2], q_lo[n % 2], i).then_inc(product, 1)
                if live(s, t) and s % NT == 7 and (t is not None or s // NT + 1 < HP):
                    diagonal(s // NT + 1, t)
                if live(s, t, O_LAG) and (s - O_LAG) % CT == 1:
                    g = s - O_LAG
                    n, c = g // NT, g // CT
                    if g % NT == 1:
                        pe.wait_ge(c_lo_r, nth(n, t, 2) + 1)
                    pe.wait_ge(f_lo_r, nth(g, t, STEP) + 5)
                    pe.wait_ge(o_copied, nth(c, t, NT) + 2)
                    for j in range(2):
                        for b in range(2):
                            last = three_products(pe, banks[6][0:DV, j * CT * TP:(j + 1) * CT * TP],
                                                  c_hi[n % 2][:, j, b, :], c_lo[n % 2][:, j, b, :],
                                                  f_hi[c % 2][:, j, b, :], f_lo[c % 2][:, j, b, :], b, 2)
                    last.then_inc(o_done, 1)
                if live(s, t, T_LAG):
                    g = s - T_LAG
                    pe.wait_ge(exped, nth(g, t, STEP) + 5)
                    pe.wait_ge(f_lo_r, nth(g, t, STEP) + 1)
                    for j in range(2):
                        for b in range(2):
                            c = (2 * j + b) * TP
                            last = pe.transpose(T_BANKS[g % 4][:, c:c + TP],
                                                e_f[g % 4][:, j, b * P:(b + 1) * P], m["ident"][0:TP, 0:TP])
                    last.then_inc(turned, 1)

            diagonal(0, None)
            drive(pe, slot)


def mix_and_route(nc, m):
    a, sem, banks, keep, x1 = m["a"], m["sem"], m["banks"], m["keep"], m["x1"]
    with ExitStack() as ctx:
        raw = [keep(f"mix_raw{i}", [P, KB, HC], F32, ctx) for i in range(1)] * 2
        w_hi = [keep(f"mix_hi{i}", [P, KB, HC], F32R, ctx) for i in range(2)]
        w_lo = [keep(f"mix_lo{i}", [P, KB, HC], F32R, ctx) for i in range(2)]
        stats = keep("stats2", [TP, NT, 2, 6], F32, ctx)
        mean_var = keep("mean_var2", [TP, NT, 2], F32, ctx)
        spread = keep("spread2", [TP, NT], F32, ctx)
        rstd = keep("rstd2", [TP, NT], F32, ctx)
        xn = [keep(f"xn{i}", [TP, C], F32, ctx) for i in range(2)]
        xn_t = [keep(f"xn_t{i}", [P, KB, TP], F32, ctx) for i in range(2)]
        gate = keep("gate", [P, KB, NE], F32, ctx)
        logits = keep("logits", [TP, NT, NE], F32, ctx)
        best = keep("best", [TP, NT], F32, ctx)
        total = keep("total", [TP, NT], F32, ctx)
        order = keep("order", [TP, NT, 8], F32, ctx)
        which = keep("which", [TP, NT, 8], U32, ctx)
        expert = keep("expert", [TP, NT, TOPK], F32, ctx)
        token_i = keep("token_i", [TP, NT, TOPK], I32, ctx)
        pair = keep("moe_pair", [TP, TJ, 2], F32, ctx)
        wide = keep("moe_wide", [TP, NE, TJ], F32, ctx)
        s = slot_buffers(m, ctx, "moe", NE, TJ, wide[:])
        s["sums"] = banks[7][0:TP, 0:2 * NE]
        unit_iota = keep("unit_iota", [1, NR], F32, ctx)
        unit_hot = keep("unit_hot", [1, NE, NR], F32, ctx)

        w_loaded, hi_r, lo_r, product = sem("m_w_loaded"), sem("m_w_hi"), sem("m_w_lo"), sem("m_product")
        added, var_r, sd_r = sem("m_added"), sem("m_var"), sem("m_sd")
        gate_loaded, xn_stored = sem("gate_loaded"), [sem("xn2_stored0"), sem("xn2_stored1")]
        xn_r, xt_done, xt_r, l_done = sem("xn2_ready"), sem("xt_done"), sem("xt_ready"), sem("logits_done")
        e_ready, e_done, consts = sem("m_exp_ready"), sem("m_exp_done"), sem("m_consts")
        totals_r, sums_r, rows_r, sent = sem("m_totals"), sem("m_sums"), sem("m_rows"), sem("m_sent")
        block = ctx.enter_context(nc.Block())

        @block.sync
        def _(sp):
            sp.dma_start(gate[:], a["gate_t"].rearrange("(k p) e -> p k e", p=P)).then_inc(gate_loaded, 16)
            for n in range(2):
                if n:
                    sp.wait_ge(lo_r, 1)
                sp.dma_start(raw[n][:], a["w_pieces"][8 + n].rearrange("p (k c) -> p k c", k=KB)
                             ).then_inc(w_loaded, 16)
            for i in range(NT):
                sp.wait_ge(xn_r, i + 1)
                sp.dma_start(m["xn2"][i * TP:(i + 1) * TP, :], xn[i % 2][:]).then_inc(xn_stored[i % 2], 16)
            for done in xn_stored:
                sp.wait_ge(done, 8 * NT)

        @block.tensor
        def _(pe):
            for h in range(2):
                pe.wait_ge(lo_r, h + 1)
                for i in range(NT):
                    n = h * NT + i
                    if n >= 4:
                        pe.wait_ge(added, n - 3)
                    for k in range(HP):
                        last = three_products(
                            pe, banks[n % 4][0:TP, 0:HC], m["att_hi"][:, k, i * TP:(i + 1) * TP],
                            m["att_lo"][:, k, i * TP:(i + 1) * TP], w_hi[h][:, k, :], w_lo[h][:, k, :], k, HP)
                    last.then_inc(product, 1)
            pe.wait_ge(added, 2 * NT)
            pe.wait_ge(gate_loaded, 16)
            for i in range(NT + 1):
                if i < NT:
                    pe.wait_ge(xn_r, i + 1)
                    if i >= 2:
                        pe.wait_ge(xt_r, i - 1)
                    for k in range(KB):
                        bank = banks[2 * (i % 2) + k // 3]
                        last = pe.transpose(bank[:, k % 3 * TP:(k % 3 + 1) * TP], xn[i % 2][:, k * P:(k + 1) * P],
                                            m["ident"][0:TP, 0:TP])
                    last.then_inc(xt_done, 1)
                if i:
                    pe.wait_ge(xt_r, i)
                    for k in range(KB):
                        last = pe.matmul(banks[6][0:TP, (i - 1) * NE:i * NE], xn_t[(i - 1) % 2][:, k, :],
                                         gate[:, k, :], start=(k == 0), stop=(k == KB - 1))
                    last.then_inc(l_done, 1)
            pe.wait_ge(totals_r, 1)
            pe.matmul(s["sums"][:, 0:NE], m["before"][0:TP, 0:TP], s["total"], start=True, stop=True)
            pe.matmul(s["sums"][:, NE:2 * NE], m["ones"][0:TP, 0:TP], s["total"], start=True,
                      stop=True).then_inc(sums_r, 1)

        @block.scalar
        def _(act):
            for n in range(2):
                act.wait_ge(w_loaded, 16 * (n + 1))
                act.activation(w_hi[n][:], raw[n][:], ACT.Copy).then_inc(hi_r, 1)
            act.wait_ge(var_r, 1)
            act.activation(rstd[:], spread[:], ACT.Sqrt).then_inc(sd_r, 1)
            for i in range(NT):
                act.wait_ge(xt_done, i + 1)
                if i >= 2:
                    act.wait_ge(l_done, i - 1)
                for h in range(2):
                    last = act.activation(xn_t[i % 2][:, 3 * h:3 * h + 3, :], banks[2 * (i % 2) + h][:, 0:3 * TP]
                                          .rearrange("p (b t) -> p b t", b=3), ACT.Copy)
                last.then_inc(xt_r, 1)
            act.wait_ge(e_ready, 1)
            act.activation(logits[:], logits[:], ACT.Exp).then_inc(e_done, 1)

        @block.vector
        def _(dve):
            own = m["own"].on(dve)
            for n in range(2):
                dve.wait_ge(hi_r, n + 1)
                dve.tensor_tensor(w_lo[n][:], raw[n][:], f32(w_hi[n][:]), ALU.subtract).then_inc(lo_r, 1)
            for h in range(2):
                for i in range(NT):
                    dve.wait_ge(product, h * NT + i + 1)
                    at = x1[:, i, h * HC:(h + 1) * HC]
                    dve.tensor_tensor(at, at, banks[(h * NT + i) % 4][0:TP, 0:HC], ALU.add).then_inc(added, 1)
            dve.wait_ge(added, 2 * NT)
            for i in range(NT):
                for h in range(2):
                    last = dve.bn_stats(stats[:, i, h, :], x1[:, i, h * HC:(h + 1) * HC])
            own(last)
            for i in range(NT):
                last = dve.bn_aggr(mean_var[:, i, :], stats[:, i, :, :])
            own(last)
            dve.tensor_scalar(spread[:], mean_var[:, :, 1], LN_EPS, None, ALU.add).then_inc(var_r, 1)
            dve.wait_ge(sd_r, 1)
            own(dve.reciprocal(rstd[:], rstd[:]))
            own(refine_rsqrt(dve, own, rstd[:], spread[:], best[:]))
            for i in range(NT):
                if i >= 2:
                    dve.wait_ge(xn_stored[i % 2], 16 * (i // 2))
                    dve.wait_ge(xt_done, i - 1)
                dve.tensor_scalar(xn[i % 2][:], x1[:, i, :], mean_var[:, i, 0:1], rstd[:, i:i + 1],
                                  ALU.subtract, ALU.mult).then_inc(xn_r, 1)
            dve.wait_ge(l_done, NT)
            own(dve.tensor_copy(logits[:].rearrange("p i e -> p (i e)"), banks[6][0:TP, 0:NT * NE]))
            own(dve.tensor_reduce(best[:], logits[:], X, ALU.max))
            own(dve.tensor_tensor(logits[:], logits[:], best[:].unsqueeze(2).broadcast_to([TP, NT, NE]),
                                  ALU.subtract))
            dve.sem_inc(e_ready, 1)
            dve.wait_ge(e_done, 1)
            own(dve.tensor_reduce(total[:], logits[:], X, ALU.add))
            own(dve.reciprocal(total[:], total[:]))
            own(dve.tensor_tensor(logits[:], logits[:], total[:].unsqueeze(2).broadcast_to([TP, NT, NE]),
                                  ALU.mult))
            for i in range(NT):
                last = dve.max(order[:, i, :], logits[:, i, :])
            own(last)
            for i in range(NT):
                last = dve.max_index(which[:, i, :], order[:, i, :], logits[:, i, :])
            own(last)
            own(dve.tensor_copy(expert[:], which[:, :, 0:TOPK]))
            own(dve.tensor_tensor(total[:], order[:, :, 0], order[:, :, 1], ALU.add))
            own(dve.tensor_scalar(total[:], total[:], 1e-8, None, ALU.add))
            own(dve.reciprocal(total[:], total[:]))
            dve.wait_ge(consts, 5)
            own(dve.tensor_tensor(pair[:, :, 1].rearrange("p (i k) -> p i k", k=TOPK), order[:, :, 0:TOPK],
                                  total[:].unsqueeze(2).broadcast_to([TP, NT, TOPK]), ALU.mult))
            find_slots(dve, own, totals_r, sums_r, s, expert[:].rearrange("p i k -> p (i k)"), NE, TJ, UT)
            own(table_rows(dve, own, s, RCOLS))
            own(dve.tensor_copy(m["slot_of"][:], s["slot_i"]))
            dve.sem_inc(rows_r, 1)
            own(dve.tensor_tensor(unit_hot[:], unit_iota[:].unsqueeze(1).broadcast_to([1, NE, NR]),
                                  s["upto"][0:1, :].unsqueeze(2).broadcast_to([1, NE, NR]), ALU.is_ge))
            own(dve.tensor_reduce(unit_iota[:], unit_hot[:].rearrange("p g j -> p j g"), X, ALU.add))
            own(dve.tensor_scalar(m["unit_expert"][:, 0:NR], unit_iota[:], float(NE - 1), None, ALU.min))

        @block.gpsimd
        def _(pool):
            pool.iota(s["iota"], [[1, NE]], base=0, channel_multiplier=0,
                      allow_small_or_imprecise_dtypes=True).then_inc(consts, 1)
            pool.iota(unit_iota[:], [[1, NR]], base=0, channel_multiplier=0,
                      allow_small_or_imprecise_dtypes=True).then_inc(consts, 1)
            pool.memset(s["keep_on"], 1.0).then_inc(consts, 1)
            pool.wait_ge(consts, 3)
            pool.memset(s["keep_on"][:, :, 0:1], 0.0).then_inc(consts, 1)
            pool.iota(pair[:, :, 0].bitcast(I32).rearrange("p (i k) -> p i k", k=TOPK), [[TP, NT], [0, TOPK]],
                      base=0, channel_multiplier=1).then_inc(consts, 1)
            for e in range(NS):
                at = m["slot_table"][:, RCOLS + e * SU * UT // P:RCOLS + (e + 1) * SU * UT // P, :]
                pool.iota(at[:, :, 0].bitcast(I32), [[P, SU * UT // P]], base=0,
                          channel_multiplier=1).then_inc(consts, 1)
                pool.memset(at[:, :, 1], 1.0 / NS).then_inc(consts, 1)
                pool.memset(m["unit_expert"][:, NR + e * SU:NR + (e + 1) * SU], NE + e).then_inc(consts, 1)
            pool.wait_ge(consts, 5 + 3 * NS)
            shared = m["slot_table"][:, RCOLS:UCOLS, 0].bitcast(I32)
            pool.tensor_scalar(shared, shared, float(T - 1), None, ALU.min).then_inc(consts, 1)
            pool.wait_ge(rows_r, 1)
            for u in range(TJ):
                pool.indirect_dma_start(m["slots"], bass.IndirectOffsetOnAxis(ap=s["row"][:, u:u + 1], axis=0),
                                        pair[:, u, :], None).then_inc(sent, 16)
            pool.wait_ge(sent, 16 * TJ)


def experts(nc, m):
    a, sem, banks, keep = m["a"], m["sem"], m["banks"], m["keep"]
    UB = UT // P
    with ExitStack() as ctx:
        raw = {w: keep(f"raw_{w}", [P, KB * HC], F32, ctx) for w in "gud"}
        w_hi = {w: keep(f"hi_{w}", [P, KB * HC], F32R, ctx) for w in "gud"}
        w_lo = {w: keep(f"lo_{w}", [P, KB * HC], F32R, ctx) for w in "gud"}
        x_in = [keep(f"unit_x{i}", [P, UB, C], F32, ctx) for i in range(2)]
        x_hi = keep("unit_hi", [P, KB, UT], F32R, ctx)
        x_lo = keep("unit_lo", [P, KB, UT], F32R, ctx)
        act_f = keep("act_f", [P, IB, UT], F32, ctx)
        h_f = keep("h_f", [P, IB, UT], F32, ctx)
        h_hi = keep("unit_h_hi", [P, IB, UT], F32R, ctx)
        h_lo = keep("unit_h_lo", [P, IB, UT], F32R, ctx)
        y_f = [keep(f"y_f{i}", [P, C], F32, ctx) for i in range(UB)]
        tokens = [keep(f"tokens{i}", [P, UB], I32, ctx) for i in range(2)]
        loaded = {w: sem(f"u_loaded_{w}") for w in "gud"}
        hi_r = {w: sem(f"u_hi_{w}") for w in "gud"}
        lo_r = {w: sem(f"u_lo_{w}") for w in "gud"}
        table_in, picked, gathered = sem("u_table"), sem("u_picked"), [sem("u_gathered0"), sem("u_gathered1")]
        x_turned, x_hi_r, x_lo_r = sem("u_turned"), sem("u_x_hi"), sem("u_x_lo")
        g_done, u_done, silu_r, h_r, h_hi_r, h_lo_r = (sem("u_gate"), sem("u_up"), sem("u_silu"), sem("u_h"),
                                                       sem("u_h_hi"), sem("u_h_lo"))
        d_done, y_r, y_stored, y_free = sem("u_down"), sem("u_y"), sem("u_y_stored"), sem("u_y_free")
        ND = 2 * UB
        G, U, TB, DB = banks[0:2], banks[2:4], banks[4:6], banks[6:8]
        block = ctx.enter_context(nc.Block())

        @block.sync
        def _(sp):
            for w in "gud":
                sp.sem_inc(lo_r[w], 1)
            which = ctx.enter_context(sp.register("expert"))

            def load(n, ws):
                sp.reg_load(which, m["unit_expert"][0:1, bass.ds(n, 1)])
                e = sp.snap(which, min_val=0, max_val=NE + NS - 1)
                for w in ws:
                    sp.wait_ge(lo_r[w], n + 1)
                    sp.dma_start(raw[w][:], a["experts"]["gud".index(w), bass.ds(e, 1), :, :].rearrange(
                        "a p c -> (a p) c")).then_inc(loaded[w], 16)

            load(0, "gu")
            with sp.Fori(0, NU - 1) as n:
                load(n + 1, "gu")
                load(n, "d")
            load(NU - 1, "d")

        @block.gpsimd
        def _(pool):
            pool.dma_start(m["slot_table"][:, 0:RCOLS, :].rearrange("p c k -> p (c k)"),
                           m["slots"].rearrange("(p c) k -> p (c k)", p=P)).then_inc(table_in, 16)
            pool.sem_inc(y_free, 1)
            pool.wait_ge(table_in, 16)

            def gather(n, at):
                if not isinstance(n, int) or n >= 2:
                    wait_alone(pool, x_turned, IB * (n - 1), m["passed"])
                pool.tensor_copy(tokens[at][:], m["slot_table"][:, bass.ds(n * UB, UB), 0].bitcast(I32)
                                 ).then_inc(picked, 1)
                wait_alone(pool, picked, n + 1, m["passed"])
                for u in range(UB):
                    pool.indirect_dma_start(x_in[at][:, u, :], None, m["xn2"],
                                            bass.IndirectOffsetOnAxis(ap=tokens[at][:, u:u + 1], axis=0)
                                            ).then_inc(gathered[at], 16)

            def low_down(n):
                pool.wait_ge(hi_r["d"], n + 1)
                pool.tensor_tensor(w_lo["d"][:], raw["d"][:], f32(w_hi["d"][:]), ALU.subtract
                                   ).then_inc(lo_r["d"], 1)

            def allow(n):
                pool.wait_ge(y_stored, 16 * UB * n)
                pool.sem_inc(y_free, 1)

            def store(n):
                for u in range(UB):
                    pool.wait_ge(y_r, 2 + ND * n + 2 * u + 2)
                    pool.dma_start(m["y"][bass.ds(n * UT + u * P, P), :], y_f[u][:]).then_inc(y_stored, 16)

            def step(n, at):
                if not isinstance(n, int) or n + 2 < NU:
                    gather(n + 2, at)
                if not isinstance(n, int) or n >= 2:
                    allow(n - 1)
                low_down(n)
                if not isinstance(n, int) or n >= 1:
                    store(n - 1)

            gather(0, 0)
            gather(1, 1)
            step(0, 0)
            step(1, 1)
            with pool.Fori(1, (NU - 3) // 2) as t:
                step(2 * t, 0)
                step(2 * t + 1, 1)
            for n in range(NU - 3, NU):
                step(n, n % 2)
            allow(NU - 1)
            store(NU - 1)
            pool.wait_ge(y_stored, 16 * UB * NU)

        @block.tensor
        def _(pe):
            pe.sem_inc(d_done, 1)

            def turn(n, at, turns, qs=range(IB)):
                pe.wait_ge(gathered[at], 16 * UB * turns)
                for q in qs:
                    pe.wait_ge(x_lo_r, IB * n + (2 if q == 2 else 1))
                    for b in range(2):
                        for u in range(UB):
                            c = b * UT + u * P
                            last = pe.transpose(TB[q % 2][:, c:c + P],
                                                x_in[at][:, u, (2 * q + b) * P:(2 * q + b + 1) * P], m["ident"][:])
                    last.then_inc(x_turned, 1)

            def into(n, w, bank, done, read):
                pe.wait_ge(lo_r[w], 1 + n + 1)
                pe.wait_ge(read, 2 * n + 1)
                for i in range(IB):
                    for k in range(KB):
                        c = k * HC + i * P
                        last = three_products(pe, bank[i // 2][:, i % 2 * UT:(i % 2 + 1) * UT],
                                              w_hi[w][:, c:c + P], w_lo[w][:, c:c + P],
                                              x_hi[:, k, :], x_lo[:, k, :], k, KB)
                    if i:
                        last.then_inc(done, 1)

            def down(n, qs=range(ND)):
                if 0 in qs:
                    pe.wait_ge(lo_r["d"], 1 + n + 1)
                    pe.wait_ge(h_lo_r, n + 1)
                for q in qs:
                    u, h = q // 2, q % 2
                    pe.wait_ge(y_r, ND * n + q + 1)
                    for i in range(IB):
                        c = i * C + h * HC
                        last = three_products(pe, DB[q % 2][:, 0:HC], h_hi[:, i, u * P:(u + 1) * P],
                                              h_lo[:, i, u * P:(u + 1) * P], w_hi["d"][:, c:c + HC],
                                              w_lo["d"][:, c:c + HC], i, IB)
                    last.then_inc(d_done, 1)

            def gate_up(n):
                pe.wait_ge(x_lo_r, 1 + IB * (n + 1))
                into(n, "g", G, g_done, silu_r)
                into(n, "u", U, u_done, h_r)

            turn(0, 0, 1)
            gate_up(0)
            turn(1, 1, 1)
            with pe.Fori(0, (NU - 3) // 2) as t:
                for v in range(2):
                    n = 2 * t + 1 + v
                    gate_up(n)
                    turn(n + 1, v, t + 2, [0, 1])
                    down(n - 1, [0])
                    turn(n + 1, v, t + 2, [2])
                    down(n - 1, range(1, ND))
            gate_up(NU - 2)
            turn(NU - 1, 0, NU // 2 + 1)
            down(NU - 3)
            gate_up(NU - 1)
            down(NU - 2)
            down(NU - 1)

        @block.scalar
        def _(act):
            act.sem_inc(silu_r, 1)

            def high(w, n, used=None):
                act.wait_ge(loaded[w], 16 * (n + 1))
                if used is not None:
                    act.wait_ge(*used)
                act.activation(w_hi[w][:], raw[w][:], ACT.Copy).then_inc(hi_r[w], 1)

            def x_high(n):
                for q in range(IB):
                    act.wait_ge(x_turned, IB * n + q + 1)
                    act.activation(x_hi[:, 2 * q:2 * q + 2, :], TB[q % 2][:].rearrange("p (b t) -> p b t", b=2),
                                   ACT.Copy).then_inc(x_hi_r, 1)

            def silu(n):
                act.wait_ge(h_r, 2 * n + 1)
                act.wait_ge(g_done, 2 * n + 1)
                act.activation(act_f[:, 0:2, :].rearrange("p i t -> p (i t)"), G[0][:], ACT.Silu
                               ).then_inc(silu_r, 1)
                act.wait_ge(g_done, 2 * n + 2)
                act.activation(act_f[:, 2, :], G[1][:, 0:UT], ACT.Silu).then_inc(silu_r, 1)

            def h_high(n):
                act.wait_ge(d_done, ND * n + 1)
                act.wait_ge(h_r, 1 + 2 * n + 2)
                act.activation(h_hi[:], h_f[:], ACT.Copy).then_inc(h_hi_r, 1)
                high("d", n)

            high("g", 0)
            high("u", 0)
            x_high(0)
            with act.Fori(0, NU - 1) as n:
                silu(n)
                high("g", n + 1, (g_done, 2 * n + 2))
                act.wait_ge(u_done, 2 * n + 2)
                x_high(n + 1)
                high("u", n + 1)
                h_high(n)
            silu(NU - 1)
            h_high(NU - 1)

        @block.vector
        def _(dve):
            dve.sem_inc(x_lo_r, 1)
            dve.sem_inc(h_r, 1)
            dve.sem_inc(y_r, 2)

            def low(w, n):
                dve.wait_ge(hi_r[w], n + 1)
                dve.tensor_tensor(w_lo[w][:], raw[w][:], f32(w_hi[w][:]), ALU.subtract).then_inc(lo_r[w], 1)

            def x_low(n):
                for q in range(IB):
                    dve.wait_ge(x_hi_r, IB * n + q + 1)
                    dve.tensor_tensor(x_lo[:, 2 * q:2 * q + 2, :], TB[q % 2][:].rearrange(
                        "p (b t) -> p b t", b=2), f32(x_hi[:, 2 * q:2 * q + 2, :]), ALU.subtract
                        ).then_inc(x_lo_r, 1)

            def hidden(n):
                dve.wait_ge(silu_r, 1 + 2 * n + 2)
                dve.wait_ge(u_done, 2 * n + 1)
                if not isinstance(n, int) or n:
                    dve.wait_ge(h_lo_r, n)
                dve.tensor_tensor(h_f[:, 0:2, :].rearrange("p i t -> p (i t)"), act_f[:, 0:2, :].rearrange(
                    "p i t -> p (i t)"), U[0][:], ALU.mult).then_inc(h_r, 1)
                dve.wait_ge(u_done, 2 * n + 2)
                dve.tensor_tensor(h_f[:, 2, :], act_f[:, 2, :], U[1][:, 0:UT], ALU.mult).then_inc(h_r, 1)

            def h_low(n):
                dve.wait_ge(h_hi_r, n + 1)
                dve.tensor_tensor(h_lo[:], h_f[:], f32(h_hi[:]), ALU.subtract).then_inc(h_lo_r, 1)

            def y_rows(n, qs):
                for q in qs:
                    u, h = q // 2, q % 2
                    if q == 0:
                        dve.wait_ge(y_free, n + 1)
                    dve.wait_ge(d_done, 1 + ND * n + q + 1)
                    dve.tensor_scalar(y_f[u][:, h * HC:(h + 1) * HC], DB[q % 2][:, 0:HC],
                                      m["slot_table"][:, bass.ds(n * UB + u, 1), 1], None, ALU.mult
                                      ).then_inc(y_r, 1)

            def body(n, behind):
                low("g", n + 1)
                hidden(n)
                x_low(n + 1)
                if behind:
                    y_rows(n - 1, range(ND))
                low("u", n + 1)
                h_low(n)

            low("g", 0)
            low("u", 0)
            x_low(0)
            dve.wait_ge(table_in, 16)
            body(0, False)
            with dve.Fori(1, NU - 1) as n:
                body(n, True)
            hidden(NU - 1)
            y_rows(NU - 2, range(ND))
            h_low(NU - 1)
            y_rows(NU - 1, range(ND))


def combine(nc, m):
    sem, keep, x1, out = m["sem"], m["keep"], m["x1"], m["out"]
    NBUF = 3
    with ExitStack() as ctx:
        rows = [keep(f"rows{i}", [TP, TOPK + NS, C], F32, ctx) for i in range(NBUF)]
        loaded, gathered = [sem(f"c_loaded{i}") for i in range(NBUF)], [sem(f"c_gathered{i}") for i in range(NBUF)]
        shared_r, chosen_r, done, stored = sem("c_shared"), sem("c_chosen"), sem("c_done"), sem("c_stored")
        block = ctx.enter_context(nc.Block())

        @block.sync
        def _(sp):
            for i in range(NT):
                if i >= NBUF:
                    sp.wait_ge(shared_r, 1 + i - NBUF)
                    sp.wait_ge(done, 1 + i - NBUF)
                for e in range(NS):
                    first = (NR + e * SU) * UT + i * TP
                    sp.dma_start(rows[i % NBUF][:, TOPK + e, :], m["y"][first:first + TP, :]
                                 ).then_inc(loaded[i % NBUF], 16)

        @block.scalar
        def _(act):
            for i in range(NT):
                act.wait_ge(done, i + 1)
                act.dma_start(out[i * TP:(i + 1) * TP, :], x1[:, i, :]).then_inc(stored, 16)
            act.wait_ge(stored, 16 * NT)

        @block.gpsimd
        def _(pool):
            def shared(i):
                r = rows[i % NBUF]
                pool.wait_ge(loaded[i % NBUF], 16 * NS * (i // NBUF + 1))
                pool.tensor_tensor(r[:, TOPK, :], r[:, TOPK, :], r[:, TOPK + 1, :], ALU.add).then_inc(shared_r, 1)

            for i in range(NT):
                if i >= NBUF:
                    pool.wait_ge(done, 1 + i - NBUF)
                for k in range(TOPK):
                    pool.indirect_dma_start(rows[i % NBUF][:, k, :], None, m["y"], bass.IndirectOffsetOnAxis(
                        ap=m["slot_of"][:, TOPK * i + k:TOPK * i + k + 1], axis=0)).then_inc(gathered[i % NBUF], 16)
                if i:
                    shared(i - 1)
            shared(NT - 1)

        @block.vector
        def _(dve):
            for i in range(NT):
                r = rows[i % NBUF]
                dve.wait_ge(gathered[i % NBUF], 16 * TOPK * (i // NBUF + 1))
                for k in range(TOPK):
                    dve.tensor_tensor(r[:, 0, :], r[:, 0, :], r[:, 1, :] if k else x1[:, i, :],
                                      ALU.add).then_inc(chosen_r, 1)
                    dve.wait_ge(chosen_r, TOPK * i + k + 1)
                dve.wait_ge(shared_r, i + 1)
                dve.tensor_tensor(x1[:, i, :], r[:, 0, :], r[:, TOPK, :], ALU.add).then_inc(done, 1)


def kernel(x, src, dst, L0_gnn_W, L0_gnn_b, L0_mix_w_qkv, L0_mix_w_proj, L0_mix_b_proj, L0_mix_proj_mat,
           L0_ffn_gate_w, L0_ffn_shared_gate, L0_ffn_shared_up, L0_ffn_shared_down, L0_ffn_routed_gate,
           L0_ffn_routed_up, L0_ffn_routed_down):
    import numpy as np
    import concourse.bacc as bacc
    from concourse.bass_utils import run_bass_kernel_spmd

    def flat(w):
        n, c = w.shape[-2] // P, w.shape[-1]
        w = w.reshape(*w.shape[:-2], n, P, c)
        return np.swapaxes(w, -3, -2).reshape(*w.shape[:-3], P, n * c)

    def halves(w):
        return [flat(w[:, :HC]), flat(w[:, HC:])]

    arr = np.asarray
    qkv_t = arr(L0_mix_w_qkv).T
    pieces = []
    for w in (arr(L0_gnn_W), qkv_t[:, 2 * C:], qkv_t[:, :C], qkv_t[:, C:2 * C], arr(L0_mix_w_proj).T):
        pieces += halves(w)
    into = [np.concatenate([arr(r), arr(s)]).transpose(0, 2, 1)
            for r, s in ((L0_ffn_routed_gate, L0_ffn_shared_gate), (L0_ffn_routed_up, L0_ffn_shared_up))]
    down = np.concatenate([arr(L0_ffn_routed_down), arr(L0_ffn_shared_down)]).transpose(0, 2, 1)
    arrays = {
        "x": arr(x), "src": arr(src), "dst": arr(dst), "w_pieces": np.stack(pieces),
        "gnn_b": arr(L0_gnn_b), "b_proj": arr(L0_mix_b_proj), "proj_t": arr(L0_mix_proj_mat).T,
        "gate_t": arr(L0_ffn_gate_w).T, "experts": np.stack([flat(into[0]), flat(into[1]), flat(down)]),
    }
    arrays = {"in_" + k: np.ascontiguousarray(v) for k, v in arrays.items()}
    nc = bacc.Bacc("TRN2", target_bir_lowering=False, num_devices=1)
    a = {k[3:]: nc.dram_tensor(k, v.shape, mybir.dt.from_np(v.dtype), kind="ExternalInput").ap()
         for k, v in arrays.items()}
    out = nc.dram_tensor("out", (T, C), F32, kind="ExternalOutput").ap()
    program(nc, a, out)
    return run_bass_kernel_spmd(nc, [arrays], core_ids=[0]).results[0]["out"]
```

```python
from contextlib import ExitStack

import concourse.bass as bass
from concourse import mybir

F32, F32R = mybir.dt.float32, mybir.dt.float32r
BF16, I32, I16, U32 = mybir.dt.bfloat16, mybir.dt.int32, mybir.dt.int16, mybir.dt.uint32
ALU = mybir.AluOpType
ACT = mybir.ActivationFunctionType
X = mybir.AxisListType.X

T, C = 1250, 768
P = 128
NT, TP = 10, 125
KB = C // P
HC = C // 2
CH = 418
CHUNKS = [(c, min(CH, T - c)) for c in range(0, T, CH)]
CHUNK_AT = [c for c, _ in CHUNKS]
LN_EPS = 1e-5

E_EDGES = 20000
EJ = E_EDGES // TP
NG = NT * len(CHUNKS)
EPAD = 512
NBATCH = (E_EDGES + NG * (EPAD - 1)) // EPAD
NBATCH += -NBATCH % 4
ECOLS = NBATCH * EPAD // P
SCAT = 8

H, D, M = 12, 64, 256
HP = H // 2
DV = D + 2
NORM = float(D) ** -0.25
DIAG = 0.5 * float(D) ** -0.5
FEPS = 1e-4

NE, NS, I = 8, 2, 384
IB = I // P
TOPK = 2
UT = 256
NR = (T * TOPK + NE * (UT - 1)) // UT
SU = -(-T // UT)
NU = NR + NS * SU
UCOLS = NU * UT // P
RCOLS = NR * UT // P
SCOLS = NS * SU * UT // P
TJ = NT * TOPK


def f32(ap):
    return ap.bitcast(F32)


class Chain:

    def __init__(self, sem):
        self.eng, self.sem, self.n = None, sem, 0

    def on(self, eng):
        self.eng = eng
        return self

    def __call__(self, ins):
        self.n += 1
        ins.then_inc(self.sem, 1)
        self.eng.wait_ge(self.sem, self.n)


def wait_alone(eng, sem, value, passed):
    eng.wait_ge(sem, value)
    eng.sem_inc(passed, 1)


def refine_rsqrt(dve, own, r, v, work):
    own(dve.tensor_tensor(work, r, r, ALU.mult))
    own(dve.tensor_tensor(work, work, v, ALU.mult))
    own(dve.tensor_scalar(work, work, -0.5, 1.5, ALU.mult, ALU.add))
    return dve.tensor_tensor(r, r, work, ALU.mult)


def three_products(pe, out, a_hi, a_lo, b_hi, b_lo, k, n):
    pe.matmul(out, a_hi, b_hi, start=(k == 0), stop=False)
    pe.matmul(out, a_hi, b_lo, start=False, stop=False)
    return pe.matmul(out, a_lo, b_hi, start=False, stop=(k == n - 1))


def program(nc, a, out):
    with ExitStack() as whole:
        live, done = [], []

        def sem(name):
            live.append(nc.alloc_semaphore(name))
            return live[-1]

        def next_phase():
            done.extend(live)
            live.clear()

        def recycle():
            nc.clear_and_free_semaphores(done)
            done.clear()

        def keep(name, shape, dtype, where=whole):
            return where.enter_context(nc.sbuf_tensor(name, shape, dtype))

        def dram(name, shape, dtype=F32):
            return nc.dram_tensor(name, shape, dtype, kind="Internal").ap()

        m = {
            "a": a, "out": out, "sem": sem, "keep": keep,
            "banks": [whole.enter_context(nc.psum_tensor(f"bank{i}", [P, 512], F32)) for i in range(8)],
            "ident": keep("ident", [P, P], F32),
            "before": keep("before", [P, P], F32),
            "ones": keep("ones", [P, P], F32),
            "batch_group": keep("batch_group", [1, NBATCH], I32),
            "passed": nc.alloc_semaphore("passed"),
            "own": Chain(nc.alloc_semaphore("dve_own")),
            "recycle": recycle,
            "hv": dram("hv", [2, T, C]),
            "qk": dram("qk", [2, C, T]),
            "edges": dram("edges", [P * ECOLS, 2]),
            "xn2": dram("xn2", [T, C]),
            "slots": dram("slots", [P * RCOLS, 2]),
            "att_raw": dram("att_raw", [H, DV, T]),
            "inverse": dram("inverse", [H, T]),
            "y": dram("y", [NU * UT, C]),
        }
        with ExitStack() as early:
            m["xn_hi"] = keep("xn_hi", [P, KB, T], F32R, early)
            m["xn_lo"] = keep("xn_lo", [P, KB, T], F32R, early)
            for name, dtype in (("raw", F32), ("w_hi", F32R), ("w_lo", F32R)):
                m[name] = [keep(f"{name}{i}", [P, KB, HC], dtype, early) for i in range(2)]
            first_norm(nc, m)
            next_phase()
            projections(nc, m)
            next_phase()
        m["x1"] = keep("x1", [TP, NT, C], F32)
        graph(nc, m)
        next_phase()
        m["slot_table"] = keep("slot_table", [P, UCOLS, 2], F32)
        m["slot_of"] = keep("slot_of", [TP, TJ], I32)
        m["unit_expert"] = keep("unit_expert", [1, NU], I32)
        m["logits"] = keep("logits", [TP, NT, NE], F32)
        m["staging"] = keep("staging", [P, KB * HC], F32)
        m["staged"] = nc.alloc_semaphore("staged")
        with ExitStack() as mid:
            m["ctx"] = keep("ctx", [P, H, 2, DV], F32, mid)
            m["proj_hi"] = keep("proj_hi", [P, 2, M], F32R, mid)
            m["proj_lo"] = keep("proj_lo", [P, 2, M], F32R, mid)
            m["head_mask"] = keep("head_mask", [P, 2], F32, mid)
            keys(nc, m)
            next_phase()
            m["att_hi"] = keep("att_hi", [P, HP, T], F32R, mid)
            m["att_lo"] = keep("att_lo", [P, HP, T], F32R, mid)
            queries(nc, m)
            next_phase()
            mix(nc, m)
            next_phase()
        experts(nc, m)
        next_phase()
        combine(nc, m)


def first_norm(nc, m):
    a, sem, banks, ident = m["a"], m["sem"], m["banks"], m["ident"]
    with ExitStack() as ctx:
        x_in = m["keep"]("x_in", [TP, NT, C], F32, ctx)
        stats = m["keep"]("stats", [TP, NT, 2, 6], F32, ctx)
        mean_var = m["keep"]("mean_var", [TP, NT, 2], F32, ctx)
        spread = m["keep"]("spread", [TP, NT], F32, ctx)
        rstd = m["keep"]("rstd", [TP, NT], F32, ctx)
        work = m["keep"]("newton", [TP, NT], F32, ctx)
        zeros = m["keep"]("zeros", [P, RCOLS * 2], F32, ctx)
        filler = m["keep"]("filler", [P, ECOLS * 2], F32, ctx)
        x_loaded = [sem(f"x_loaded{i}") for i in range(NT // 2)]
        consts = sem("consts")
        var_ready, sd_ready, xn_ready = sem("var_ready"), sem("sd_ready"), sem("xn_ready")
        turned, hi_done, lo_done, filled = sem("turned"), sem("n1_hi"), sem("n1_lo"), sem("filled")
        w_loaded, w_high = [sem("n1_w_loaded0"), sem("n1_w_loaded1")], sem("n1_w_hi")
        NB = 4
        block = ctx.enter_context(nc.Block())

        @block.sync
        def _(sp):
            for i in range(0, NT, 2):
                sp.dma_start(x_in[:, i:i + 2, :], a["x"][i * TP:(i + 2) * TP, :].rearrange("(i p) c -> p i c", p=TP)
                             ).then_inc(x_loaded[i // 2], 16)
            for n in range(2):
                sp.dma_start(m["raw"][n][:], a["w_pieces"][n].rearrange("p (k c) -> p k c", k=KB)
                             ).then_inc(w_loaded[n], 16)
            sp.wait_ge(consts, 4)
            sp.dma_start(m["edges"].rearrange("(p c) k -> p (c k)", p=P), filler[:]).then_inc(filled, 16)
            sp.wait_ge(consts, 5)
            sp.dma_start(m["slots"].rearrange("(p c) k -> p (c k)", p=P),
                         zeros[:]).then_inc(filled, 16)
            sp.wait_ge(filled, 32)

        @block.gpsimd
        def _(pool):
            pool.memset(m["ones"][:], 1.0).then_inc(consts, 1)
            pool.wait_ge(consts, 1)
            pool.affine_select(out=ident[:], in_=m["ones"][:], compare_op=ALU.is_equal, fill=0.0, base=0,
                               pattern=[[-1, P]], channel_multiplier=1).then_inc(consts, 1)
            pool.affine_select(out=m["before"][:], in_=m["ones"][:], compare_op=ALU.is_gt, fill=0.0, base=0,
                               pattern=[[1, P]], channel_multiplier=-1).then_inc(consts, 1)
            pool.memset(filler[:], -1.0).then_inc(consts, 1)
            pool.memset(zeros[:], 0.0).then_inc(consts, 1)
            for n in range(2):
                pool.wait_ge(w_high, n + 1)
                pool.tensor_tensor(m["w_lo"][n][:], m["raw"][n][:], f32(m["w_hi"][n][:]), ALU.subtract)

        @block.vector
        def _(dve):
            own = m["own"].on(dve)
            for i in range(NT):
                dve.wait_ge(x_loaded[i // 2], 16)
                for h in range(2):
                    last = dve.bn_stats(stats[:, i, h, :], x_in[:, i, h * HC:(h + 1) * HC])
            own(last)
            for i in range(NT):
                last = dve.bn_aggr(mean_var[:, i, :], stats[:, i, :, :])
            own(last)
            dve.tensor_scalar(spread[:], mean_var[:, :, 1], LN_EPS, None, ALU.add).then_inc(var_ready, 1)
            dve.wait_ge(sd_ready, 1)
            own(dve.reciprocal(rstd[:], rstd[:]))
            own(refine_rsqrt(dve, own, rstd[:], spread[:], work[:]))

            def lows(n):
                dve.wait_ge(hi_done, n + 1)
                i, h = n // 2, n % 2
                at = (slice(None), slice(3 * h, 3 * h + 3), slice(i * TP, (i + 1) * TP))
                dve.tensor_tensor(m["xn_lo"][at], banks[n % NB][:, 0:3 * TP].rearrange("p (b t) -> p b t", b=3),
                                  f32(m["xn_hi"][at]), ALU.subtract).then_inc(lo_done, 1)

            for i in range(NT):
                dve.tensor_scalar(x_in[:, i, :], x_in[:, i, :], mean_var[:, i, 0:1], rstd[:, i:i + 1],
                                  ALU.subtract, ALU.mult).then_inc(xn_ready, 1)
                if i:
                    lows(2 * i - 2)
                    lows(2 * i - 1)
            lows(2 * NT - 2)
            lows(2 * NT - 1)

        @block.scalar
        def _(act):
            act.wait_ge(var_ready, 1)
            act.activation(rstd[:], spread[:], ACT.Sqrt).then_inc(sd_ready, 1)
            for n in range(2 * NT):
                i, h = n // 2, n % 2
                act.wait_ge(turned, n + 1)
                act.activation(m["xn_hi"][:, 3 * h:3 * h + 3, i * TP:(i + 1) * TP],
                               banks[n % NB][:, 0:3 * TP].rearrange("p (b t) -> p b t", b=3),
                               ACT.Copy).then_inc(hi_done, 1)
                if n in (3, 7):
                    act.wait_ge(w_loaded[n // 4], 16)
                    act.activation(m["w_hi"][n // 4][:], m["raw"][n // 4][:], ACT.Copy).then_inc(w_high, 1)

        @block.tensor
        def _(pe):
            pe.wait_ge(consts, 3)
            for n in range(2 * NT):
                i, h = n // 2, n % 2
                pe.wait_ge(xn_ready, i + 1)
                if n >= NB:
                    pe.wait_ge(lo_done, n - NB + 1)
                for b in range(3):
                    k = 3 * h + b
                    last = pe.transpose(banks[n % NB][:, b * TP:(b + 1) * TP],
                                        x_in[:, i, k * P:(k + 1) * P], ident[0:TP, 0:TP])
                last.then_inc(turned, 1)


def rank_items(dve, own, pe_ready, s, group, groups, per):
    shape = [TP, groups, per]
    own(dve.tensor_tensor(s["hot"], group.unsqueeze(1).broadcast_to(shape),
                          s["iota"].unsqueeze(2).broadcast_to(shape), ALU.is_equal))
    flat = "p g j -> p (g j)"
    own(dve.tensor_tensor_scan(s["rank"].rearrange(flat), s["keep_on"].rearrange(flat),
                               s["hot"].rearrange(flat), 0.0, ALU.mult, ALU.add))
    dve.tensor_copy(s["total"], s["rank"][:, :, per - 1]).then_inc(pe_ready, 1)


def place_items(dve, own, s, groups, per, pad):
    shape = [TP, groups, per]
    own(dve.tensor_scalar(s["count"], s["sums"][:, groups:2 * groups], float(pad - 1), None, ALU.add))
    own(dve.tensor_scalar(s["count"], s["count"], pad.bit_length() - 1, None, ALU.logical_shift_right))
    own(dve.tensor_copy(s["batches"], s["count"]))
    own(dve.tensor_tensor_scan(s["upto"], s["ones"], s["batches"], 0.0, ALU.mult, ALU.add))
    own(dve.tensor_tensor(s["base"], s["upto"], s["batches"], ALU.subtract))
    own(dve.tensor_scalar(s["base"], s["base"], float(pad), -1.0, ALU.mult, ALU.add))
    own(dve.tensor_tensor(s["base"], s["sums"][:, 0:groups], s["base"], ALU.add))
    own(dve.tensor_tensor(s["wide"], s["rank"], s["base"].unsqueeze(2).broadcast_to(shape), ALU.add))
    own(dve.tensor_tensor(s["wide"], s["wide"], s["hot"], ALU.mult))
    own(dve.tensor_reduce(s["slot"], s["wide"].rearrange("p g j -> p j g"), X, ALU.add))


def table_rows(dve, own, s, cols):
    own(dve.tensor_copy(s["slot_i"], s["slot"]))
    own(dve.tensor_scalar(s["part"], s["slot_i"], P - 1, None, ALU.bitwise_and))
    own(dve.tensor_scalar(s["col"], s["slot_i"], P.bit_length() - 1, None, ALU.logical_shift_right))
    return dve.scalar_tensor_tensor(s["row"], s["part"], float(cols), s["col"], ALU.mult, ALU.add)


def slot_buffers(m, ctx, name, groups, per, wide):
    k = m["keep"]
    s = {
        "iota": k(name + "_iota", [TP, groups], F32, ctx)[:],
        "hot": k(name + "_hot", [TP, groups, per], BF16, ctx)[:],
        "keep_on": k(name + "_keep_on", [TP, groups, per], BF16, ctx)[:],
        "rank": k(name + "_rank", [TP, groups, per], BF16, ctx)[:],
        "wide": wide,
        "ones": m["ones"][0:TP, 0:groups],
    }
    for n in ("total", "batches", "upto", "base"):
        s[n] = k(f"{name}_{n}", [TP, groups], F32, ctx)[:]
    s["count"] = k(name + "_count", [TP, groups], I32, ctx)[:]
    s["slot"] = k(name + "_slot", [TP, per], F32, ctx)[:]
    for n in ("slot_i", "part", "col", "row"):
        s[n] = k(f"{name}_{n}", [TP, per], I32, ctx)[:]
    return s


def projections(nc, m):
    a, sem, banks = m["a"], m["sem"], m["banks"]
    keep = m["keep"]
    NPIECE = 8
    NB = 6
    with ExitStack() as ctx:
        raw, w_hi, w_lo = m["raw"], m["w_hi"], m["w_lo"]
        stage = [keep(f"stage{i}", [P, NT * HC], F32, ctx) for i in range(2)]
        src_i = keep("src_i", [TP, EJ], I32, ctx)
        dst_i = keep("dst_i", [TP, EJ], I32, ctx)
        src_f = keep("src_f", [TP, EJ], F32, ctx)
        dst_f = keep("dst_f", [TP, EJ], F32, ctx)
        tile_f = keep("tile_f", [TP, EJ], F32, ctx)
        chunk_f = keep("chunk_f", [TP, EJ], F32, ctx)
        group = keep("group", [TP, EJ], F32, ctx)
        pair = keep("pair", [TP, EJ, 2], F32, ctx)
        wide = keep("wide", [TP, NG, EJ], F32, ctx)
        s = slot_buffers(m, ctx, "edge", NG, EJ, wide[:])
        s["sums"] = banks[7][0:TP, 0:2 * NG]
        batch_iota = keep("batch_iota", [1, NBATCH], F32, ctx)
        set_row = [keep(f"set_row{i}", [TP, SCAT], I32, ctx) for i in range(2)]
        set_pair = [keep(f"set_pair{i}", [TP, SCAT, 2], F32, ctx) for i in range(2)]

        w_loaded, stored = [sem("w_loaded0"), sem("w_loaded1")], [sem("stored0"), sem("stored1")]
        hi_ready, lo_ready = sem("w_hi"), sem("w_lo")
        product, evacuated = sem("product"), sem("evacuated")
        e_loaded, e_const = sem("e_loaded"), sem("e_const")
        totals_ready, sums_ready, rows_ready = sem("totals_ready"), sem("sums_ready"), sem("rows_ready")
        set_filled, scattered = sem("set_filled"), [sem("scattered0"), sem("scattered1")]

        def groups_upto(n):
            return NT * min(n, 4) + KB // 2 * len(CHUNKS) * max(n - 4, 0)

        def bank_of(n, j):
            return (n * NT + j) % NB if n < 4 else (4 * NT + n % 2 * 9 + j) % NB

        block = ctx.enter_context(nc.Block())

        @block.sync
        def _(sp):
            sp.dma_start(src_i[:], a["src"].rearrange("(p j) -> p j", p=TP)).then_inc(e_loaded, 16)
            sp.dma_start(dst_i[:], a["dst"].rearrange("(p j) -> p j", p=TP)).then_inc(e_loaded, 16)
            for n in range(2, NPIECE + 2):
                if n < NPIECE:
                    if n >= 4:
                        sp.wait_ge(lo_ready, n - 3)
                    sp.dma_start(raw[n % 2][:], a["w_pieces"][n].rearrange("p (k c) -> p k c", k=KB)
                                 ).then_inc(w_loaded[n % 2], 16)
                q = n - 2
                sp.wait_ge(evacuated, NB + groups_upto(q + 1))
                half = slice((q % 2) * HC, (q % 2 + 1) * HC)
                if q < 4:
                    sp.dma_start(m["hv"][q // 2, :, half].rearrange("(i p) c -> p i c", p=TP),
                                 stage[q % 2][0:TP, :].rearrange("p (i c) -> p i c", i=NT)
                                 ).then_inc(stored[q % 2], 16)
                else:
                    sp.dma_start(m["qk"][q // 2 - 2, half, :].rearrange("(b p) t -> p b t", p=P),
                                 stage[q % 2][:, 0:3 * T].rearrange("p (b t) -> p b t", b=3)
                                 ).then_inc(stored[q % 2], 16)
            for done in stored:
                sp.wait_ge(done, 8 * NPIECE)

        @block.tensor
        def _(pe):
            def piece(n, at, kind):
                if not isinstance(n, int) or n >= 2:
                    pe.wait_ge(lo_ready, n - 1)
                if kind == "tokens":
                    for i in range(NT):
                        g = n * NT + i
                        pe.wait_ge(evacuated, g + 1)
                        bank = banks[bank_of(n, i)]
                        for k in range(KB):
                            last = three_products(
                                pe, bank[0:TP, 0:HC], m["xn_hi"][:, k, i * TP:(i + 1) * TP],
                                m["xn_lo"][:, k, i * TP:(i + 1) * TP], w_hi[at][:, k, :], w_lo[at][:, k, :], k, KB)
                        last.then_inc(product, 1)
                        if isinstance(n, int) and n * NT + i == 7:
                            group_sums()
                else:
                    for b in range(3):
                        for c, (c0, cn) in enumerate(CHUNKS):
                            j = 3 * b + c
                            pe.wait_ge(evacuated, n * 9 + 4 + j + 1)
                            bank = banks[bank_of(4 + at, j)]
                            for k in range(KB):
                                last = three_products(
                                    pe, bank[:, 0:cn], w_hi[at][:, k, b * P:(b + 1) * P],
                                    w_lo[at][:, k, b * P:(b + 1) * P], m["xn_hi"][:, k, c0:c0 + cn],
                                    m["xn_lo"][:, k, c0:c0 + cn], k, KB)
                            last.then_inc(product, 1)

            def group_sums():
                pe.wait_ge(totals_ready, 1)
                pe.matmul(s["sums"][:, 0:NG], m["before"][0:TP, 0:TP], s["total"], start=True, stop=True)
                pe.matmul(s["sums"][:, NG:2 * NG], m["ones"][0:TP, 0:TP], s["total"], start=True,
                          stop=True).then_inc(sums_ready, 1)

            piece(0, 0, "tokens")
            piece(1, 1, "tokens")
            piece(2, 0, "tokens")
            piece(3, 1, "tokens")
            with pe.Fori(4, 8, 2) as n:
                piece(n, 0, "features")
                piece(n + 1, 1, "features")

        @block.scalar
        def _(act):
            def high(n):
                act.wait_ge(w_loaded[n % 2], 16 * (n // 2))
                act.activation(w_hi[n % 2][:], raw[n % 2][:], ACT.Copy).then_inc(hi_ready, 1)

            act.sem_inc(evacuated, NB)
            g = 0
            for n in range(NPIECE):
                if n >= 2:
                    act.wait_ge(stored[n % 2], 16 * (n // 2))
                if n < 4:
                    for i in range(NT):
                        act.wait_ge(product, g + 1)
                        act.activation(stage[n % 2][0:TP, i * HC:(i + 1) * HC], banks[bank_of(n, i)][0:TP, 0:HC],
                                       ACT.Copy).then_inc(evacuated, 1)
                        g += 1
                else:
                    for j in range(9):
                        b, (c0, cn) = j // 3, CHUNKS[j % 3]
                        act.wait_ge(product, g + 1)
                        act.activation(stage[n % 2][:, b * T + c0:b * T + c0 + cn],
                                       banks[bank_of(n, j)][:, 0:cn], ACT.Copy).then_inc(evacuated, 1)
                        g += 1
                if n + 2 < NPIECE:
                    high(n + 2)

        @block.vector
        def _(dve):
            own = m["own"].on(dve)

            def low(n):
                dve.wait_ge(hi_ready, n - 1)
                dve.tensor_tensor(w_lo[n % 2][:], raw[n % 2][:], f32(w_hi[n % 2][:]),
                                  ALU.subtract).then_inc(lo_ready, 1)

            dve.wait_ge(e_loaded, 32)
            dve.tensor_copy(src_f[:], src_i[:])
            own(dve.tensor_copy(dst_f[:], dst_i[:]))
            own(dve.tensor_scalar(tile_f[:], src_f[:], float(TP), None, ALU.is_ge))
            own(dve.tensor_scalar(chunk_f[:], dst_f[:], float(CHUNK_AT[1]), None, ALU.is_ge))
            for i in range(2, NT):
                own(dve.scalar_tensor_tensor(tile_f[:], src_f[:], float(i * TP), tile_f[:], ALU.is_ge, ALU.add))
            own(dve.scalar_tensor_tensor(dst_f[:], chunk_f[:], -float(CHUNK_AT[1]), dst_f[:], ALU.mult, ALU.add))
            own(dve.tensor_scalar(group[:], dst_f[:], float(CHUNK_AT[2] - CHUNK_AT[1]), None, ALU.is_ge))
            own(dve.tensor_tensor(group[:], group[:], chunk_f[:], ALU.mult))
            own(dve.tensor_tensor(chunk_f[:], chunk_f[:], group[:], ALU.add))
            own(dve.scalar_tensor_tensor(pair[:, :, 1], group[:], -float(CHUNK_AT[2] - CHUNK_AT[1]), dst_f[:],
                                         ALU.mult, ALU.add))
            dve.scalar_tensor_tensor(pair[:, :, 0], tile_f[:], -float(TP), src_f[:], ALU.mult, ALU.add)
            own(dve.scalar_tensor_tensor(group[:], tile_f[:], float(len(CHUNKS)), chunk_f[:], ALU.mult, ALU.add))
            dve.wait_ge(e_const, 4)
            rank_items(dve, own, totals_ready, s, group[:], NG, EJ)
            dve.wait_ge(sums_ready, 1)
            place_items(dve, own, s, NG, EJ, EPAD)
            table_rows(dve, own, s, ECOLS).then_inc(rows_ready, 1)
            first = wide[0:1, 0:NG, 0:NBATCH]
            own(dve.tensor_tensor(first, batch_iota[:].unsqueeze(1).broadcast_to([1, NG, NBATCH]),
                                  s["upto"][0:1, :].unsqueeze(2).broadcast_to([1, NG, NBATCH]), ALU.is_ge))
            own(dve.tensor_reduce(batch_iota[:], first.rearrange("p g j -> p j g"), X, ALU.add))
            own(dve.tensor_scalar(m["batch_group"][:], batch_iota[:], float(NG - 1), None, ALU.min))
            for n in range(2, NPIECE):
                low(n)

        @block.gpsimd
        def _(pool):
            pool.iota(s["iota"], [[1, NG]], base=0, channel_multiplier=0,
                      allow_small_or_imprecise_dtypes=True).then_inc(e_const, 1)
            pool.iota(batch_iota[:], [[1, NBATCH]], base=0, channel_multiplier=0,
                      allow_small_or_imprecise_dtypes=True).then_inc(e_const, 1)
            pool.memset(s["keep_on"], 1.0).then_inc(e_const, 1)
            pool.wait_ge(e_const, 3)
            pool.memset(s["keep_on"][:, :, 0:1], 0.0).then_inc(e_const, 1)

            def send(n, at, turn):
                if turn is not None:
                    wait_alone(pool, scattered[at], 16 * SCAT * turn, m["passed"])
                pool.tensor_copy(set_row[at][:], s["row"][:, bass.ds(n * SCAT, SCAT)])
                pool.tensor_copy(set_pair[at][:], pair[:, bass.ds(n * SCAT, SCAT), :]).then_inc(set_filled, 1)
                wait_alone(pool, set_filled, n + 1, m["passed"])
                for u in range(SCAT):
                    pool.indirect_dma_start(m["edges"], bass.IndirectOffsetOnAxis(ap=set_row[at][:, u:u + 1], axis=0),
                                            set_pair[at][:, u, :], None).then_inc(scattered[at], 16)

            pool.wait_ge(rows_ready, 1)
            send(0, 0, None)
            send(1, 1, None)
            turns = EJ // SCAT // 2
            with pool.Fori(1, turns) as t:
                send(2 * t, 0, t)
                send(2 * t + 1, 1, t)
            pool.wait_ge(scattered[0], 16 * SCAT * turns)
            pool.wait_ge(scattered[1], 16 * SCAT * turns)


def graph(nc, m):
    a, sem, banks, keep, x1 = m["a"], m["sem"], m["banks"], m["keep"], m["x1"]
    AW = len(CHUNKS) * CH
    U = EPAD // P
    SETS = 4
    NHOT = SETS * U
    HALF = NT * AW // 2
    DVE_SRC = 1
    with ExitStack() as ctx:
        adj = keep("adj", [TP, NT * AW], F32, ctx)
        adj3 = adj[:].rearrange("p (a d) -> p a d", a=NT)
        table = keep("table", [P, ECOLS, 2], F32, ctx)
        iota = keep("iota", [P, CH], I16, ctx)
        iota_f = keep("iota_f", [P, TP], F32, ctx)
        distance = [[keep(f"distance{v}_{u}", [P, TP], BF16, ctx) for u in range(U)] for v in range(SETS)]
        hot_src = [keep(f"hot_src{i}", [P, TP], BF16, ctx) for i in range(NHOT)]
        column = keep("column", [TP, AW], F32, ctx)
        hot_dst = [keep(f"hot_dst{i}", [P, CH], BF16, ctx) for i in range(NHOT)]
        h_hi = keep("h_hi", [TP, NT, C], F32R, ctx)
        h_lo = keep("h_lo", [TP, NT, C], F32R, ctx)
        a_hi = [keep(f"a_hi{i}", [TP, NT, TP], F32R, ctx) for i in range(2)]
        a_lo = [keep(f"a_lo{i}", [TP, NT, TP], F32R, ctx) for i in range(2)]
        bias = keep("bias", [TP, 2, C], F32, ctx)
        dis = keep("dis", [TP, NT], F32, ctx)
        dis_work = keep("dis_work", [TP, NT], F32, ctx)

        table_in, x_in, h_loaded = sem("table_in"), sem("g_x_in"), sem("h_loaded")
        consts, adj_zero, hot_ready, hot_used = sem("g_consts"), sem("adj_zero"), sem("hot_ready"), sem("hot_used")
        added, column_ready = sem("added"), sem("column_ready")
        distances, src_ready = sem("distances"), sem("src_ready")
        degree_ready, sd_ready, dis_ready = sem("degree_ready"), sem("g_sd"), sem("dis_ready")
        h_hi_ready, h_lo_ready = sem("h_hi_ready"), sem("h_lo_ready")
        a_hi_ready, a_lo_ready, row_done, row_read = sem("a_hi"), sem("a_lo"), sem("row_done"), sem("row_read")
        bias_ready = sem("bias_ready")
        block = ctx.enter_context(nc.Block())

        @block.sync
        def _(sp):
            sp.dma_start(table[:].rearrange("p c k -> p (c k)"), m["edges"].rearrange("(p c) k -> p (c k)", p=P)
                         ).then_inc(table_in, 16)
            sp.dma_start(x1[:], a["x"].rearrange("(i p) c -> p i c", p=TP)).then_inc(x_in, 16)
            sp.dma_start(bias[:, 0, :], a["gnn_b"].partition_broadcast(TP)).then_inc(x_in, 16)
            sp.dma_start(bias[:, 1, :], a["b_proj"].partition_broadcast(TP)).then_inc(x_in, 16)
            sp.dma_start(f32(h_lo[:]), m["hv"][0].rearrange("(i p) c -> p i c", p=TP)).then_inc(h_loaded, 16)

        @block.gpsimd
        def _(pool):
            pool.iota(iota[:], [[1, CH]], base=0, channel_multiplier=0,
                      allow_small_or_imprecise_dtypes=True).then_inc(consts, 1)
            pool.iota(iota_f[:], [[1, TP]], base=0, channel_multiplier=0,
                      allow_small_or_imprecise_dtypes=True).then_inc(consts, 1)
            pool.memset(adj[:, HALF:], 0.0).then_inc(adj_zero, 1)
            pool.wait_ge(adj_zero, 2)
            for i in range(0, NT, 2):
                pool.tensor_copy(adj3[:, i, i * TP:(i + 1) * TP], m["ident"][0:TP, 0:TP]).then_inc(adj_zero, 1)
            pool.wait_ge(x_in, 48)
            pool.tensor_tensor(bias[:, 0, :], bias[:, 0, :], bias[:, 1, :], ALU.add).then_inc(bias_ready, 1)
            pool.wait_ge(bias_ready, 1)
            for i in range(NT):
                pool.tensor_tensor(x1[:, i, :], x1[:, i, :], bias[:, 0, :], ALU.add).then_inc(bias_ready, 1)

        @block.vector
        def _(dve):
            own = m["own"].on(dve)
            dve.sem_inc(added, SETS)
            dve.memset(adj[:, 0:HALF], 0.0).then_inc(adj_zero, 1)
            dve.wait_ge(table_in, 16)
            dve.wait_ge(consts, 1)
            def hots(b, v):
                for u in range(U):
                    q = v * U + u
                    col = b * U + u
                    dve.wait_ge(hot_used, col + 1)
                    if u < DVE_SRC:
                        dve.tensor_scalar(hot_src[q][:], iota[:, 0:TP], table[:, bass.ds(col, 1), 0], None,
                                          ALU.is_equal)
                    dve.tensor_scalar(hot_dst[q][:], iota[:], table[:, bass.ds(col, 1), 1], None,
                                      ALU.is_equal).then_inc(hot_ready, 1)

            groups = [ctx.enter_context(dve.register(f"group{v}")) for v in range(SETS)]

            def add(b, v, ahead=None):
                dve.reg_load(groups[v], m["batch_group"][0:1, bass.ds(b, 1)])
                first = dve.snap(groups[v], min_val=0, max_val=NG - 1) * CH
                if ahead is not None:
                    hots(*ahead)
                dve.wait_ge(hot_used, NHOT + (b + 1) * U)
                dve.wait_ge(added, b + SETS)
                at = adj[:, bass.ds(first, CH)]
                dve.tensor_tensor(at, at, banks[v][0:TP, 0:CH], ALU.add).then_inc(added, 1)

            hots(0, 0)
            hots(1, 1)
            dve.wait_ge(adj_zero, 2 + NT)
            with dve.Fori(0, NBATCH // SETS - 1) as step:
                for v in range(SETS):
                    add(SETS * step + v, v, (SETS * step + v + 2, (v + 2) % SETS))
            for v in range(SETS):
                add(NBATCH - SETS + v, v, (NBATCH - SETS + v + 2, v + 2) if v + 2 < SETS else None)
            dve.wait_ge(added, NBATCH + SETS)
            dve.tensor_reduce(column[:], adj[:].rearrange("p (a d) -> p d a", a=NT), X, ALU.add
                              ).then_inc(column_ready, 1)
            dve.wait_ge(sd_ready, 1)
            own(dve.reciprocal(dis[:], dis[:]))
            refine_rsqrt(dve, own, dis[:], banks[6][0:TP, 0:NT], dis_work[:]).then_inc(dis_ready, 1)

            def a_low(i):
                dve.wait_ge(a_hi_ready, i + 1)
                dve.tensor_tensor(a_lo[i % 2][:], adj3[:, :, i * TP:(i + 1) * TP], f32(a_hi[i % 2][:]),
                                  ALU.subtract).then_inc(a_lo_ready, 1)

            dve.wait_ge(dis_ready, 1)
            for i in range(NT):
                dve.wait_ge(h_hi_ready, i + 1)
                dve.scalar_tensor_tensor(h_lo[:, i, :], f32(h_lo[:, i, :]), dis[:, i:i + 1], f32(h_hi[:, i, :]),
                                         ALU.mult, ALU.subtract).then_inc(h_lo_ready, 1)
                if i in (1, 3):
                    a_low(i // 2)
            for i in range(NT):
                for h in range(2):
                    n = 2 * i + h
                    dve.wait_ge(row_done, n + 1)
                    dve.wait_ge(bias_ready, i + 2)
                    at = x1[:, i, h * HC:(h + 1) * HC]
                    dve.scalar_tensor_tensor(at, banks[2 + n % 4][0:TP, 0:HC], dis[:, i:i + 1], at,
                                             ALU.mult, ALU.add).then_inc(row_read, 1)
                if i + 2 < NT:
                    a_low(i + 2)

        @block.scalar
        def _(act):
            def a_high(i):
                act.activation(a_hi[i % 2][:], adj3[:, :, i * TP:(i + 1) * TP], ACT.Copy).then_inc(a_hi_ready, 1)

            act.wait_ge(adj_zero, 2)
            for i in range(1, NT, 2):
                act.activation(adj3[:, i, i * TP:(i + 1) * TP], m["ident"][0:TP, 0:TP], ACT.Copy
                               ).then_inc(adj_zero, 1)
            act.wait_ge(table_in, 16)
            act.wait_ge(consts, 2)
            with act.Fori(0, NBATCH // SETS) as step:
                n = SETS * step
                for v in range(SETS):
                    for u in range(DVE_SRC, U):
                        col = n * U + v * U + u
                        act.activation(distance[v][u][:], iota_f[:], ACT.Abs, scale=-1.0,
                                       bias=table[:, bass.ds(col, 1), 0]).then_inc(distances, 1)
                    for u in range(DVE_SRC, U):
                        q = v * U + u
                        act.wait_ge(hot_used, n * U + q + 1)
                        act.wait_ge(distances, (n + v) * (U - DVE_SRC) + u - DVE_SRC + 1)
                        act.activation(hot_src[q][:], distance[v][u][:], ACT.Relu, scale=-1.0, bias=1.0
                                       ).then_inc(src_ready, 1)
            act.wait_ge(added, NBATCH + SETS)
            a_high(0)
            a_high(1)
            act.wait_ge(degree_ready, 1)
            act.activation(dis[:], banks[6][0:TP, 0:NT], ACT.Sqrt).then_inc(sd_ready, 1)
            act.wait_ge(dis_ready, 1)
            act.wait_ge(h_loaded, 16)
            for i in range(NT):
                act.activation(h_hi[:, i, :], f32(h_lo[:, i, :]), ACT.Copy,
                               scale=dis[:, i:i + 1]).then_inc(h_hi_ready, 1)
            for i in range(2, NT):
                act.wait_ge(row_read, 2 * (i - 1))
                a_high(i)

        @block.tensor
        def _(pe):
            pe.sem_inc(hot_used, NHOT)
            with pe.Fori(0, NBATCH // SETS) as step:
                n = SETS * step
                for v in range(SETS):
                    pe.wait_ge(added, n + v + 1)
                    for u in range(U):
                        q = v * U + u
                        pe.wait_ge(hot_ready, n * U + q + 1)
                        if u >= DVE_SRC:
                            pe.wait_ge(src_ready, (n + v) * (U - DVE_SRC) + u - DVE_SRC + 1)
                        last = pe.matmul(banks[v][0:TP, 0:CH], hot_src[q][:], hot_dst[q][:],
                                         start=(u == 0), stop=(u == U - 1))
                        last.then_inc(hot_used, 1)
            pe.wait_ge(column_ready, 1)
            for i in range(NT):
                last = pe.matmul(banks[6][0:TP, i:i + 1], column[:, i * TP:(i + 1) * TP], m["ones"][0:TP, 0:1],
                                 start=True, stop=True)
            last.then_inc(degree_ready, 1)
            for i in range(NT):
                pe.wait_ge(a_lo_ready, i + 1)
                for h in range(2):
                    n = 2 * i + h
                    if n >= 4:
                        pe.wait_ge(row_read, n - 3)
                    for s in range(NT):
                        if i == 0 and h == 0:
                            pe.wait_ge(h_lo_ready, s + 1)
                        last = three_products(pe, banks[2 + n % 4][0:TP, 0:HC], a_hi[i % 2][:, s, :],
                                              a_lo[i % 2][:, s, :], h_hi[:, s, h * HC:(h + 1) * HC],
                                              h_lo[:, s, h * HC:(h + 1) * HC], s, NT)
                    last.then_inc(row_done, 1)


def keys(nc, m):
    a, sem, banks, keep = m["a"], m["sem"], m["banks"], m["keep"]
    with ExitStack() as ctx:
        proj_in = keep("proj_in", [P, 2, M], F32, ctx)
        k_in = m["staging"][:, 0:T]
        k_hi = [keep(f"k_hi{i}", [P, T], F32R, ctx) for i in range(2)]
        k_lo = [keep(f"k_lo{i}", [P, T], F32R, ctx) for i in range(2)]
        k_sq = keep("k_sq", [P, T], F32, ctx)
        v_in = [keep(f"v_in{i}", [TP, NT, 2, DV], F32, ctx) for i in range(2)]
        e_f = [keep(f"e_f{i}", [TP, 2, M], F32, ctx) for i in range(4)]
        e_hi = [keep(f"e_hi{i}", [TP, NT, 2, M], F32R, ctx) for i in range(2)]
        e_lo = [keep(f"e_lo{i}", [TP, NT, 2, M], F32R, ctx) for i in range(2)]
        neg_max = [keep(f"neg_max{i}", [TP, NT, 2], F32, ctx) for i in range(2)]
        shift = [keep(f"shift{i}", [TP, NT, 2], F32, ctx) for i in range(2)]
        weight = [keep(f"weight{i}", [TP, NT, 2], F32, ctx) for i in range(2)]
        top = [keep(f"top{i}", [P, 2], F32, ctx) for i in range(2)]
        head_top = [keep(f"head_top{i}", [P, 2], F32, ctx) for i in range(2)]
        neg_top = [keep(f"neg_top{i}", [P, 2], F32, ctx) for i in range(2)]
        tops = keep("tops", [P, H], F32, ctx)
        v_w = keep("v_w", [TP, NT, 2, DV], F32, ctx)
        v_hi = keep("v_hi", [TP, NT, 2, DV], F32R, ctx)
        v_lo = keep("v_lo", [TP, NT, 2, DV], F32R, ctx)
        sums = keep("sums", [DV, H, M], F32, ctx)
        v_sum = keep("v_sum", [DV, H], F32, ctx)
        all_top = keep("all_top", [P, 1], F32, ctx)
        factor = keep("factor", [P, H], F32, ctx)

        p_loaded, k_loaded, v_loaded = sem("p_loaded"), sem("k_loaded"), [sem("v_loaded0"), sem("v_loaded1")]
        setup, p_scaled, p_hi_ready, p_ready = sem("k_setup"), sem("p_scaled"), sem("p_hi"), sem("p_ready")
        k_hi_r, k_lo_r, k_sq_r, diag_done = sem("k_hi"), sem("k_lo"), sem("k_sq"), sem("k_diag")
        product, maxed, exped = sem("k_product"), sem("k_maxed"), sem("k_exped")
        e_hi_r, e_lo_r, top_r, shifted = sem("e_hi"), sem("e_lo"), sem("k_top"), sem("k_shifted")
        all_red, neg_r, weight_r = sem("k_reduced"), sem("k_neg_top"), sem("k_weight")
        v_w_r, v_hi_r, v_lo_r = sem("v_weighed"), sem("v_hi"), sem("v_lo")
        summed, sums_read, fin = sem("k_summed"), sem("k_sums_read"), sem("k_final")
        fin_act, fin_turned = sem("k_final_act"), sem("k_final_turned")
        m["recycle"]()
        block = ctx.enter_context(nc.Block())

        def drive(eng, step):
            step(0, 0, True, False)
            with eng.Fori(0, HP // 2 - 1) as turn:
                step(2 * turn + 1, 1, False, False)
                step(2 * turn + 2, 0, False, False)
            step(HP - 1, 1, False, True)

        def ring(v, i):
            return (v * NT + i) % 4

        @block.sync
        def _(sp):
            sp.wait_ge(setup, 1)
            for h in range(2):
                sp.dma_start(proj_in[h * D:(h + 1) * D, h, :], a["proj_t"]).then_inc(p_loaded, 16)
            for hp in range(HP):
                if hp:
                    sp.wait_ge(k_lo_r, hp)
                    sp.wait_ge(k_sq_r, hp)
                sp.dma_start(k_in, m["qk"][1, hp * P:(hp + 1) * P, :]).then_inc(k_loaded, 16)
                if hp == 0:
                    sp.wait_ge(setup, 3)
                if hp >= 2:
                    sp.wait_ge(summed, 2 + hp - 1)
                for j in range(2):
                    h = 2 * hp + j
                    sp.dma_start(v_in[hp % 2][:, :, j, 0:D],
                                 m["hv"][1, :, h * D:(h + 1) * D].rearrange("(i p) d -> p i d", p=TP)
                                 ).then_inc(v_loaded[hp % 2], 16)

        @block.gpsimd
        def _(pool):
            pool.memset(proj_in[:], 0.0).then_inc(setup, 1)
            pool.memset(v_in[0][:], 1.0).then_inc(setup, 1)
            pool.memset(v_in[1][:], 1.0).then_inc(setup, 1)
            for t in top:
                pool.memset(t[:], -3e38).then_inc(setup, 1)
            pool.memset(m["head_mask"][:], 0.0).then_inc(setup, 1)
            pool.wait_ge(setup, 6)
            for j in range(2):
                pool.memset(m["head_mask"][j * D:(j + 1) * D, j:j + 1], DIAG).then_inc(setup, 1)
            pool.wait_ge(setup, 8)

            def square(hp):
                pool.wait_ge(k_loaded, 16 * (hp + 1))
                pool.wait_ge(diag_done, hp + 1)
                pool.tensor_tensor(k_sq[:], k_in, k_in, ALU.mult).then_inc(k_sq_r, 1)

            def weigh(hp, v):
                pool.wait_ge(weight_r, 2 * hp + 2)
                if isinstance(hp, int):
                    pool.wait_ge(v_loaded[v], 32 * (hp // 2 + 1))
                else:
                    pool.wait_ge(v_loaded[v], 16 * (hp + 2 - v))
                pool.wait_ge(v_lo_r, hp + 1)
                pool.tensor_tensor(v_w[:], v_in[v][:], weight[v][:].unsqueeze(3)
                                   .broadcast_to([TP, NT, 2, DV]), ALU.mult).then_inc(v_w_r, 1)

            def step(hp, v, first, last):
                if not first:
                    weigh(hp - 1, 1 - v)
                if not last:
                    square(hp + 1)
                wait_alone(pool, top_r, hp + 1, m["passed"])
                pool.partition_all_reduce(head_top[v][:], top[v][:], P, bass.bass_isa.ReduceOp.max
                                          ).then_inc(all_red, 1)
                wait_alone(pool, all_red, hp + 1, m["passed"])
                pool.tensor_copy(tops[:, bass.ds(2 * hp, 2)], head_top[v][:])
                pool.tensor_scalar(neg_top[v][:], head_top[v][:], -1.0, None, ALU.mult).then_inc(neg_r, 1)

            square(0)
            drive(pool, step)
            weigh(HP - 1, 1)

        @block.scalar
        def _(act):
            act.wait_ge(p_scaled, 1)
            act.activation(m["proj_hi"][:], proj_in[:], ACT.Copy).then_inc(p_hi_ready, 1)
            act.sem_inc(exped, 4)
            act.sem_inc(sums_read, 1)

            def high(hp, v):
                act.wait_ge(k_loaded, 16 * (hp + 1))
                act.activation(k_hi[v][:], k_in, ACT.Copy).then_inc(k_hi_r, 1)

            def weights(hp, v):
                act.wait_ge(neg_r, hp + 1)
                act.wait_ge(shifted, 2 + hp + 1)
                for j in range(2):
                    act.activation(weight[v][:, :, j], shift[v][:, :, j], ACT.Exp, scale=-1.0,
                                   bias=neg_top[v][0:TP, j:j + 1]).then_inc(weight_r, 1)

            def values(hp):
                act.wait_ge(v_w_r, hp + 1)
                act.wait_ge(summed, 2 + hp)
                act.activation(v_hi[:], v_w[:], ACT.Copy).then_inc(v_hi_r, 1)

            def read_sums(hp):
                act.wait_ge(summed, 2 + hp + 1)
                act.activation(sums[:, bass.ds(2 * hp, 2), :].rearrange("p h f -> p (h f)"), banks[7][0:DV, :],
                               ACT.Copy)
                act.activation(v_sum[:, bass.ds(2 * hp, 2)], banks[6][0:DV, 0:2], ACT.Copy
                               ).then_inc(sums_read, 1)

            def step(hp, v, first, last):
                for i in range(NT + 1):
                    if i < NT:
                        r = ring(v, i)
                        act.wait_ge(maxed, hp * NT + i + 1)
                        act.wait_ge(e_lo_r, hp * NT + i + 1)
                        for j in range(2):
                            done = act.activation(e_f[r][:, j, :], banks[r][0:TP, j * M:(j + 1) * M], ACT.Exp,
                                                  bias=neg_max[v][:, i, j:j + 1])
                        done.then_inc(exped, 1)
                    if i == 1:
                        act.wait_ge(summed, hp + 1)
                    if i:
                        act.wait_ge(exped, 4 + hp * NT + i)
                        act.activation(e_hi[v][:, i - 1, :, :], e_f[ring(v, i - 1)][:], ACT.Copy
                                       ).then_inc(e_hi_r, 1)
                    if not first and i == 0:
                        weights(hp - 1, 1 - v)
                    if not first and i == 3:
                        values(hp - 1)
                    if not last and i == 6:
                        high(hp + 1, 1 - v)
                if not first:
                    read_sums(hp - 1)

            high(0, 0)
            drive(act, step)
            weights(HP - 1, 1)
            values(HP - 1)
            read_sums(HP - 1)
            act.wait_ge(fin, 1)
            act.activation(factor[:], tops[:], ACT.Exp, bias=all_top[:]).then_inc(fin_act, 1)

        @block.vector
        def _(dve):
            dve.wait_ge(p_loaded, 32)
            dve.tensor_scalar(proj_in[:], proj_in[:], NORM, None, ALU.mult).then_inc(p_scaled, 1)
            dve.wait_ge(p_hi_ready, 1)
            dve.tensor_tensor(m["proj_lo"][:], proj_in[:], f32(m["proj_hi"][:]), ALU.subtract).then_inc(p_ready, 1)
            dve.sem_inc(e_lo_r, 4)
            dve.sem_inc(v_lo_r, 1)
            dve.sem_inc(shifted, 2)
            dve.wait_ge(setup, 8)

            def low(hp, v):
                dve.wait_ge(k_hi_r, hp + 1)
                dve.tensor_tensor(k_lo[v][:], k_in, f32(k_hi[v][:]), ALU.subtract).then_inc(k_lo_r, 1)

            def value_lows(hp):
                dve.wait_ge(v_hi_r, hp + 1)
                dve.tensor_tensor(v_lo[:], v_w[:], f32(v_hi[:]), ALU.subtract).then_inc(v_lo_r, 1)

            def step(hp, v, first, last):
                for i in range(NT + 2):
                    if i < NT:
                        dve.wait_ge(product, hp * NT + i + 1)
                        dve.tensor_reduce(neg_max[v][:, i, :],
                                          banks[ring(v, i)][0:TP, :].rearrange("p (j f) -> p j f", j=2), X,
                                          ALU.max, negate=True).then_inc(maxed, 1)
                    if i >= 2:
                        dve.wait_ge(e_hi_r, hp * NT + i - 1)
                        dve.tensor_tensor(e_lo[v][:, i - 2, :, :], e_f[ring(v, i - 2)][:],
                                          f32(e_hi[v][:, i - 2, :, :]), ALU.subtract).then_inc(e_lo_r, 1)
                    if not first and i == 4:
                        value_lows(hp - 1)
                    if not last and i == 8:
                        low(hp + 1, 1 - v)
                    if i == NT:
                        dve.wait_ge(maxed, (hp + 1) * NT)
                        dve.tensor_reduce(top[v][0:TP, :], neg_max[v][:].rearrange("p i j -> p j i"), X, ALU.min,
                                          negate=True).then_inc(top_r, 1)
                dve.wait_ge(diag_done, hp + 2)
                dve.tensor_tensor(shift[v][:], neg_max[v][:],
                                  banks[4 + v][0:TP, 0:2 * NT].rearrange("p (i j) -> p i j", j=2),
                                  ALU.add).then_inc(shifted, 1)

            low(0, 0)
            drive(dve, step)
            value_lows(HP - 1)
            dve.wait_ge(neg_r, HP)
            dve.tensor_reduce(all_top[:], tops[:], X, ALU.max, negate=True).then_inc(fin, 1)
            dve.wait_ge(fin_act, 1)
            dve.wait_ge(sums_read, HP + 1)
            dve.tensor_scalar(v_sum[:], v_sum[:], FEPS, None, ALU.mult).then_inc(fin, 1)
            dve.wait_ge(fin, 2)
            for h in range(H):
                last = dve.tensor_scalar(sums[:, h, :], sums[:, h, :], factor[0:DV, h:h + 1], v_sum[:, h:h + 1],
                                         ALU.mult, ALU.add)
            last.then_inc(fin, 1)
            for q in range(4):
                dve.wait_ge(fin_turned, q + 1)
                dve.tensor_copy(m["ctx"][:, 3 * q:3 * q + 3, :, :].rearrange("p h b d -> p (h b d)"),
                                banks[q][:, 0:6 * DV])

        @block.tensor
        def _(pe):
            pe.sem_inc(diag_done, 1)
            pe.sem_inc(summed, 2)
            pe.wait_ge(p_ready, 1)
            pe.wait_ge(setup, 8)

            def diagonal(hp, v):
                pe.wait_ge(k_sq_r, hp + 1)
                pe.wait_ge(shifted, hp + 1)
                for i in range(NT):
                    last = pe.matmul(banks[4 + v][0:TP, 2 * i:2 * i + 2], k_sq[:, i * TP:(i + 1) * TP],
                                     m["head_mask"][:], start=True, stop=True)
                last.then_inc(diag_done, 1)

            def plain_sums(hp, v):
                pe.wait_ge(sums_read, hp + 1)
                pe.wait_ge(v_w_r, hp + 1)
                for j in range(2):
                    for i in range(NT):
                        pe.matmul(banks[6][0:DV, j:j + 1], v_in[v][:, i, j, :], m["ones"][0:TP, 0:1],
                                  start=(i == 0), stop=(i == NT - 1))

            def sum_head(hp, v, j):
                if j == 0:
                    pe.wait_ge(v_lo_r, 1 + hp + 1)
                    pe.wait_ge(e_lo_r, 4 + (hp + 1) * NT)
                for i in range(NT):
                    done = three_products(pe, banks[7][0:DV, j * M:(j + 1) * M], v_hi[:, i, j, :],
                                          v_lo[:, i, j, :], e_hi[v][:, i, j, :], e_lo[v][:, i, j, :], i, NT)
                if j == 1:
                    done.then_inc(summed, 1)

            def step(hp, v, first, last):
                pe.wait_ge(k_lo_r, hp + 1)
                for i in range(NT):
                    pe.wait_ge(exped, hp * NT + i + 1)
                    features(pe, m, banks[ring(v, i)], k_hi[v], k_lo[v], i).then_inc(product, 1)
                    if not first and i == 6:
                        plain_sums(hp - 1, 1 - v)
                    if not first and i == 8:
                        sum_head(hp - 1, 1 - v, 0)
                if not last:
                    diagonal(hp + 1, 1 - v)
                if not first:
                    sum_head(hp - 1, 1 - v, 1)

            diagonal(0, 0)
            drive(pe, step)
            plain_sums(HP - 1, 1)
            sum_head(HP - 1, 1, 0)
            sum_head(HP - 1, 1, 1)
            pe.wait_ge(fin, 3)
            for q in range(4):
                for n in range(6):
                    h, b = 3 * q + n // 2, n % 2
                    last = pe.transpose(banks[q][:, n * DV:(n + 1) * DV], sums[:, h, b * P:(b + 1) * P],
                                        m["ident"][0:DV, 0:DV])
                last.then_inc(fin_turned, 1)


def features(pe, m, bank, x_hi, x_lo, i):
    at = (slice(None), slice(i * TP, (i + 1) * TP))
    return three_products(pe, bank[0:TP, :], x_hi[at], x_lo[at], m["proj_hi"][:].rearrange("p j f -> p (j f)"),
                          m["proj_lo"][:].rearrange("p j f -> p (j f)"), 0, 1)


def queries(nc, m):
    sem, banks, keep = m["sem"], m["banks"], m["keep"]
    STEP = 2 * NT
    SLOTS = HP * NT
    LEAD = 12
    E_LAG, T_LAG, HI_LAG, LO_LAG, O_LAG, D_LAG, N_LAG = 1, 2, 3, 4, 5, 15, 21
    CT = 2
    SPLIT = [slice(c, c + n) for c, n in CHUNKS]
    with ExitStack() as ctx:
        q_in = [keep(f"q_in{i}", [P, T], F32, ctx) for i in range(2)]
        q_hi = [keep(f"q_hi{i}", [P, T], F32R, ctx) for i in range(2)]
        q_lo = [keep(f"q_lo{i}", [P, T], F32R, ctx) for i in range(2)]
        q_sq = keep("q_sq", [P, T], F32, ctx)
        diag = [keep(f"diag{i}", [TP, NT, 2], F32, ctx) for i in range(2)]
        neg = keep("neg", [TP, 4, 2], F32, ctx)
        shift = keep("q_shift", [TP, 4, 2], F32, ctx)
        e_f = [keep(f"q_e{i}", [TP, 2, M], F32, ctx) for i in range(4)]
        f_hi = [keep(f"f_hi{i}", [P, 2, 2, CT * TP], F32R, ctx) for i in range(2)]
        f_lo = [keep(f"f_lo{i}", [P, 2, 2, CT * TP], F32R, ctx) for i in range(2)]
        c_hi = [keep(f"c_hi{i}", [P, 2, 2, DV], F32R, ctx) for i in range(2)]
        c_lo = [keep(f"c_lo{i}", [P, 2, 2, DV], F32R, ctx) for i in range(2)]
        o_f = [keep(f"o_f{i}", [DV, 2, CT * TP], F32, ctx) for i in range(2)]
        upper = keep("upper", [P, T], F32, ctx)
        lower = keep("lower", [P, T], F32, ctx)

        divisors = keep("divisors", [TP, 2, NT], F32, ctx)
        F_BANKS, T_BANKS = banks[0:2], banks[2:6]

        q_loaded = [sem("q_loaded0"), sem("q_loaded1")]
        q_hi_r, q_lo_r, q_sq_r = sem("q_hi"), sem("q_lo"), sem("q_sq")
        diag_done, diag_read, product = sem("q_diag"), sem("q_diag_read"), sem("q_product")
        maxed, shifted, exped, turned = sem("q_maxed"), sem("q_shifted"), sem("q_exped"), sem("q_turned")
        c_hi_r, c_lo_r = sem("c_hi"), sem("c_lo")
        f_hi_r, f_lo_r, o_done, o_copied = sem("f_hi"), sem("f_lo"), sem("o_done"), sem("o_copied")
        o_stored, parts_in = [sem("o_stored0"), sem("o_stored1")], sem("parts_in")
        inverted, divided, a_hi_r, a_lo_r = sem("inverted"), sem("divided"), sem("att_hi_r"), sem("att_lo_r")
        d_in, d_out = sem("divisors_in"), sem("divisors_out")
        block = ctx.enter_context(nc.Block())

        def drive(eng, slot):
            for s in range(LEAD):
                slot(s, None)
            with eng.Fori(0, 2) as t:
                for s in range(LEAD, LEAD + STEP):
                    slot(s, t)
            for s in range(LEAD + 2 * STEP, SLOTS + N_LAG - NT + 1):
                slot(s, None)

        def live(s, t, lag=0):
            return t is not None or 0 <= s - lag < SLOTS

        def nth(n, t, step):
            return n if t is None else n + step * t

        @block.sync
        def _(sp):
            def slot(s, t):
                if t is None and s == SLOTS - 5:
                    sp.dma_start(m["staging"][:], m["a"]["w_pieces"][8]).then_inc(m["staged"], 16)
                if live(s, t, O_LAG + 1) and (s - O_LAG - 1) % CT == 1:
                    n = (s - O_LAG - 1) // CT
                    c = n % (NT // CT)
                    hp = nth(n // (NT // CT), t, 2)
                    wait_alone(sp, o_copied, nth(n, t, NT) + 3, m["passed"])
                    sp.dma_start(m["att_raw"][bass.ds(hp * 2, 2), :, c * CT * TP:(c + 1) * CT * TP]
                                 .rearrange("j d t -> d j t"), o_f[n % 2][:]).then_inc(o_stored[n % 2], 16)
                if live(s, t, D_LAG) and (s - D_LAG) % NT == 0:
                    n = (s - D_LAG) // NT
                    hp = nth(n, t, 2)
                    chunks = NT // CT * (n + 1)
                    sp.wait_ge(o_stored[0], 16 * nth((chunks + 1) // 2, t, NT // CT))
                    wait_alone(sp, o_stored[1], 16 * nth(chunks // 2, t, NT // CT), m["passed"])
                    for j in range(2):
                        sp.dma_start(divisors[:, j, :], m["att_raw"][bass.ds(hp * 2 + j, 1), D, :].rearrange(
                            "j (p c) -> (j p) c", p=TP)).then_inc(d_in, 16)
                if live(s, t, D_LAG + 1) and (s - D_LAG - 1) % NT == 0:
                    n = (s - D_LAG - 1) // NT
                    hp, at = nth(n, t, 2), n % 2
                    wait_alone(sp, inverted, hp + 1, m["passed"])
                    for j in range(2):
                        sp.dma_start(m["inverse"][bass.ds(hp * 2 + j, 1), :].rearrange("j (p c) -> (j p) c", p=TP),
                                     divisors[:, j, :]).then_inc(d_out, 16)
                    sp.wait_ge(d_out, 32 * (hp + 1))
                    wait_alone(sp, a_lo_r, hp + 1, m["passed"])
                    for j in range(2):
                        rows, h = slice(j * D, (j + 1) * D), bass.ds(hp * 2 + j, 1)
                        sp.dma_start(upper[rows, :], m["att_raw"][h, 0:D, :].rearrange("j d t -> (j d) t")
                                     ).then_inc(parts_in, 16)
                        sp.dma_start(lower[rows, :], m["inverse"][h, :].broadcast_to([D, T])
                                     ).then_inc(parts_in, 16)

            drive(sp, slot)

        @block.gpsimd
        def _(pool):
            def load(hp, at):
                pool.dma_start(q_in[at][:], m["qk"][0, bass.ds(hp * P, P), :]).then_inc(q_loaded[at], 16)

            load(0, 0)
            load(1, 1)

            def slot(s, t):
                if s % NT == 2 and s > NT and (t is not None or s // NT + 1 < HP):
                    hp, at = nth(s // NT + 1, t, 2), (s // NT + 1) % 2
                    pool.wait_ge(q_lo_r, (hp - 1) * 3)
                    wait_alone(pool, q_sq_r, hp - 1, m["passed"])
                    load(hp, at)
                if s % NT == 6 and (t is not None or s // NT + 1 < HP):
                    square(s // NT + 1, t)
                if live(s, t, D_LAG + 2) and (s - D_LAG - 2) % NT == 0:
                    n = (s - D_LAG - 2) // NT
                    pool.wait_ge(parts_in, 64 * (nth(n, t, 2) + 1))
                    pool.tensor_tensor(upper[:], upper[:], lower[:], ALU.mult
                                       ).then_inc(divided, 1)

            def square(n, t):
                pool.wait_ge(q_loaded[n % 2], 16 * (nth(n // 2, t, 1) + 1))
                pool.wait_ge(diag_done, nth(n, t, 2) + 1)
                pool.tensor_tensor(q_sq[:], q_in[n % 2][:], q_in[n % 2][:], ALU.mult).then_inc(q_sq_r, 1)

            square(0, None)
            drive(pool, slot)

        @block.scalar
        def _(act):
            act.sem_inc(exped, 4)
            act.sem_inc(o_copied, 2)

            def high(n, t, c):
                act.wait_ge(q_loaded[n % 2], 16 * (nth(n // 2, t, 1) + 1))
                act.activation(q_hi[n % 2][:, SPLIT[c]], q_in[n % 2][:, SPLIT[c]], ACT.Copy).then_inc(q_hi_r, 1)

            def slot(s, t):
                if live(s, t) and s % NT == 0:
                    n = s // NT
                    act.activation(c_hi[n % 2][:], m["ctx"][:, bass.ds(nth(2 * n, t, 4), 2), :, :],
                                   ACT.Copy).then_inc(c_hi_r, 1)
                if live(s, t, E_LAG):
                    g = s - E_LAG
                    act.wait_ge(shifted, nth(g, t, STEP) + 1)
                    act.wait_ge(turned, nth(g, t, STEP) + 1)
                    for j in range(2):
                        last = act.activation(e_f[g % 4][:, j, :], F_BANKS[g % 2][0:TP, j * M:(j + 1) * M],
                                              ACT.Exp, bias=shift[:, g % 4, j:j + 1])
                    last.then_inc(exped, 1)
                if live(s, t, HI_LAG):
                    g = s - HI_LAG
                    c, u = g // CT, g % CT
                    act.wait_ge(turned, nth(g, t, STEP) + 5)
                    act.wait_ge(o_done, nth(c, t, NT) + 1)
                    act.activation(f_hi[c % 2][:, :, :, u * TP:(u + 1) * TP], T_BANKS[g % 4][:, 0:4 * TP]
                                   .rearrange("p (j b t) -> p j b t", j=2, b=2), ACT.Copy, bias=FEPS
                                   ).then_inc(f_hi_r, 1)
                if live(s, t, O_LAG + 1) and (s - O_LAG - 1) % CT == 1:
                    n = (s - O_LAG - 1) // CT
                    act.wait_ge(o_done, nth(n, t, NT) + 3)
                    if t is not None or n >= 2:
                        act.wait_ge(o_stored[n % 2], 16 * nth(n // 2, t, NT // CT))
                    act.activation(o_f[n % 2][:], banks[6][0:DV, 0:2 * CT * TP].rearrange(
                        "p (j t) -> p j t", j=2), ACT.Copy).then_inc(o_copied, 1)
                if live(s, t) and s % NT in (5, 6, 7) and (t is not None or s // NT + 1 < HP):
                    high(s // NT + 1, t, s % NT - 5)
                if live(s, t, N_LAG) and (s - N_LAG) % NT == 0:
                    n = (s - N_LAG) // NT
                    act.wait_ge(divided, nth(n, t, 2) + 1)
                    act.activation(m["att_hi"][:, bass.ds(nth(n, t, 2), 1), :], upper[:].unsqueeze(1),
                                   ACT.Copy).then_inc(a_hi_r, 1)

            for c in range(3):
                high(0, None, c)
            drive(act, slot)

        @block.vector
        def _(dve):
            dve.sem_inc(diag_read, 1)
            dve.sem_inc(f_lo_r, 4)
            dve.sem_inc(a_lo_r, 1)

            def low(n, t, c):
                dve.wait_ge(q_hi_r, nth(3 * n, t, 6) + c + 1)
                dve.tensor_tensor(q_lo[n % 2][:, SPLIT[c]], q_in[n % 2][:, SPLIT[c]],
                                  f32(q_hi[n % 2][:, SPLIT[c]]), ALU.subtract).then_inc(q_lo_r, 1)

            def read_diag(n, t):
                dve.wait_ge(diag_done, nth(n, t, 2) + 2)
                dve.tensor_copy(diag[n % 2][:].rearrange("p i j -> p (i j)"), banks[7][0:TP, 0:2 * NT]
                                ).then_inc(diag_read, 1)

            def slot(s, t):
                if live(s, t) and s % NT == 1:
                    n = s // NT
                    dve.wait_ge(c_hi_r, nth(n, t, 2) + 1)
                    dve.tensor_tensor(c_lo[n % 2][:], m["ctx"][:, bass.ds(nth(2 * n, t, 4), 2), :, :],
                                      f32(c_hi[n % 2][:]), ALU.subtract).then_inc(c_lo_r, 1)
                if live(s, t):
                    dve.wait_ge(product, nth(s, t, STEP) + 1)
                    dve.tensor_reduce(neg[:, s % 4, :], F_BANKS[s % 2][0:TP, :].rearrange(
                        "p (j f) -> p j f", j=2), X, ALU.max, negate=True).then_inc(maxed, 1)
                if live(s, t, LO_LAG):
                    g = s - LO_LAG
                    c, u = g // CT, g % CT
                    dve.wait_ge(f_hi_r, nth(g, t, STEP) + 1)
                    at = (slice(None), slice(None), slice(None), slice(u * TP, (u + 1) * TP))
                    dve.scalar_tensor_tensor(
                        f_lo[c % 2][at], T_BANKS[g % 4][:, 0:4 * TP].rearrange(
                            "p (j b t) -> p j b t", j=2, b=2), FEPS, f32(f_hi[c % 2][at]), ALU.add,
                        ALU.subtract).then_inc(f_lo_r, 1)
                if live(s, t):
                    n = s // NT
                    dve.wait_ge(maxed, nth(s, t, STEP) + 1)
                    if s % NT == 0:
                        dve.wait_ge(diag_read, nth(n, t, 2) + 2)
                    dve.wait_ge(exped, nth(s, t, STEP) + 1)
                    dve.tensor_tensor(shift[:, s % 4, :], neg[:, s % 4, :], diag[n % 2][:, s % NT, :],
                                      ALU.subtract).then_inc(shifted, 1)
                if live(s, t) and (t is not None or s // NT + 1 < HP):
                    if s % NT in (6, 7, 8):
                        low(s // NT + 1, t, s % NT - 6)
                    if s % NT == 9:
                        read_diag(s // NT + 1, t)
                if live(s, t, D_LAG + 2) and (s - D_LAG - 2) % NT == 0:
                    n = (s - D_LAG - 2) // NT
                    dve.wait_ge(d_in, 32 * (nth(n, t, 2) + 1))
                    dve.reciprocal(divisors[:], divisors[:]).then_inc(inverted, 1)
                if live(s, t, N_LAG) and (s - N_LAG) % NT == 0:
                    n = (s - N_LAG) // NT
                    dve.wait_ge(a_hi_r, nth(n, t, 2) + 1)
                    at = bass.ds(nth(n, t, 2), 1)
                    dve.tensor_tensor(m["att_lo"][:, at, :], upper[:].unsqueeze(1),
                                      f32(m["att_hi"][:, at, :]), ALU.subtract).then_inc(a_lo_r, 1)

            for c in range(3):
                low(0, None, c)
            read_diag(0, None)
            drive(dve, slot)

        @block.tensor
        def _(pe):
            pe.sem_inc(diag_done, 1)
            pe.sem_inc(turned, 4)
            pe.sem_inc(o_done, 2)

            def diagonal(n, t):
                pe.wait_ge(q_sq_r, nth(n, t, 2) + 1)
                pe.wait_ge(diag_read, nth(n, t, 2) + 1)
                for i in range(NT):
                    last = pe.matmul(banks[7][0:TP, 2 * i:2 * i + 2], q_sq[:, i * TP:(i + 1) * TP],
                                     m["head_mask"][:], start=True, stop=True)
                last.then_inc(diag_done, 1)

            def slot(s, t):
                if live(s, t):
                    n, i = s // NT, s % NT
                    if i == 0:
                        pe.wait_ge(q_lo_r, nth(3 * n, t, 6) + 3)
                    pe.wait_ge(exped, nth(s, t, STEP) + 3)
                    features(pe, m, F_BANKS[s % 2], q_hi[n % 2], q_lo[n % 2], i).then_inc(product, 1)
                if live(s, t) and s % NT == 8 and (t is not None or s // NT + 1 < HP):
                    diagonal(s // NT + 1, t)
                if live(s, t, O_LAG) and (s - O_LAG) % CT == 1:
                    g = s - O_LAG
                    n, c = g // NT, g // CT
                    if g % NT == 1:
                        pe.wait_ge(c_lo_r, nth(n, t, 2) + 1)
                    pe.wait_ge(f_lo_r, nth(g, t, STEP) + 5)
                    pe.wait_ge(o_copied, nth(c, t, NT) + 2)
                    for j in range(2):
                        for b in range(2):
                            last = three_products(pe, banks[6][0:DV, j * CT * TP:(j + 1) * CT * TP],
                                                  c_hi[n % 2][:, j, b, :], c_lo[n % 2][:, j, b, :],
                                                  f_hi[c % 2][:, j, b, :], f_lo[c % 2][:, j, b, :], b, 2)
                    last.then_inc(o_done, 1)
                if live(s, t, T_LAG):
                    g = s - T_LAG
                    pe.wait_ge(exped, nth(g, t, STEP) + 5)
                    pe.wait_ge(f_lo_r, nth(g, t, STEP) + 1)
                    for j in range(2):
                        for b in range(2):
                            c = (2 * j + b) * TP
                            last = pe.transpose(T_BANKS[g % 4][:, c:c + TP],
                                                e_f[g % 4][:, j, b * P:(b + 1) * P], m["ident"][0:TP, 0:TP])
                    last.then_inc(turned, 1)

            diagonal(0, None)
            drive(pe, slot)


def mix(nc, m):
    a, sem, banks, keep, x1 = m["a"], m["sem"], m["banks"], m["keep"], m["x1"]
    L_LAG = 2
    with ExitStack() as ctx:
        raw = [m["staging"][:].rearrange("p (k c) -> p k c", k=KB), keep("mix_raw", [P, KB, HC], F32, ctx)[:]]
        w_hi = [keep(f"mix_hi{i}", [P, KB, HC], F32R, ctx) for i in range(2)]
        w_lo = [keep(f"mix_lo{i}", [P, KB, HC], F32R, ctx) for i in range(2)]
        stats = keep("stats2", [TP, NT, 2, 6], F32, ctx)
        mean_var = keep("mean_var2", [TP, NT, 2], F32, ctx)
        spread = keep("spread2", [TP, NT], F32, ctx)
        rstd = keep("rstd2", [TP, NT], F32, ctx)
        work = keep("newton2", [TP, NT], F32, ctx)
        xn = [keep(f"xn_rows{i}", [TP, C], F32, ctx) for i in range(4)]
        xn_t = [keep(f"xn_t{i}", [P, KB, TP], F32, ctx) for i in range(2)]
        gate = keep("gate", [P, KB, NE], F32, ctx)
        l_t = [keep(f"l_t{i}", [NE, TP], F32, ctx) for i in range(2)]

        w_loaded, hi_r, lo_r, product = sem("m_w_loaded"), sem("m_w_hi"), sem("m_w_lo"), sem("m_product")
        added, var_r, sd_r = sem("m_added"), sem("m_var"), sem("m_sd")
        gate_loaded, xn_stored = sem("gate_loaded"), [sem(f"xn2_stored{i}") for i in range(4)]
        xn_r, xt_done, xt_r, l_done = sem("xn2_ready"), sem("xt_done"), sem("xt_ready"), sem("logits_done")
        l_read, l_turned = sem("logits_read"), sem("logits_turned")
        block = ctx.enter_context(nc.Block())

        @block.sync
        def _(sp):
            sp.dma_start(raw[1], a["w_pieces"][9].rearrange("p (k c) -> p k c", k=KB)).then_inc(w_loaded, 16)
            sp.dma_start(gate[:], a["gate_t"].rearrange("(k p) e -> p k e", p=P)).then_inc(gate_loaded, 16)
            sp.wait_ge(lo_r, 1)
            sp.dma_start(m["staging"][:], a["experts"][0, NE]).then_inc(m["staged"], 16)
            for i in range(NT):
                sp.wait_ge(xn_r, i + 1)
                sp.dma_start(m["xn2"][i * TP:(i + 1) * TP, :], xn[i % 4][:]).then_inc(xn_stored[i % 4], 16)
            for i in range(4):
                sp.wait_ge(xn_stored[i], 16 * len(range(i, NT, 4)))

        @block.tensor
        def _(pe):
            def logits(i):
                pe.wait_ge(xn_r, i + 1)
                if i:
                    pe.wait_ge(xt_r, i)
                for k in range(KB):
                    done = pe.transpose(banks[4 + k // 3][:, k % 3 * TP:(k % 3 + 1) * TP],
                                        xn[i % 4][:, k * P:(k + 1) * P], m["ident"][0:TP, 0:TP])
                done.then_inc(xt_done, 1)
                if i:
                    route(i - 1)
                if i >= 2:
                    turn(i - 2)

            def route(i):
                pe.wait_ge(xt_r, i + 1)
                if i:
                    pe.wait_ge(l_read, i)
                for k in range(KB):
                    done = pe.matmul(banks[6][0:NE, 0:TP], gate[:, k, :], xn_t[i % 2][:, k, :],
                                     start=(k == 0), stop=(k == KB - 1))
                done.then_inc(l_done, 1)

            def turn(i):
                pe.wait_ge(l_read, i + 1)
                pe.transpose(banks[7][0:TP, i * NE:(i + 1) * NE], l_t[i % 2][:], m["ident"][0:NE, 0:NE]
                             ).then_inc(l_turned, 1)

            pe.wait_ge(gate_loaded, 16)
            for i in range(NT + L_LAG):
                if i < NT:
                    for h in range(2):
                        n = 2 * i + h
                        if i == 0:
                            pe.wait_ge(lo_r, h + 1)
                        if n >= 4:
                            pe.wait_ge(added, n - 3)
                        for k in range(HP):
                            done = three_products(
                                pe, banks[n % 4][0:TP, 0:HC], m["att_hi"][:, k, i * TP:(i + 1) * TP],
                                m["att_lo"][:, k, i * TP:(i + 1) * TP], w_hi[h][:, k, :], w_lo[h][:, k, :], k, HP)
                        done.then_inc(product, 1)
                if i >= L_LAG:
                    logits(i - L_LAG)
            route(NT - 1)
            turn(NT - 2)
            turn(NT - 1)

        @block.scalar
        def _(act):
            for n in range(2):
                act.wait_ge(w_loaded if n else m["staged"], 16)
                act.activation(w_hi[n][:], raw[n], ACT.Copy).then_inc(hi_r, 1)
            def read_logits(i):
                act.wait_ge(l_done, i + 1)
                if i >= 2:
                    act.wait_ge(l_turned, i - 1)
                act.activation(l_t[i % 2][:], banks[6][0:NE, 0:TP], ACT.Copy).then_inc(l_read, 1)

            for i in range(NT + L_LAG):
                if i < NT:
                    act.wait_ge(var_r, i + 1)
                    act.activation(rstd[:, i:i + 1], spread[:, i:i + 1], ACT.Sqrt).then_inc(sd_r, 1)
                if i >= L_LAG:
                    t = i - L_LAG
                    act.wait_ge(xt_done, t + 1)
                    if t >= 2:
                        act.wait_ge(l_done, t - 1)
                    for h in range(2):
                        done = act.activation(xn_t[t % 2][:, 3 * h:3 * h + 3, :], banks[4 + h][:, 0:3 * TP]
                                              .rearrange("p (b t) -> p b t", b=3), ACT.Copy)
                    done.then_inc(xt_r, 1)
                    if t:
                        read_logits(t - 1)
            read_logits(NT - 1)

        @block.vector
        def _(dve):
            own = m["own"].on(dve)
            for n in range(2):
                dve.wait_ge(hi_r, n + 1)
                dve.tensor_tensor(w_lo[n][:], raw[n], f32(w_hi[n][:]), ALU.subtract).then_inc(lo_r, 1)
            for i in range(NT):
                for h in range(2):
                    dve.wait_ge(product, 2 * i + h + 1)
                    at = x1[:, i, h * HC:(h + 1) * HC]
                    dve.tensor_tensor(at, at, banks[(2 * i + h) % 4][0:TP, 0:HC], ALU.add).then_inc(added, 1)
                dve.wait_ge(added, 2 * i + 2)
                for h in range(2):
                    done = dve.bn_stats(stats[:, i, h, :], x1[:, i, h * HC:(h + 1) * HC])
                own(done)
                own(dve.bn_aggr(mean_var[:, i, :], stats[:, i, :, :]))
                one = slice(i, i + 1)
                dve.tensor_scalar(spread[:, one], mean_var[:, one, 1], LN_EPS, None, ALU.add).then_inc(var_r, 1)
                dve.wait_ge(sd_r, i + 1)
                own(dve.reciprocal(rstd[:, one], rstd[:, one]))
                own(refine_rsqrt(dve, own, rstd[:, one], spread[:, one], work[:, one]))
                if i >= 4:
                    dve.wait_ge(xn_stored[i % 4], 16 * (i // 4))
                    dve.wait_ge(xt_done, i - 3)
                dve.tensor_scalar(xn[i % 4][:], x1[:, i, :], mean_var[:, i, 0:1], rstd[:, i:i + 1],
                                  ALU.subtract, ALU.mult).then_inc(xn_r, 1)
            dve.wait_ge(l_turned, NT)
            dve.tensor_copy(m["logits"][:].rearrange("p i e -> p (i e)"), banks[7][0:TP, 0:NT * NE])


class Routing:

    def __init__(self, m, ctx):
        keep, sem = m["keep"], m["sem"]
        self.m = m
        self.best = keep("best", [TP, NT], F32, ctx)
        self.total = keep("total", [TP, NT], F32, ctx)
        self.order = keep("order", [TP, NT, 8], F32, ctx)
        self.which = keep("which", [TP, NT, 8], U32, ctx)
        self.expert = keep("expert", [TP, NT, TOPK], F32, ctx)
        self.pair = keep("moe_pair", [TP, TJ, 2], F32, ctx)
        self.s = slot_buffers(m, ctx, "moe", NE, TJ, keep("moe_wide", [TP, NE, TJ], F32, ctx)[:])
        self.bank = m["banks"][5][0:TP, 0:2 * NE]
        self.s["sums"] = keep("moe_sums", [TP, 2 * NE], F32, ctx)[:]
        self.unit_iota = keep("unit_iota", [1, NR], F32, ctx)
        self.unit_hot = keep("unit_hot", [1, NE, NR], F32, ctx)
        self.exp_ready, self.exp_done, self.consts = sem("m_exp_ready"), sem("m_exp_done"), sem("m_consts")
        self.totals_r, self.sums_r, self.sums_read = sem("m_totals"), sem("m_sums"), sem("m_sums_read")
        self.rows_r = sem("m_rows")
        self.sent, self.table_in = sem("m_sent"), sem("u_table")

    def constants(self, pool):
        m, s, consts = self.m, self.s, self.consts
        for e in range(NS):
            at = m["slot_table"][:, e * SU * UT // P:(e + 1) * SU * UT // P, :]
            pool.iota(at[:, :, 0].bitcast(I32), [[P, SU * UT // P]], base=0, channel_multiplier=1).then_inc(consts, 1)
            pool.memset(at[:, :, 1], 1.0 / NS).then_inc(consts, 1)
            pool.memset(m["unit_expert"][:, e * SU:(e + 1) * SU], NE + e).then_inc(consts, 1)
        pool.wait_ge(consts, 3 * NS)
        shared = m["slot_table"][:, 0:SCOLS, 0].bitcast(I32)
        pool.tensor_scalar(shared, shared, float(T - 1), None, ALU.min).then_inc(consts, 1)
        pool.wait_ge(consts, 3 * NS + 1)
        pool.iota(s["iota"], [[1, NE]], base=0, channel_multiplier=0,
                  allow_small_or_imprecise_dtypes=True).then_inc(consts, 1)
        pool.iota(self.unit_iota[:], [[1, NR]], base=0, channel_multiplier=0,
                  allow_small_or_imprecise_dtypes=True).then_inc(consts, 1)
        pool.memset(s["keep_on"], 1.0).then_inc(consts, 1)
        pool.iota(self.pair[:, :, 0].bitcast(I32).rearrange("p (i k) -> p i k", k=TOPK), [[TP, NT], [0, TOPK]],
                  base=0, channel_multiplier=1).then_inc(consts, 1)
        pool.wait_ge(consts, 3 * NS + 5)
        pool.memset(s["keep_on"][:, :, 0:1], 0.0).then_inc(consts, 1)

    def shift_logits(self, dve, own):
        logits = self.m["logits"]
        own(dve.tensor_reduce(self.best[:], logits[:], X, ALU.max))
        dve.tensor_tensor(logits[:], logits[:], self.best[:].unsqueeze(2).broadcast_to([TP, NT, NE]),
                          ALU.subtract).then_inc(self.exp_ready, 1)

    def exponentials(self, act):
        act.wait_ge(self.exp_ready, 1)
        act.activation(self.m["logits"][:], self.m["logits"][:], ACT.Exp).then_inc(self.exp_done, 1)

    def choose(self, dve, own):
        logits, total, order, which = self.m["logits"], self.total, self.order, self.which
        dve.wait_ge(self.exp_done, 1)
        own(dve.tensor_reduce(total[:], logits[:], X, ALU.add))
        own(dve.reciprocal(total[:], total[:]))
        own(dve.tensor_tensor(logits[:], logits[:], total[:].unsqueeze(2).broadcast_to([TP, NT, NE]), ALU.mult))
        for i in range(NT):
            done = dve.max(order[:, i, :], logits[:, i, :])
        own(done)
        for i in range(NT):
            done = dve.max_index(which[:, i, :], order[:, i, :], logits[:, i, :])
        own(done)
        own(dve.tensor_copy(self.expert[:], which[:, :, 0:TOPK]))
        own(dve.tensor_tensor(total[:], order[:, :, 0], order[:, :, 1], ALU.add))
        own(dve.tensor_scalar(total[:], total[:], 1e-8, None, ALU.add))
        own(dve.reciprocal(total[:], total[:]))
        dve.wait_ge(self.consts, 3 * NS + 6)
        own(dve.tensor_tensor(self.pair[:, :, 1].rearrange("p (i k) -> p i k", k=TOPK), order[:, :, 0:TOPK],
                              total[:].unsqueeze(2).broadcast_to([TP, NT, TOPK]), ALU.mult))
        rank_items(dve, own, self.totals_r, self.s, self.expert[:].rearrange("p i k -> p (i k)"), NE, TJ)

    def group_sums(self, pe):
        pe.wait_ge(self.totals_r, 1)
        for half, rows in enumerate((self.m["before"], self.m["ones"])):
            done = pe.matmul(self.bank[:, half * NE:(half + 1) * NE], rows[0:TP, 0:TP], self.s["total"],
                             start=True, stop=True)
        done.then_inc(self.sums_r, 1)

    def place(self, dve, own):
        m, s = self.m, self.s
        dve.wait_ge(self.sums_r, 1)
        dve.tensor_copy(s["sums"], self.bank).then_inc(self.sums_read, 1)
        dve.wait_ge(self.sums_read, 1)
        place_items(dve, own, s, NE, TJ, UT)
        own(table_rows(dve, own, s, RCOLS))
        own(dve.tensor_scalar(m["slot_of"][:], s["slot_i"], float(NS * SU * UT), None, ALU.add))
        own(dve.tensor_tensor(self.unit_hot[:], self.unit_iota[:].unsqueeze(1).broadcast_to([1, NE, NR]),
                              s["upto"][0:1, :].unsqueeze(2).broadcast_to([1, NE, NR]), ALU.is_ge))
        own(dve.tensor_reduce(self.unit_iota[:], self.unit_hot[:].rearrange("p g j -> p j g"), X, ALU.add))
        dve.tensor_scalar(m["unit_expert"][:, NS * SU:NU], self.unit_iota[:], float(NE - 1), None, ALU.min
                          ).then_inc(self.rows_r, 1)

    def send(self, pool, us):
        pool.wait_ge(self.rows_r, 1)
        for u in us:
            pool.indirect_dma_start(self.m["slots"], bass.IndirectOffsetOnAxis(ap=self.s["row"][:, u:u + 1], axis=0),
                                    self.pair[:, u, :], None).then_inc(self.sent, 16)

    def fetch(self, pool):
        pool.wait_ge(self.sent, 16 * TJ)
        pool.dma_start(self.m["slot_table"][:, SCOLS:UCOLS, :].rearrange("p c k -> p (c k)"),
                       self.m["slots"].rearrange("(p c) k -> p (c k)", p=P)).then_inc(self.table_in, 16)
        pool.wait_ge(self.table_in, 16)


def experts(nc, m):
    a, sem, banks, keep = m["a"], m["sem"], m["banks"], m["keep"]
    UB = UT // P
    SEND_FROM = 5
    SEND_COLS = -(-TJ // 3)
    SHARED_AT = NS * SU + 2
    with ExitStack() as ctx:
        raw = {"g": m["staging"], **{w: keep(f"raw_{w}", [P, KB * HC], F32, ctx) for w in "ud"}}
        w_hi = {w: keep(f"hi_{w}", [P, KB * HC], F32R, ctx) for w in "gud"}
        w_lo = {w: keep(f"lo_{w}", [P, KB * HC], F32R, ctx) for w in "gud"}
        x_in = [keep(f"unit_x{i}", [P, UB, C], F32, ctx) for i in range(2)]
        x_hi = keep("unit_hi", [P, KB, UT], F32R, ctx)
        x_lo = keep("unit_lo", [P, KB, UT], F32R, ctx)
        act_f = keep("act_f", [P, IB, UT], F32, ctx)
        h_f = keep("h_f", [P, IB, UT], F32, ctx)
        h_hi = keep("unit_h_hi", [P, IB, UT], F32R, ctx)
        h_lo = keep("unit_h_lo", [P, IB, UT], F32R, ctx)
        y_f = [keep(f"y_f{i}", [P, C], F32, ctx) for i in range(UB)]
        shared_rows = keep("shared_rows", [TP, NS, C], F32, ctx)
        tokens = [keep(f"tokens{i}", [P, UB], I32, ctx) for i in range(2)]
        loaded = {"g": m["staged"], **{w: sem(f"u_loaded_{w}") for w in "ud"}}
        BEFORE = {"g": 1, "u": 0, "d": 0}
        hi_r = {w: sem(f"u_hi_{w}") for w in "gud"}
        lo_r = {w: sem(f"u_lo_{w}") for w in "gud"}
        routing = Routing(m, ctx)
        shared_in, shared_added = sem("shared_in"), sem("shared_added")
        picked, gathered = sem("u_picked"), [sem("u_gathered0"), sem("u_gathered1")]
        x_turned, x_hi_r, x_lo_r = sem("u_turned"), sem("u_x_hi"), sem("u_x_lo")
        g_done, u_done, silu_r, h_r, h_hi_r, h_lo_r = (sem("u_gate"), sem("u_up"), sem("u_silu"), sem("u_h"),
                                                       sem("u_h_hi"), sem("u_h_lo"))
        d_done, y_r, y_stored, y_free = sem("u_down"), sem("u_y"), sem("u_y_stored"), sem("u_y_free")
        ND = 2 * UB
        G, U, TB, DB = banks[0:2], banks[2:4], banks[4:6], banks[6:8]
        block = ctx.enter_context(nc.Block())

        @block.sync
        def _(sp):
            for w in "gud":
                sp.sem_inc(lo_r[w], 1)
            which = ctx.enter_context(sp.register("expert"))

            def load(n, ws):
                sp.reg_load(which, m["unit_expert"][0:1, bass.ds(n, 1)])
                e = sp.snap(which, min_val=0, max_val=NE + NS - 1)
                for w in ws:
                    sp.wait_ge(lo_r[w], n + 1)
                    sp.dma_start(raw[w][:], a["experts"]["gud".index(w), bass.ds(e, 1), :, :].rearrange(
                        "a p c -> (a p) c")).then_inc(loaded[w], 16)

            sp.wait_ge(routing.consts, 3 * NS)
            load(0, "u")
            with sp.Fori(0, NS * SU - 1) as n:
                load(n + 1, "gu")
                load(n, "d")
            sp.wait_ge(routing.rows_r, 1)
            with sp.Fori(NS * SU - 1, NU - 1) as n:
                load(n + 1, "gu")
                load(n, "d")
            load(NU - 1, "d")

        @block.gpsimd
        def _(pool):
            pool.sem_inc(y_free, 1)

            def gather(n, at):
                if not isinstance(n, int) or n >= 2:
                    wait_alone(pool, x_turned, IB * (n - 1), m["passed"])
                pool.tensor_copy(tokens[at][:], m["slot_table"][:, bass.ds(n * UB, UB), 0].bitcast(I32)
                                 ).then_inc(picked, 1)
                wait_alone(pool, picked, n + 1, m["passed"])
                for u in range(UB):
                    pool.indirect_dma_start(x_in[at][:, u, :], None, m["xn2"],
                                            bass.IndirectOffsetOnAxis(ap=tokens[at][:, u:u + 1], axis=0)
                                            ).then_inc(gathered[at], 16)

            def low_down(n):
                pool.wait_ge(hi_r["d"], n + 1)
                pool.tensor_tensor(w_lo["d"][:], raw["d"][:], f32(w_hi["d"][:]), ALU.subtract
                                   ).then_inc(lo_r["d"], 1)

            def allow(n):
                pool.wait_ge(y_stored, 16 * UB * n)
                pool.sem_inc(y_free, 1)

            def store(n):
                for u in range(UB):
                    pool.wait_ge(y_r, 2 + ND * n + 2 * u + 2)
                    pool.dma_start(m["y"][bass.ds(n * UT + u * P, P), :], y_f[u][:]).then_inc(y_stored, 16)

            def load_shared_rows(i):
                wait_alone(pool, shared_added, NS * (i + 1), m["passed"])
                for e in range(NS):
                    pool.dma_start(shared_rows[:, e, :], m["y"][bass.ds(e * SU * UT + i * TP, TP), :]
                                   ).then_inc(shared_in, 16)

            def step(n, at):
                if not isinstance(n, int) or n + 2 < NU:
                    gather(n + 2, at)
                if not isinstance(n, int) or n >= 2:
                    allow(n - 1)
                low_down(n)
                if not isinstance(n, int) or n >= 1:
                    store(n - 1)

            routing.constants(pool)
            gather(0, 0)
            gather(1, 1)
            for n in range(NS * SU - 2):
                step(n, n % 2)
                if n >= SEND_FROM:
                    routing.send(pool, range((n - SEND_FROM) * SEND_COLS, min((n - SEND_FROM + 1) * SEND_COLS, TJ)))
            routing.fetch(pool)
            with pool.Fori(NS * SU // 2 - 1, SHARED_AT // 2) as t:
                step(2 * t, 0)
                step(2 * t + 1, 1)
            with pool.Fori(SHARED_AT // 2, (SHARED_AT + NT) // 2) as t:
                for v in range(2):
                    load_shared_rows(2 * t + v - SHARED_AT)
                    step(2 * t + v, v)
            with pool.Fori((SHARED_AT + NT) // 2, (NU - 3) // 2) as t:
                step(2 * t, 0)
                step(2 * t + 1, 1)
            for n in range(NU - 3, NU):
                step(n, n % 2)
            allow(NU - 1)
            store(NU - 1)
            pool.wait_ge(y_stored, 16 * UB * NU)

        @block.tensor
        def _(pe):
            pe.sem_inc(d_done, 1)

            def turn(n, at, turns, qs=range(IB)):
                pe.wait_ge(gathered[at], 16 * UB * turns)
                for q in qs:
                    pe.wait_ge(x_lo_r, IB * n + (2 if q == 2 else 1))
                    for b in range(2):
                        for u in range(UB):
                            c = b * UT + u * P
                            last = pe.transpose(TB[q % 2][:, c:c + P],
                                                x_in[at][:, u, (2 * q + b) * P:(2 * q + b + 1) * P], m["ident"][:])
                    last.then_inc(x_turned, 1)

            def into(n, w, bank, done, read):
                pe.wait_ge(lo_r[w], 1 + n + 1)
                pe.wait_ge(read, 2 * n + 1)
                for i in range(IB):
                    for k in range(KB):
                        c = k * HC + i * P
                        last = three_products(pe, bank[i // 2][:, i % 2 * UT:(i % 2 + 1) * UT],
                                              w_hi[w][:, c:c + P], w_lo[w][:, c:c + P],
                                              x_hi[:, k, :], x_lo[:, k, :], k, KB)
                    if i:
                        last.then_inc(done, 1)

            def down(n, qs=range(ND)):
                if 0 in qs:
                    pe.wait_ge(lo_r["d"], 1 + n + 1)
                    pe.wait_ge(h_lo_r, n + 1)
                for q in qs:
                    u, h = q // 2, q % 2
                    pe.wait_ge(y_r, ND * n + q + 1)
                    for i in range(IB):
                        c = i * C + h * HC
                        last = three_products(pe, DB[q % 2][:, 0:HC], h_hi[:, i, u * P:(u + 1) * P],
                                              h_lo[:, i, u * P:(u + 1) * P], w_hi["d"][:, c:c + HC],
                                              w_lo["d"][:, c:c + HC], i, IB)
                    last.then_inc(d_done, 1)

            def gate_up(n):
                pe.wait_ge(x_lo_r, 1 + IB * (n + 1))
                into(n, "g", G, g_done, silu_r)
                into(n, "u", U, u_done, h_r)

            turn(0, 0, 1)
            gate_up(0)
            turn(1, 1, 1)

            def pair_of_units(t, summed=False):
                for v in range(2):
                    n = 2 * t + 1 + v
                    gate_up(n)
                    if summed:
                        pe.wait_ge(routing.sums_read, 1)
                    turn(n + 1, v, t + 2, [0, 1])
                    down(n - 1, [0])
                    turn(n + 1, v, t + 2, [2])
                    down(n - 1, range(1, ND))

            with pe.Fori(0, 2) as t:
                pair_of_units(t)
            pe.wait_ge(x_lo_r, 1 + IB * 5 + 2)
            routing.group_sums(pe)
            with pe.Fori(2, (NU - 3) // 2) as t:
                pair_of_units(t, True)
            gate_up(NU - 2)
            turn(NU - 1, 0, NU // 2 + 1)
            down(NU - 3)
            gate_up(NU - 1)
            down(NU - 2)
            down(NU - 1)

        @block.scalar
        def _(act):
            act.sem_inc(silu_r, 1)

            def high(w, n, used=None):
                act.wait_ge(loaded[w], 16 * (n + 1 + BEFORE[w]))
                if used is not None:
                    act.wait_ge(*used)
                act.activation(w_hi[w][:], raw[w][:], ACT.Copy).then_inc(hi_r[w], 1)

            def x_high(n):
                for q in range(IB):
                    act.wait_ge(x_turned, IB * n + q + 1)
                    act.activation(x_hi[:, 2 * q:2 * q + 2, :], TB[q % 2][:].rearrange("p (b t) -> p b t", b=2),
                                   ACT.Copy).then_inc(x_hi_r, 1)

            def silu(n):
                act.wait_ge(h_r, 2 * n + 1)
                act.wait_ge(g_done, 2 * n + 1)
                act.activation(act_f[:, 0:2, :].rearrange("p i t -> p (i t)"), G[0][:], ACT.Silu
                               ).then_inc(silu_r, 1)
                act.wait_ge(g_done, 2 * n + 2)
                act.activation(act_f[:, 2, :], G[1][:, 0:UT], ACT.Silu).then_inc(silu_r, 1)

            def h_high(n):
                act.wait_ge(d_done, ND * n + 1)
                act.wait_ge(h_r, 1 + 2 * n + 2)
                act.activation(h_hi[:], h_f[:], ACT.Copy).then_inc(h_hi_r, 1)
                high("d", n)

            high("g", 0)
            high("u", 0)
            x_high(0)

            def body(n):
                silu(n)
                high("g", n + 1, (g_done, 2 * n + 2))
                act.wait_ge(u_done, 2 * n + 2)
                x_high(n + 1)
                high("u", n + 1)
                h_high(n)

            body(0)
            body(1)
            routing.exponentials(act)
            with act.Fori(2, NU - 1) as n:
                body(n)
            silu(NU - 1)
            h_high(NU - 1)

        @block.vector
        def _(dve):
            dve.sem_inc(x_lo_r, 1)
            dve.sem_inc(h_r, 1)
            dve.sem_inc(y_r, 2)

            def low(w, n):
                dve.wait_ge(hi_r[w], n + 1)
                dve.tensor_tensor(w_lo[w][:], raw[w][:], f32(w_hi[w][:]), ALU.subtract).then_inc(lo_r[w], 1)

            def x_low(n):
                for q in range(IB):
                    dve.wait_ge(x_hi_r, IB * n + q + 1)
                    dve.tensor_tensor(x_lo[:, 2 * q:2 * q + 2, :], TB[q % 2][:].rearrange(
                        "p (b t) -> p b t", b=2), f32(x_hi[:, 2 * q:2 * q + 2, :]), ALU.subtract
                        ).then_inc(x_lo_r, 1)

            def hidden(n):
                dve.wait_ge(silu_r, 1 + 2 * n + 2)
                dve.wait_ge(u_done, 2 * n + 1)
                if not isinstance(n, int) or n:
                    dve.wait_ge(h_lo_r, n)
                dve.tensor_tensor(h_f[:, 0:2, :].rearrange("p i t -> p (i t)"), act_f[:, 0:2, :].rearrange(
                    "p i t -> p (i t)"), U[0][:], ALU.mult).then_inc(h_r, 1)
                dve.wait_ge(u_done, 2 * n + 2)
                dve.tensor_tensor(h_f[:, 2, :], act_f[:, 2, :], U[1][:, 0:UT], ALU.mult).then_inc(h_r, 1)

            def h_low(n):
                dve.wait_ge(h_hi_r, n + 1)
                dve.tensor_tensor(h_lo[:], h_f[:], f32(h_hi[:]), ALU.subtract).then_inc(h_lo_r, 1)

            def y_rows(n, qs):
                for q in qs:
                    u, h = q // 2, q % 2
                    if q == 0:
                        dve.wait_ge(y_free, n + 1)
                    dve.wait_ge(d_done, 1 + ND * n + q + 1)
                    dve.tensor_scalar(y_f[u][:, h * HC:(h + 1) * HC], DB[q % 2][:, 0:HC],
                                      m["slot_table"][:, bass.ds(n * UB + u, 1), 1], None, ALU.mult
                                      ).then_inc(y_r, 1)

            def body(n, behind):
                low("g", n + 1)
                hidden(n)
                x_low(n + 1)
                if behind:
                    y_rows(n - 1, range(ND))
                low("u", n + 1)
                h_low(n)

            low("g", 0)
            low("u", 0)
            x_low(0)
            def add_shared(i):
                dve.wait_ge(shared_in, 16 * NS * (i + 1))
                at = m["x1"][:, bass.ds(i, 1), :]
                for e in range(NS):
                    dve.wait_ge(shared_added, NS * (i + 1) + e)
                    dve.tensor_tensor(at, at, shared_rows[:, e:e + 1, :], ALU.add).then_inc(shared_added, 1)

            dve.sem_inc(shared_added, NS)
            own = m["own"].on(dve)
            body(0, False)
            body(1, True)
            routing.shift_logits(dve, own)
            body(2, True)
            routing.choose(dve, own)
            body(3, True)
            body(4, True)
            routing.place(dve, own)
            with dve.Fori(5, SHARED_AT) as n:
                body(n, True)
            with dve.Fori(SHARED_AT, SHARED_AT + NT) as n:
                body(n, True)
                add_shared(n - SHARED_AT)
            with dve.Fori(SHARED_AT + NT, NU - 1) as n:
                body(n, True)
            hidden(NU - 1)
            y_rows(NU - 2, range(ND))
            h_low(NU - 1)
            y_rows(NU - 1, range(ND))


def combine(nc, m):
    sem, keep, x1, out = m["sem"], m["keep"], m["x1"], m["out"]
    NBUF = 5
    with ExitStack() as ctx:
        rows = [keep(f"rows{i}", [TP, TOPK, C], F32, ctx) for i in range(NBUF)]
        gathered = [sem(f"c_gathered{i}") for i in range(NBUF)]
        chosen, done, stored = sem("c_chosen"), sem("c_done"), sem("c_stored")
        block = ctx.enter_context(nc.Block())

        @block.scalar
        def _(act):
            for i in range(NT):
                act.wait_ge(done, i + 1)
                act.dma_start(out[i * TP:(i + 1) * TP, :], x1[:, i, :]).then_inc(stored, 16)
            act.wait_ge(stored, 16 * NT)

        @block.gpsimd
        def _(pool):
            for i in range(NT):
                if i >= NBUF:
                    pool.wait_ge(done, 1 + i - NBUF)
                for k in range(TOPK):
                    pool.indirect_dma_start(rows[i % NBUF][:, k, :], None, m["y"], bass.IndirectOffsetOnAxis(
                        ap=m["slot_of"][:, TOPK * i + k:TOPK * i + k + 1], axis=0)).then_inc(gathered[i % NBUF], 16)

        @block.vector
        def _(dve):
            for i in range(NT):
                r = rows[i % NBUF]
                dve.wait_ge(gathered[i % NBUF], 16 * TOPK * (i // NBUF + 1))
                dve.tensor_tensor(r[:, 0, :], r[:, 0, :], r[:, 1, :], ALU.add).then_inc(chosen, 1)
                dve.wait_ge(chosen, i + 1)
                dve.tensor_tensor(x1[:, i, :], x1[:, i, :], r[:, 0, :], ALU.add).then_inc(done, 1)


def kernel(x, src, dst, L0_gnn_W, L0_gnn_b, L0_mix_w_qkv, L0_mix_w_proj, L0_mix_b_proj, L0_mix_proj_mat,
           L0_ffn_gate_w, L0_ffn_shared_gate, L0_ffn_shared_up, L0_ffn_shared_down, L0_ffn_routed_gate,
           L0_ffn_routed_up, L0_ffn_routed_down):
    import numpy as np
    import concourse.bacc as bacc
    from concourse.bass_utils import run_bass_kernel_spmd

    def flat(w):
        n, c = w.shape[-2] // P, w.shape[-1]
        w = w.reshape(*w.shape[:-2], n, P, c)
        return np.swapaxes(w, -3, -2).reshape(*w.shape[:-3], P, n * c)

    def halves(w):
        return [flat(w[:, :HC]), flat(w[:, HC:])]

    arr = np.asarray
    qkv_t = arr(L0_mix_w_qkv).T
    pieces = []
    for w in (arr(L0_gnn_W), qkv_t[:, 2 * C:], qkv_t[:, :C], qkv_t[:, C:2 * C], arr(L0_mix_w_proj).T):
        pieces += halves(w)
    into = [np.concatenate([arr(r), arr(s)]).transpose(0, 2, 1)
            for r, s in ((L0_ffn_routed_gate, L0_ffn_shared_gate), (L0_ffn_routed_up, L0_ffn_shared_up))]
    down = np.concatenate([arr(L0_ffn_routed_down), arr(L0_ffn_shared_down)]).transpose(0, 2, 1)
    arrays = {
        "x": arr(x), "src": arr(src), "dst": arr(dst), "w_pieces": np.stack(pieces),
        "gnn_b": arr(L0_gnn_b), "b_proj": arr(L0_mix_b_proj), "proj_t": arr(L0_mix_proj_mat).T,
        "gate_t": arr(L0_ffn_gate_w).T, "experts": np.stack([flat(into[0]), flat(into[1]), flat(down)]),
    }
    arrays = {"in_" + k: np.ascontiguousarray(v) for k, v in arrays.items()}
    nc = bacc.Bacc("TRN2", target_bir_lowering=False, num_devices=1)
    a = {k[3:]: nc.dram_tensor(k, v.shape, mybir.dt.from_np(v.dtype), kind="ExternalInput").ap()
         for k, v in arrays.items()}
    out = nc.dram_tensor("out", (T, C), F32, kind="ExternalOutput").ap()
    program(nc, a, out)
    return run_bass_kernel_spmd(nc, [arrays], core_ids=[0]).results[0]["out"]
```
